# Optimizing a Trainium2 kernel written in Bass

```python
import numpy as np
import jax
import jax.numpy as jnp

def _softmax(x, axis=-1):
    return jax.nn.softmax(x, axis=axis)

def _gelu(x):
    return jax.nn.gelu(x, approximate=True)

def _silu(x):
    return jax.nn.silu(x)

def _sigmoid(x):
    return jax.nn.sigmoid(x)

def _layernorm(x, axis=-1, eps=1e-05):
    m = jnp.mean(x, axis=axis, keepdims=True)
    v = jnp.var(x, axis=axis, keepdims=True)
    return (x - m) / jnp.sqrt(v + eps)

def _scatter_add(tgt, idx, src, axis=0):
    return tgt.at[idx].add(src)

def _segment_sum(src, seg, n):
    return jax.ops.segment_sum(src, seg, n)
kernel_name = 'mk_seq_preln_d2_jaxref_r8_2c1e12'

def setup_inputs(seed: int=0):
    np.random.seed(seed)
    _w = jnp.asarray

    def _L0_attn_setup():
        import jax, jax.numpy as jnp
        import numpy as np
        B, T, D, H = (4, 256, 128, 16)
        E = D // H
        DH = D // 4
        key = jax.random.key(seed)
        ks = jax.random.split(key, 9)
        s = D ** (-0.5)
        return {'x': jax.random.normal(ks[0], (B, T, D), jnp.float32), 'q_w': jax.random.normal(ks[1], (D, D), jnp.float32) * s, 'k_w': jax.random.normal(ks[2], (D, D), jnp.float32) * s, 'v_w': jax.random.normal(ks[3], (D, D), jnp.float32) * s, 'o_w': jax.random.normal(ks[4], (D, D), jnp.float32) * s, 'cs_w1': jax.random.normal(ks[5], (DH, D), jnp.float32) * s, 'cs_b1': jnp.zeros((DH,), jnp.float32), 'cs_w2': jax.random.normal(ks[6], (H, DH), jnp.float32) * DH ** (-0.5), 'cs_b2': jnp.zeros((H,), jnp.float32), 'decay_params': jax.random.normal(ks[7], (H, E), jnp.float32) + 3.0}
    _L0_attn_in = _L0_attn_setup()

    def _L0_ffn_setup():
        import jax, jax.numpy as jnp
        import numpy as np
        E = 8
        TOPK = 2

        def _moe_forward(x, Wg, W1, W2, W3):
            B, S, D = x.shape
            xt = x.reshape(-1, D)
            T = xt.shape[0]
            logits = xt @ Wg.T
            scores = jax.nn.softmax(logits, axis=-1)
            w, idx = jax.lax.top_k(scores, TOPK)
            w = w / (w.sum(axis=-1, keepdims=True) + 1e-20)
            cw = jnp.zeros((T, E), xt.dtype).at[jnp.arange(T)[:, None], idx].add(w)
            h = jax.nn.silu(jnp.einsum('td,ehd->teh', xt, W1)) * jnp.einsum('td,ehd->teh', xt, W3)
            out = jnp.einsum('teh,edh->ted', h, W2)
            y = jnp.einsum('te,ted->td', cw, out)
            return y.reshape(B, S, D)
        key = jax.random.key(seed)
        k0, k1, k2, k3, k4 = jax.random.split(key, 5)
        B, S, D, H = (1, 256, 128, 352)
        scale = 0.02
        x = jax.random.normal(k0, (B, S, D), jnp.float32)
        Wg = jax.random.normal(k1, (E, D), jnp.float32) * scale
        W1 = jax.random.normal(k2, (E, H, D), jnp.float32) * scale
        W2 = jax.random.normal(k3, (E, D, H), jnp.float32) * scale
        W3 = jax.random.normal(k4, (E, H, D), jnp.float32) * scale
        return {'x': x, 'Wg': Wg, 'W1': W1, 'W2': W2, 'W3': W3}
    _L0_ffn_in = _L0_ffn_setup()

    def _L1_attn_setup():
        import jax, jax.numpy as jnp
        import numpy as np
        B, T, D, N = (4, 128, 128, 16)

        def _depthwise_conv3_same(x, w, b):
            xp = jnp.pad(x, ((0, 0), (1, 1), (0, 0)))
            return xp[:, :-2] * w[:, 0] + xp[:, 1:-1] * w[:, 1] + xp[:, 2:] * w[:, 2] + b

        def _selective_scan(x, A, Wb, bb, Wc, bc, Wdt, bdt):
            dt = jax.nn.softplus(x @ Wdt + bdt)
            Bm = x @ Wb + bb
            Cm = x @ Wc + bc
            dA = jnp.exp(dt[..., None] * A)
            dBx = dt[..., None] * Bm[:, :, None, :] * x[..., None]

            def step(h, ins):
                dA_t, dBx_t, C_t = ins
                h = dA_t * h + dBx_t
                y = jnp.einsum('bdn,bn->bd', h, C_t)
                return (h, y)
            h0 = jnp.zeros((x.shape[0], x.shape[2], A.shape[1]), x.dtype)
            _, ys = jax.lax.scan(step, h0, (dA.transpose(1, 0, 2, 3), dBx.transpose(1, 0, 2, 3), Cm.transpose(1, 0, 2)))
            return ys.transpose(1, 0, 2)
        key = jax.random.key(seed)
        ks = jax.random.split(key, 16)
        s = 1.0 / np.sqrt(D)
        inp = {'u': jax.random.normal(ks[0], (B, T, D), jnp.float32), 'Win': jax.random.normal(ks[1], (D, D), jnp.float32) * s, 'b_in': jnp.zeros((D,), jnp.float32), 'Wg': jax.random.normal(ks[2], (D, D), jnp.float32) * s, 'bg': jnp.zeros((D,), jnp.float32), 'Wout': jax.random.normal(ks[3], (D, D), jnp.float32) * s, 'bout': jnp.zeros((D,), jnp.float32), 'convw': jax.random.normal(ks[4], (D, 3), jnp.float32) * 0.5, 'convb': jnp.zeros((D,), jnp.float32), 'A': -jnp.exp(jax.random.normal(ks[5], (D, N), jnp.float32) * 0.5), 'Wb': jax.random.normal(ks[6], (D, N), jnp.float32) * s, 'bb': jnp.zeros((N,), jnp.float32), 'Wc': jax.random.normal(ks[7], (D, N), jnp.float32) * s, 'bc': jnp.zeros((N,), jnp.float32), 'Wdt': jax.random.normal(ks[8], (D, D), jnp.float32) * s, 'bdt': jnp.full((D,), -2.0, jnp.float32)}
        return inp
    _L1_attn_in = _L1_attn_setup()

    def _L1_ffn_setup():
        import jax, jax.numpy as jnp
        import numpy as np
        DIM = 128
        INTER = 128
        N_EXPERTS = 8
        TOPK = 2
        N_SHARED = 2
        key = jax.random.key(seed)
        ks = jax.random.split(key, 10)
        s = 0.02
        return {'x': jax.random.normal(ks[0], (4, 256, DIM), dtype=jnp.float32), 'gate_w': jax.random.normal(ks[1], (N_EXPERTS, DIM), dtype=jnp.float32) * s, 'gate_bias': jax.random.normal(ks[2], (N_EXPERTS,), dtype=jnp.float32) * s, 'w1': jax.random.normal(ks[3], (N_EXPERTS, INTER, DIM), dtype=jnp.float32) * s, 'w3': jax.random.normal(ks[4], (N_EXPERTS, INTER, DIM), dtype=jnp.float32) * s, 'w2': jax.random.normal(ks[5], (N_EXPERTS, DIM, INTER), dtype=jnp.float32) * s, 'sw1': jax.random.normal(ks[6], (N_SHARED * INTER, DIM), dtype=jnp.float32) * s, 'sw3': jax.random.normal(ks[7], (N_SHARED * INTER, DIM), dtype=jnp.float32) * s, 'sw2': jax.random.normal(ks[8], (DIM, N_SHARED * INTER), dtype=jnp.float32) * s}
    _L1_ffn_in = _L1_ffn_setup()
    _d = {'L0_attn_x': _L0_attn_in['x'], 'L0_attn_q_w': _L0_attn_in['q_w'], 'L0_attn_k_w': _L0_attn_in['k_w'], 'L0_attn_v_w': _L0_attn_in['v_w'], 'L0_attn_o_w': _L0_attn_in['o_w'], 'L0_attn_cs_w1': _L0_attn_in['cs_w1'], 'L0_attn_cs_b1': _L0_attn_in['cs_b1'], 'L0_attn_cs_w2': _L0_attn_in['cs_w2'], 'L0_attn_cs_b2': _L0_attn_in['cs_b2'], 'L0_attn_decay_params': _L0_attn_in['decay_params'], 'L0_ffn_Wg': _L0_ffn_in['Wg'], 'L0_ffn_W1': _L0_ffn_in['W1'], 'L0_ffn_W2': _L0_ffn_in['W2'], 'L0_ffn_W3': _L0_ffn_in['W3'], 'L1_attn_Win': _L1_attn_in['Win'], 'L1_attn_b_in': _L1_attn_in['b_in'], 'L1_attn_Wg': _L1_attn_in['Wg'], 'L1_attn_bg': _L1_attn_in['bg'], 'L1_attn_Wout': _L1_attn_in['Wout'], 'L1_attn_bout': _L1_attn_in['bout'], 'L1_attn_convw': _L1_attn_in['convw'], 'L1_attn_convb': _L1_attn_in['convb'], 'L1_attn_A': _L1_attn_in['A'], 'L1_attn_Wb': _L1_attn_in['Wb'], 'L1_attn_bb': _L1_attn_in['bb'], 'L1_attn_Wc': _L1_attn_in['Wc'], 'L1_attn_bc': _L1_attn_in['bc'], 'L1_attn_Wdt': _L1_attn_in['Wdt'], 'L1_attn_bdt': _L1_attn_in['bdt'], 'L1_ffn_gate_w': _L1_ffn_in['gate_w'], 'L1_ffn_gate_bias': _L1_ffn_in['gate_bias'], 'L1_ffn_w1': _L1_ffn_in['w1'], 'L1_ffn_w3': _L1_ffn_in['w3'], 'L1_ffn_w2': _L1_ffn_in['w2'], 'L1_ffn_sw1': _L1_ffn_in['sw1'], 'L1_ffn_sw3': _L1_ffn_in['sw3'], 'L1_ffn_sw2': _L1_ffn_in['sw2']}
    _x0 = _d['L0_attn_x']
    _d['L0_attn_x'] = jax.random.normal(jax.random.fold_in(jax.random.key(seed), 1), (8, 1024, 128), dtype=_x0.dtype)
    del _x0
    return _d

def reference(L0_attn_x, L0_attn_q_w, L0_attn_k_w, L0_attn_v_w, L0_attn_o_w, L0_attn_cs_w1, L0_attn_cs_b1, L0_attn_cs_w2, L0_attn_cs_b2, L0_attn_decay_params, L0_ffn_Wg, L0_ffn_W1, L0_ffn_W2, L0_ffn_W3, L1_attn_Win, L1_attn_b_in, L1_attn_Wg, L1_attn_bg, L1_attn_Wout, L1_attn_bout, L1_attn_convw, L1_attn_convb, L1_attn_A, L1_attn_Wb, L1_attn_bb, L1_attn_Wc, L1_attn_bc, L1_attn_Wdt, L1_attn_bdt, L1_ffn_gate_w, L1_ffn_gate_bias, L1_ffn_w1, L1_ffn_w3, L1_ffn_w2, L1_ffn_sw1, L1_ffn_sw3, L1_ffn_sw2):

    def _L0_attn_ref(x, q_w, k_w, v_w, o_w, cs_w1, cs_b1, cs_w2, cs_b2, decay_params):
        import jax, jax.numpy as jnp
        import numpy as np
        B, T, D, H = (4, 256, 128, 16)
        E = D // H
        DH = D // 4
        Bx, Tx, Dx = x.shape
        q = (x @ q_w.T).reshape(Bx, Tx, H, E)
        k = (x @ k_w.T).reshape(Bx, Tx, H, E)
        v = (x @ v_w.T).reshape(Bx, Tx, H, E)
        lc = jax.nn.sigmoid(jnp.tanh(x @ cs_w1.T + cs_b1) @ cs_w2.T + cs_b2)
        base = jax.nn.sigmoid(decay_params)[None, None]
        lam = jnp.clip(base * (1.0 + 0.2 * lc[..., None]), 0.0, 0.9995)

        def step(state, inp):
            qt, kt, vt, dt = inp
            state = state * dt[..., None] + kt[..., None] * vt[:, :, None, :]
            out_t = jnp.einsum('bhe,bhef->bhf', qt, state)
            return (state, out_t)
        init = jnp.zeros((Bx, H, E, E), x.dtype)
        xs = (jnp.swapaxes(q, 0, 1), jnp.swapaxes(k, 0, 1), jnp.swapaxes(v, 0, 1), jnp.swapaxes(lam, 0, 1))
        _, ys = jax.lax.scan(step, init, xs)
        y = jnp.swapaxes(ys, 0, 1).reshape(Bx, Tx, Dx)
        return y @ o_w.T

    def _L0_ffn_ref(x, Wg, W1, W2, W3):
        import jax, jax.numpy as jnp
        import numpy as np
        E = 8
        TOPK = 2

        def _moe_forward(x, Wg, W1, W2, W3):
            B, S, D = x.shape
            xt = x.reshape(-1, D)
            T = xt.shape[0]
            logits = xt @ Wg.T
            scores = jax.nn.softmax(logits, axis=-1)
            w, idx = jax.lax.top_k(scores, TOPK)
            w = w / (w.sum(axis=-1, keepdims=True) + 1e-20)
            cw = jnp.zeros((T, E), xt.dtype).at[jnp.arange(T)[:, None], idx].add(w)
            h = jax.nn.silu(jnp.einsum('td,ehd->teh', xt, W1)) * jnp.einsum('td,ehd->teh', xt, W3)
            out = jnp.einsum('teh,edh->ted', h, W2)
            y = jnp.einsum('te,ted->td', cw, out)
            return y.reshape(B, S, D)
        return _moe_forward(x, Wg, W1, W2, W3)

    def _L1_attn_ref(u, Win, b_in, Wg, bg, Wout, bout, convw, convb, A, Wb, bb, Wc, bc, Wdt, bdt):
        import jax, jax.numpy as jnp
        import numpy as np
        B, T, D, N = (4, 128, 128, 16)

        def _depthwise_conv3_same(x, w, b):
            xp = jnp.pad(x, ((0, 0), (1, 1), (0, 0)))
            return xp[:, :-2] * w[:, 0] + xp[:, 1:-1] * w[:, 1] + xp[:, 2:] * w[:, 2] + b

        def _selective_scan(x, A, Wb, bb, Wc, bc, Wdt, bdt):
            dt = jax.nn.softplus(x @ Wdt + bdt)
            Bm = x @ Wb + bb
            Cm = x @ Wc + bc
            dA = jnp.exp(dt[..., None] * A)
            dBx = dt[..., None] * Bm[:, :, None, :] * x[..., None]

            def step(h, ins):
                dA_t, dBx_t, C_t = ins
                h = dA_t * h + dBx_t
                y = jnp.einsum('bdn,bn->bd', h, C_t)
                return (h, y)
            h0 = jnp.zeros((x.shape[0], x.shape[2], A.shape[1]), x.dtype)
            _, ys = jax.lax.scan(step, h0, (dA.transpose(1, 0, 2, 3), dBx.transpose(1, 0, 2, 3), Cm.transpose(1, 0, 2)))
            return ys.transpose(1, 0, 2)
        x = u @ Win + b_in
        x = _depthwise_conv3_same(x, convw, convb)
        x = jax.nn.silu(x)
        x_ssm = _selective_scan(x, A, Wb, bb, Wc, bc, Wdt, bdt)
        z = jax.nn.silu(u @ Wg + bg)
        return x_ssm * z @ Wout + bout

    def _L1_ffn_ref(x, gate_w, gate_bias, w1, w3, w2, sw1, sw3, sw2):
        import jax, jax.numpy as jnp
        import numpy as np
        DIM = 128
        INTER = 128
        N_EXPERTS = 8
        TOPK = 2
        N_SHARED = 2
        shape = x.shape
        xt = x.reshape(-1, shape[-1])
        scores = jax.nn.softmax((xt @ gate_w.T).astype(jnp.float32), axis=-1)
        _, idx = jax.lax.top_k(scores + gate_bias, TOPK)
        weights = jnp.take_along_axis(scores, idx, axis=1).astype(x.dtype)
        y = jnp.zeros_like(xt)
        for e in range(N_EXPERTS):
            gate_e = jnp.sum(jnp.where(idx == e, weights, 0.0), axis=1)
            h = jax.nn.silu(xt @ w1[e].T) * (xt @ w3[e].T)
            y = y + gate_e[:, None] * (h @ w2[e].T)
        z = jax.nn.silu(xt @ sw1.T) * (xt @ sw3.T) @ sw2.T
        return (y + z).reshape(shape)
    x = L0_attn_x
    x = x + _L0_attn_ref(_layernorm(x, axis=-1), L0_attn_q_w, L0_attn_k_w, L0_attn_v_w, L0_attn_o_w, L0_attn_cs_w1, L0_attn_cs_b1, L0_attn_cs_w2, L0_attn_cs_b2, L0_attn_decay_params)
    x = x + _L0_ffn_ref(_layernorm(x, axis=-1), L0_ffn_Wg, L0_ffn_W1, L0_ffn_W2, L0_ffn_W3)
    x = x + _L1_attn_ref(_layernorm(x, axis=-1), L1_attn_Win, L1_attn_b_in, L1_attn_Wg, L1_attn_bg, L1_attn_Wout, L1_attn_bout, L1_attn_convw, L1_attn_convb, L1_attn_A, L1_attn_Wb, L1_attn_bb, L1_attn_Wc, L1_attn_bc, L1_attn_Wdt, L1_attn_bdt)
    x = x + _L1_ffn_ref(_layernorm(x, axis=-1), L1_ffn_gate_w, L1_ffn_gate_bias, L1_ffn_w1, L1_ffn_w3, L1_ffn_w2, L1_ffn_sw1, L1_ffn_sw3, L1_ffn_sw2)
    return x

_drawn_inputs = setup_inputs


def setup_inputs(seed=0):
    import zlib

    import numpy as np

    out = dict(_drawn_inputs(seed))
    spreads = {'L0_attn_cs_b1': (0.0, 0.1),
     'L0_attn_cs_b2': (0.0, 0.1),
     'L1_attn_b_in': (0.0, 0.1),
     'L1_attn_bg': (0.0, 0.1),
     'L1_attn_bout': (0.0, 0.1),
     'L1_attn_convb': (0.0, 0.1),
     'L1_attn_bb': (0.0, 0.1),
     'L1_attn_bc': (0.0, 0.1),
     'L1_attn_bdt': (-2.0, 0.2)}
    factors = {}
    for name, (base, spread) in spreads.items():
        noise = np.random.default_rng([zlib.crc32(name.encode()), seed]).standard_normal(out[name].shape)
        drawn = base * np.exp(spread * noise) if base else spread * noise
        out[name] = jnp.asarray(drawn.astype(out[name].dtype))
    for name, factor in factors.items():
        out[name] = (out[name] * factor).astype(out[name].dtype)
    return out
```

```python
from contextlib import ExitStack

import concourse.bass as bass
from concourse import mybir

F32 = mybir.dt.float32
BF16 = mybir.dt.bfloat16
U32 = mybir.dt.uint32
ALU = mybir.AluOpType
ACT = mybir.ActivationFunctionType
AX = mybir.AxisListType

P = 128
EPS = 1e-5
LAM_MAX = 0.9995


class Signal:

    def __init__(self, sem, per_batch, first=0):
        self.sem = sem
        self.per_batch = per_batch
        self.first = first

    def at(self, batch, n):
        return batch * self.per_batch + (n + self.first)


class BankUses:

    def __init__(self, uses, filled, read):
        self.uses = uses
        self.place = {u[0]: i for i, u in enumerate(uses)}
        assert len(self.place) == len(uses)
        self.filled = Signal(filled, len(uses))
        self.read = {r: Signal(s, sum(u[2] == r for u in uses), first=1) for r, s in read.items()}

    def bank(self, name):
        return self.uses[self.place[name]][1]

    def wait_filled(self, eng, b, name):
        eng.wait_ge(self.filled.sem, self.filled.at(b, self.place[name] + 1))

    def wait_bank_free(self, eng, b, name):
        i = self.place[name]
        before = [u[0] for u in self.uses[:i] if u[1] == self.uses[i][1]]
        if before:
            self.wait_read(eng, b, before[-1])

    def wait_read(self, eng, b, name):
        i = self.place[name]
        reader = self.uses[i][2]
        n = sum(u[2] == reader for u in self.uses[:i + 1])
        eng.wait_ge(self.read[reader].sem, self.read[reader].at(b, n))

    def wait_all_read(self, eng, b):
        for s in self.read.values():
            eng.wait_ge(s.sem, s.at(b, 0))


def mlp_tiles(experts, rows, shared):
    tiles = []
    for e in range(experts):
        for r in range(0, rows, P):
            tiles.append((len(tiles), e, min(P, rows - r), e * rows + r))
    for s in range(shared):
        tiles.append((len(tiles), None, P, experts * rows + s * P))
    return tiles


def build(nc, t, out):
    B, T, D = t["x"].shape
    TT = T // P
    HW = 512
    NH = T // HW
    TH = HW // P
    E = t["Wg0"].shape[1]
    HEADS = 16
    EF = D // HEADS
    DH = t["cs1"].shape[1]
    NS = t["A"].shape[1]
    R0 = t["W2_0"].shape[1]
    R1 = t["W2_1"].shape[1]
    SH = t["W1_1"].shape[1] // R1 - E
    TILES = {"B": mlp_tiles(E, R0, 0), "D": mlp_tiles(E, R1, SH)}

    ctx = ExitStack()
    with ctx:
        def sb(name, shape, dt=F32):
            return ctx.enter_context(nc.sbuf_tensor(name, shape, dt))

        def sem(name):
            return ctx.enter_context(nc.semaphore(name))

        def signal(name, per_batch):
            return Signal(sem(name), per_batch)

        banks = [ctx.enter_context(nc.psum_tensor(f"bank{i}", [P, HW], F32)) for i in range(8)]

        Wk, Wq = sb("Wk", [P, D]), sb("Wq", [P, D])
        Wv = sb("Wv", [P, EF, P])
        Wo = sb("Wo", [P, EF, D])
        cs1 = sb("cs1_w", [P, DH])
        cs2 = sb("cs2_w", [DH, P])
        Win, Wz, Wdt, Wout = (sb(n, [P, D]) for n in ("Win_w", "Wz_w", "Wdt_w", "Wout_w"))
        Wbc = sb("Wbc_w", [P, 3 * 2 * NS])
        W1 = {"B": sb("W1_0w", [P, E * R0]), "D": sb("W1_1w", [P, (E + SH) * R1])}
        W3 = {"B": sb("W3_0w", [P, E * R0]), "D": sb("W3_1w", [P, (E + SH) * R1])}
        W2 = {s: sb(f"W2_{s}w", [P, len(TILES[s]), D]) for s in "BD"}
        Wgate = {"B": sb("Wg_0w", [P, E]), "D": sb("Wg_1w", [P, E])}
        gate_bias = sb("gate_bias", [P, E])
        cols = sb("cols", [P, 10])
        COL = {n: i for i, n in enumerate(("decay", "cs_b2", "cs_b1", "b_in", "bg", "bout", "convb", "bdt", "bbc"))}
        col = {n: cols[:, i:i + 1] for n, i in COL.items()}
        convw = sb("convw_w", [P, 3])
        A_sb = sb("A_w", [P, NS])

        ident = sb("ident", [P, P])
        ident16 = sb("ident16", [P, P], BF16)
        sel_bc = sb("sel_bc", [3 * 2 * NS, 2 * NS, P], BF16)
        sel_gate = sb("sel_gate", [3 * E, E, P], BF16)
        expert_no = sb("expert_no", [P, TT, E])
        expert_i = sb("expert_i", [P, TT * E], U32)
        neg_half = sb("neg_half", [P, TT])
        eps_t = sb("eps_t", [P, TT])
        tb = sb("tanh_base", [P, 1])
        lam_mul, lam_add = sb("lam_mul", [P, 1]), sb("lam_add", [P, 1])
        half_b2, half_bg = sb("half_b2", [P, 1]), sb("half_bg", [P, 1])

        x0, x1, x2, x3, x4 = (sb(f"x{i}", [P, TT, D]) for i in range(5))
        XIN = {"A": x0, "B": x1, "C": x2, "D": x3}
        XOUT = {"A": x1, "B": x2, "C": x3, "D": x4}

        NORM = {}
        for g in ("AC", "BD"):
            bufs = dict(stats=sb(f"stats{g}", [P, TT, 6]), mv=sb(f"mv{g}", [P, TT, 2]),
                        ve=sb(f"ve{g}", [P, TT]), rstd=sb(f"rstd{g}", [P, TT]),
                        xn=sb(f"xn{g}", [P, TT, D]), xnT=sb(f"xnT{g}", [P, T]))
            for s in g:
                NORM[s] = bufs

        upad = sb("upad", [P, T + 2])
        xs2 = sb("xs2", [P, T])
        dt = sb("dt", [P, T])
        w = sb("w", [P, T])
        z2 = sb("z2", [P, T])
        y = sb("y", [P, T])
        dA = sb("dA", [P, 4, T])
        dBx = sb("dBx", [P, 2, T])
        hst = sb("hst", [P, 2, T])
        prod = sb("prod", [P, 2, T])
        bc_parts = sb("bc_parts", [3 * 2 * NS, T], BF16)
        bc_mid = sb("bc_mid", [3 * 2 * NS, T], BF16)
        oT = {"AC": hst[:, 0, :].rearrange("p (r n) -> p r n", n=HW), "BD": sb("oT_bd", [P, NH, HW])}
        conv = y
        conv_th, zth, zz = prod[:, 0, :], hst[:, 0, :], hst[:, 1, :]
        sp_abs, sp_log = prod[:, 0, :], prod[:, 1, :]
        bc_f, bc_r = dBx[0:3 * 2 * NS, 0, :], dBx[0:3 * 2 * NS, 1, :]
        hid, lam_th, lam, kT, qT = xs2[0:DH, :], dt, w, z2, y
        kv = dBx[:, 0, :].rearrange("p (r n) -> p r n", n=HW)
        qs = prod[:, 0, :].rearrange("p (r n) -> p r n", n=HW)
        S = dA[:, :, :].rearrange("p a (r n) -> p (a r) n", n=HW)

        th_ring = sb("th_ring", [P, 2, HW])
        h1_ring = sb("h1_ring", [P, 2, HW])
        h_ring = sb("h_ring", [P, 3, HW])
        xg = sb("xg", [P, 2, HW])
        g_lg, g_e, g_sc, g_sel, g_m, g_ms, g_r1 = (sb(f"g_{n}", [P, TT, E]) for n in
                                                   ("lg", "e", "sc", "sel", "m", "ms", "r1"))
        g_top = sb("g_top", [P, TT, 8])
        g_idx = sb("g_idx", [P, TT, 8], U32)
        g_idf = sb("g_idf", [P, TT, 2])
        g_mx, g_sum, g_rs, g_den, g_rd = (sb(f"g_{n}", [P, TT]) for n in ("mx", "sum", "rs", "den", "rd"))
        g_parts = sb("g_parts", [P, TT, 3, E], BF16)
        gT = sb("gT", [3 * E, T], BF16)

        norm_uses = lambda b0, b1: [("lnT0", b0, "act"), ("lnT1", b1, "act")]
        usesA = norm_uses(5, 6)
        usesA += [(f"cs{h}", 5 + h, "act") for h in range(NH)]
        usesA += [(f"k{h}", 5 + h, "act") for h in range(NH)]
        usesA += [(f"q{h}", 5 + h, "act") for h in range(NH)]
        usesA += [(f"lam{h}", 5 + h, "act") for h in range(NH)]
        for h in range(NH):
            usesA += [(f"v{h}_{f}", 5 + f % 2, "dve") for f in range(EF)] + [(f"o{h}", 7, "act")]
            usesA += [(f"outT{h}", 5, "dve")]
        usesC = norm_uses(5, 6)
        for name, reader in (("u", "act"), ("z", "act"), ("dt", "act"), ("bc", "act")):
            usesC += [(f"{name}{h}", 5 + h, reader) for h in range(NH)]
        ring = 0
        for s in range(NS + 2):
            for kind, n in (("B", s), ("C", s - 2)):
                if 0 <= n < NS:
                    for h in range(NH):
                        usesC.append((f"{kind}{n}_{h}", 5 + ring % 3, "dve"))
                        ring += 1
        usesC += [(f"o{h}", 5 + h, "act") for h in range(NH)] + [(f"outT{h}", 5 + h, "dve") for h in range(NH)]

        def mixture_uses(tiles):
            uses = norm_uses(0, 1) + [("logits", 2, "dve"), ("gT", 3, "act")]
            ring = 0
            for h in range(NH):
                uses.append((f"g{h}_0", ring % 4, "dve"))
                ring += 1
                for i, e, _, _ in tiles:
                    first = i == 0 or tiles[i - 1][1] != e
                    if first and e is not None and e + 1 < E:
                        uses.append((f"g{h}_{e + 1}", ring % 4, "dve"))
                        ring += 1
                    for kind in "ab":
                        uses.append((f"{kind}{h}_{i}", ring % 4, "dve"))
                        ring += 1
                uses.append((f"y{h}", 4, "act"))
                uses.append((f"outT{h}", ring % 4, "dve"))
                ring += 1
            return uses

        U = {}
        for s, uses in (("A", usesA), ("B", mixture_uses(TILES["B"])), ("C", usesC), ("D", mixture_uses(TILES["D"]))):
            U[s] = BankUses(uses, sem(f"{s}_bank_filled"),
                            {"act": sem(f"{s}_bank_read_act"), "dve": sem(f"{s}_bank_read_dve")})

        s_w = {n: sem(f"loaded_weights_{n}") for n in "ABCD"}
        s_cons, s_cons0 = sem("constants_ready"), sem("zeros_ready")
        s_turn_dve, s_turn_pool = sem("dve_wait_passed"), sem("pool_wait_passed")
        s_base, s_lamc = sem("tanh_decay_ready"), sem("decay_scalars_ready")
        x_in, x_out = signal("x_loaded", 16), Signal(sem("x_stored"), 16, first=16)
        stats = {s: signal(f"{s}_stats_done", TT) for s in "ABCD"}
        mv = {s: signal(f"{s}_mean_var_done", TT) for s in "ABCD"}
        veps = {s: signal(f"{s}_var_eps_done", 1) for s in "ABCD"}
        rstd = {s: signal(f"{s}_rstd_done", 1) for s in "ABCD"}
        xn = {s: signal(f"{s}_normalised", TT) for s in "ABCD"}
        a_th = signal("A_tanh_lam", NH)
        a_lin, a_lam = signal("A_lam_scaled", NH), signal("A_lam_clipped", NH)
        a_kv, a_scan, a_qs = signal("A_kv", NH * EF), signal("A_scan", NH * EF), signal("A_qs", NH * EF)
        a_oacc = signal("A_qs_used", NH * EF)
        c_pad = sem("C_pads_zero")
        c_conv = signal("C_conv_steps", 3)
        c_th, c_xs, c_zz, c_z = signal("C_conv_tanh", 1), signal("C_xs", 1), signal("C_gate_tanh", NH), signal("C_gate", 1)
        c_sp = signal("C_softplus_parts", NH + 2)
        c_dt, c_w = signal("C_dt", 1), signal("C_w", 1)
        c_bcf, c_hi, c_r, c_mid = signal("C_bc_f32", NH), signal("C_bc_hi", 1), signal("C_bc_rest", 1), signal("C_bc_mid", 1)
        c_lo, c_midc = signal("C_bc_lo", 1), signal("C_bc_mid_placed", 1)
        c_dA, c_dbx, c_scan = signal("C_dA", NS), signal("C_dBx", NS), signal("C_scan", NS)
        c_sum, c_yz = signal("C_sum", NS - 1), signal("C_y_gated", 1)
        GATE_STEPS = {"B": 18, "D": 15}
        g_step = {s: signal(f"{s}_gate_steps", GATE_STEPS[s]) for s in "BD"}
        g_exp, g_done = ({s: signal(f"{s}_gate_{n}", 1) for s in "BD"} for n in ("exp", "parts"))
        m_th = {s: signal(f"{s}_tanh", NH * len(TILES[s])) for s in "BD"}
        m_used = {s: signal(f"{s}_hidden_used", NH * len(TILES[s])) for s in "BD"}

        N_W = {"A": 9, "B": 6, "C": 13, "D": 5}

        LAST_OUT = f"outT{NH - 1}"

        def wait_weights(eng, s):
            eng.wait_ge(s_w[s], 16 * N_W[s])

        def half(ap, h):
            return ap[:, h * HW:(h + 1) * HW]

        block = ctx.enter_context(nc.Block())

        @block.sync
        def _(sp):
            xv = t["x"].rearrange("b (j p) d -> b p j d", p=P)
            ov = out.rearrange("b (j p) d -> b p j d", p=P)

            def load_x(b):
                sp.dma_start(x0[:, :, :], xv[b]).then_inc(x_in.sem, 16)

            sp.sem_inc(x_out.sem, x_out.first)
            load_x(0)
            for dst, n in ((Wk, "Wk"), (Wq, "Wq"), (cs1, "cs1"), (cs2, "cs2"), (Wv, "Wv"), (Wo, "Wo")):
                sp.dma_start(dst[:], t[n]).then_inc(s_w["A"], 16)
            for n in ("decay", "cs_b2"):
                sp.dma_start(col[n], t[n]).then_inc(s_w["A"], 16)
            sp.dma_start(col["cs_b1"][0:DH], t["cs_b1"]).then_inc(s_w["A"], 16)
            sp.dma_start(Wgate["B"][:], t["Wg0"]).then_inc(s_w["B"], 16)
            sp.dma_start(W1["B"][:], t["W1_0"]).then_inc(s_w["B"], 16)
            sp.dma_start(W3["B"][:], t["W3_0"]).then_inc(s_w["B"], 16)
            per = -(-R0 // P)
            w2v = W2["B"][:, :, :].rearrange("p (e j) d -> p e j d", j=per)
            for j in range(per):
                rows = min(P, R0 - j * P)
                sp.dma_start(w2v[0:rows, :, j, :],
                             t["W2_0"][:, j * P:j * P + rows, :].rearrange("e r d -> r e d")).then_inc(s_w["B"], 16)
            for dst, n in ((Win, "Win"), (Wz, "Wz"), (Wdt, "Wdt"), (Wout, "Wout"), (Wbc, "Wbc"), (convw, "convw"), (A_sb, "A")):
                sp.dma_start(dst[:], t[n]).then_inc(s_w["C"], 16)
            for n in ("b_in", "bg", "bout", "convb", "bdt"):
                sp.dma_start(col[n], t[n]).then_inc(s_w["C"], 16)
            sp.dma_start(col["bbc"][0:3 * 2 * NS], t["bbc"]).then_inc(s_w["C"], 16)
            sp.dma_start(Wgate["D"][:], t["Wg1"]).then_inc(s_w["D"], 16)
            sp.dma_start(gate_bias[:], t["gate_bias"]).then_inc(s_w["D"], 16)
            sp.dma_start(W1["D"][:], t["W1_1"]).then_inc(s_w["D"], 16)
            sp.dma_start(W3["D"][:], t["W3_1"]).then_inc(s_w["D"], 16)
            sp.dma_start(W2["D"][:], t["W2_1"].rearrange("e r d -> r e d")).then_inc(s_w["D"], 16)
            with sp.Fori(0, B - 1) as b:
                U["A"].wait_read(sp, b, LAST_OUT)
                load_x(b + 1)
                U["D"].wait_read(sp, b, LAST_OUT)
                sp.dma_start(ov[b], x4[:, :, :]).then_inc(x_out.sem, 16)
            U["D"].wait_read(sp, B - 1, LAST_OUT)
            sp.dma_start(ov[B - 1], x4[:, :, :]).then_inc(x_out.sem, 16)
            sp.wait_ge(x_out.sem, x_out.at(B, 0))

        @block.gpsimd
        def _(pool):
            zeroed = (ident, ident16, sel_bc, sel_gate)
            for z in zeroed:
                pool.memset(z[:], 0.0).then_inc(s_cons0, 1)
            pool.memset(neg_half[:], -0.5)
            pool.memset(eps_t[:], EPS)
            pool.memset(upad[:, 0:1], 0.0)
            pool.memset(upad[:, T + 1:T + 2], 0.0)
            pool.iota(expert_i[:], pattern=[[0, TT], [1, E]], base=0, channel_multiplier=0).then_inc(s_cons0, 1)
            pool.wait_ge(s_cons0, len(zeroed) + 1)
            pool.tensor_copy(expert_no[:, :, :].rearrange("p a b -> p (a b)"), expert_i[:]).then_inc(s_cons, 1)
            for m in (ident, ident16):
                pool.affine_select(out=m[:], in_=m[:], compare_op=ALU.not_equal, fill=1.0, base=0,
                                   pattern=[[-1, P]], channel_multiplier=1).then_inc(s_cons, 1)
            done = 0
            for m, rows in ((sel_bc, 2 * NS), (sel_gate, E)):
                for part in range(3):
                    pool.affine_select(out=m[:], in_=m[:], compare_op=ALU.not_equal, fill=1.0, base=-part * rows,
                                       pattern=[[-1, rows], [0, P]], channel_multiplier=1).then_inc(s_cons, 1)
                    done += 1
                    pool.wait_ge(s_cons, 3 + done)

            def rstd_of(s, b):
                n = NORM[s]
                pool.wait_ge(mv[s].sem, mv[s].at(b, TT))
                pool.tensor_tensor(n["ve"][:], n["mv"][:, :, 1], eps_t[:], ALU.add).then_inc(veps[s].sem, 1)
                pool.wait_ge(veps[s].sem, veps[s].at(b, 1))
                pool.tensor_tensor(n["rstd"][:], n["ve"][:], neg_half[:], ALU.pow).then_inc(rstd[s].sem, 1)

            def attention_qs(b):
                for h in range(NH):
                    for f in range(EF):
                        k = h * EF + f
                        if k == 0:
                            U["A"].wait_read(pool, b, f"q{NH - 1}")
                        pool.wait_ge(a_scan.sem, a_scan.at(b, k + 1))
                        if k >= 2:
                            pool.wait_ge(a_oacc.sem, a_oacc.at(b, k - 1))
                        pool.tensor_tensor(qs[:, k % 2, :], half(qT, h), S[:, f, :], ALU.mult).then_inc(a_qs.sem, 1)

            def ssm(b):
                pool.wait_ge(c_mid.sem, c_mid.at(b, 1))
                pool.sem_inc(s_turn_pool, 1)
                pool.tensor_copy(bc_parts[2 * NS:4 * NS, :], bc_mid[2 * NS:4 * NS, :]).then_inc(c_midc.sem, 1)
                for n in range(1, NS):
                    U["C"].wait_read(pool, b, f"C{n}_{NH - 1}")
                    if n > 1:
                        pool.wait_ge(c_sum.sem, c_sum.at(b, n - 1))
                    pool.tensor_tensor(y[:], y[:], prod[:, n % 2, :], ALU.add).then_inc(c_sum.sem, 1)

            with pool.Fori(0, B) as b:
                rstd_of("A", b)
                attention_qs(b)
                rstd_of("B", b)
                rstd_of("C", b)
                ssm(b)
                rstd_of("D", b)

        @block.tensor
        def _(pe):
            pe.wait_ge(s_cons, 9)

            def fill(s, b, name, cols=HW, rows=P, free=True):
                if free:
                    U[s].wait_bank_free(pe, b, name)
                return banks[U[s].bank(name)][0:rows, 0:cols]

            def filled(s, ins):
                ins.then_inc(U[s].filled.sem, 1)

            def transpose_norm(s, b):
                for h in range(NH):
                    bank = fill(s, b, f"lnT{h}")
                    for j in range(TH):
                        pe.wait_ge(xn[s].sem, xn[s].at(b, h * TH + j + 1))
                        last = pe.transpose(bank[:, j * P:(j + 1) * P], NORM[s]["xn"][:, h * TH + j, :], ident[:])
                    filled(s, last)

            def wait_xnT(s, b):
                U[s].wait_read(pe, b, f"lnT{NH - 1}")

            def transpose_out(s, b, h, g, acc):
                U[s].wait_read(pe, b, f"{acc}{h}")
                bank = fill(s, b, f"outT{h}")
                for j in range(TH):
                    last = pe.transpose(bank[:, j * P:(j + 1) * P], oT[g][:, h, j * P:(j + 1) * P], ident[:])
                filled(s, last)

            def attention(b):
                xnT = NORM["A"]["xnT"]
                if isinstance(b, int) and b == 0:
                    wait_weights(pe, "A")
                U["C"].wait_all_read(pe, b)
                transpose_norm("A", b)
                wait_xnT("A", b)
                for name, wt, rows in (("cs", cs1, DH), ("k", Wk, P), ("q", Wq, P)):
                    for h in range(NH):
                        filled("A", pe.matmul(fill("A", b, f"{name}{h}", rows=rows), wt[:], half(xnT, h),
                                              start=True, stop=True))
                for h in range(NH):
                    U["A"].wait_read(pe, b, f"cs{h}")
                    filled("A", pe.matmul(fill("A", b, f"lam{h}"), cs2[:], half(hid, h), start=True, stop=True))

                def value(h, f):
                    filled("A", pe.matmul(fill("A", b, f"v{h}_{f}"), Wv[:, f, :], half(xnT, h), start=True, stop=True))

                for h in range(NH):
                    value(h, 0)
                    value(h, 1)
                    bank = fill("A", b, f"o{h}")
                    for f in range(EF):
                        if f + 2 < EF:
                            value(h, f + 2)
                        k = h * EF + f
                        pe.wait_ge(a_qs.sem, a_qs.at(b, k + 1))
                        last = pe.matmul(bank, Wo[:, f, :], qs[:, k % 2, :], start=(f == 0), stop=(f == EF - 1))
                        last.then_inc(a_oacc.sem, 1)
                    pe.wait_ge(a_oacc.sem, a_oacc.at(b, (h + 1) * EF))
                    pe.sem_inc(U["A"].filled.sem, 1)
                    transpose_out("A", b, h, "AC", "o")

            def ssm(b):
                xnT = NORM["C"]["xnT"]
                U["A"].wait_all_read(pe, b + 1)
                transpose_norm("C", b)
                wait_xnT("C", b)
                for name, wt in (("u", Win), ("z", Wz)):
                    for h in range(NH):
                        filled("C", pe.matmul(fill("C", b, f"{name}{h}"), wt[:], half(xnT, h), start=True, stop=True))
                pe.wait_ge(c_xs.sem, c_xs.at(b, 1))
                for name, wt, rows in (("dt", Wdt, P), ("bc", Wbc, 3 * 2 * NS)):
                    for h in range(NH):
                        filled("C", pe.matmul(fill("C", b, f"{name}{h}", rows=rows), wt[:], half(xs2, h),
                                              start=True, stop=True))
                pe.wait_ge(c_lo.sem, c_lo.at(b, 1))
                pe.wait_ge(c_midc.sem, c_midc.at(b, 1))
                for s in range(NS + 2):
                    for kind, n in (("B", s), ("C", s - 2)):
                        if 0 <= n < NS:
                            row = n + NS * (kind == "C")
                            for h in range(NH):
                                filled("C", pe.matmul(fill("C", b, f"{kind}{n}_{h}"), sel_bc[:, row, :],
                                                      half(bc_parts, h), start=True, stop=True))
                pe.wait_ge(c_yz.sem, c_yz.at(b, 1))
                for h in range(NH):
                    filled("C", pe.matmul(fill("C", b, f"o{h}"), Wout[:], half(w, h), start=True, stop=True))
                for h in range(NH):
                    transpose_out("C", b, h, "AC", "o")

            def mixture(s, b, before):
                tiles = TILES[s]
                NT = len(tiles)
                xnT = NORM[s]["xnT"]
                U[before[0]].wait_all_read(pe, before[1])
                transpose_norm(s, b)
                wait_xnT(s, b)
                bank = fill(s, b, "logits", cols=TT * E)
                for j in range(TT):
                    last = pe.matmul(bank[:, j * E:(j + 1) * E], xnT[:, j * P:(j + 1) * P], Wgate[s][:],
                                     start=True, stop=True)
                filled(s, last)
                pe.wait_ge(g_done[s].sem, g_done[s].at(b, 1))
                fill(s, b, "gT")
                gbank = banks[U[s].bank("gT")].bitcast(BF16)
                for j in range(TT):
                    last = pe.transpose(gbank[0:3 * E, j * P:(j + 1) * P],
                                        g_parts[:, j, :, :].rearrange("p c e -> p (c e)"), ident16[:])
                filled(s, last)
                U[s].wait_read(pe, b, "gT")

                for h in range(NH):
                    def gate_rows(e):
                        filled(s, pe.matmul(fill(s, b, f"g{h}_{e}"), sel_gate[:, e, :], half(gT, h),
                                            start=True, stop=True))

                    def down(i):
                        _, e, rows, _ = tiles[i]
                        k = h * NT + i
                        U[s].wait_read(pe, b, f"b{h}_{i}")
                        if i == 0:
                            fill(s, b, f"y{h}")
                        pe.matmul(banks[4][:], W2[s][0:rows, i, :], h_ring[0:rows, k % 3, :],
                                  start=(i == 0), stop=(i == NT - 1)).then_inc(m_used[s].sem, 1)

                    gate_rows(0)
                    for i, e, rows, r0 in tiles:
                        first = i == 0 or tiles[i - 1][1] != e
                        last_of = i == NT - 1 or tiles[i + 1][1] != e
                        if first and e is not None and e + 1 < E:
                            gate_rows(e + 1)
                        pe.matmul(fill(s, b, f"a{h}_{i}", rows=rows), W1[s][:, r0:r0 + rows], half(xnT, h),
                                  start=True, stop=True).then_inc(U[s].filled.sem, 1)
                        rhs = half(xnT, h)
                        if e is not None:
                            if first:
                                U[s].wait_read(pe, b, f"g{h}_{e}")
                            rhs = xg[:, e % 2, :]
                        mm = pe.matmul(fill(s, b, f"b{h}_{i}", rows=rows), W3[s][:, r0:r0 + rows], rhs,
                                       start=True, stop=True)
                        mm.then_inc(U[s].filled.sem, 1)
                        if i >= 1:
                            down(i - 1)
                    down(NT - 1)
                    pe.wait_ge(m_used[s].sem, m_used[s].at(b, (h + 1) * NT))
                    pe.sem_inc(U[s].filled.sem, 1)
                    transpose_out(s, b, h, "BD", "y")

            def batch(b):
                attention(b)
                mixture("B", b, ("D", b))
                ssm(b)
                mixture("D", b, ("B", b + 1))

            for s in "ABCD":
                wait_weights(pe, s)
            with pe.Fori(0, B) as b:
                batch(b)

        @block.scalar
        def _(act):
            for s in "ABCD":
                act.sem_inc(U[s].read["act"].sem, 1)
            for s in "AC":
                wait_weights(act, s)
            act.activation(tb[:], col["decay"], ACT.Tanh, scale=0.5).then_inc(s_base, 1)
            act.mul(half_b2[:], col["cs_b2"], 0.5).then_inc(s_base, 1)
            act.mul(half_bg[:], col["bg"], 0.5).then_inc(s_base, 1)
            act.wait_ge(s_base, 3)

            def read(s, ins):
                ins.then_inc(U[s].read["act"].sem, 1)

            def bank(s, name, rows=P):
                return banks[U[s].bank(name)][0:rows, :]

            def move_norm(s, b):
                for h in range(NH):
                    U[s].wait_filled(act, b, f"lnT{h}")
                    read(s, act.copy(half(NORM[s]["xnT"], h), bank(s, f"lnT{h}")))

            def attention(b):
                move_norm("A", b)
                for h in range(NH):
                    U["A"].wait_filled(act, b, f"cs{h}")
                    read("A", act.activation(half(hid, h), bank("A", f"cs{h}", DH), ACT.Tanh, bias=col["cs_b1"][0:DH]))
                for name, dst in (("k", kT), ("q", qT)):
                    for h in range(NH):
                        U["A"].wait_filled(act, b, f"{name}{h}")
                        read("A", act.copy(half(dst, h), bank("A", f"{name}{h}")))
                for h in range(NH):
                    U["A"].wait_filled(act, b, f"lam{h}")
                    ins = act.activation(half(lam_th, h), bank("A", f"lam{h}"), ACT.Tanh, bias=half_b2[:], scale=0.5)
                    read("A", ins)
                for h in range(NH):
                    U["A"].wait_filled(act, b, f"o{h}")
                    read("A", act.copy(oT["AC"][:, h, :], bank("A", f"o{h}")))

            def ssm(b):
                move_norm("C", b)
                for h in range(NH):
                    U["C"].wait_filled(act, b, f"u{h}")
                    read("C", act.activation(upad[:, 1 + h * HW:1 + (h + 1) * HW], bank("C", f"u{h}"), ACT.Identity,
                                             bias=col["b_in"]))
                for h in range(NH):
                    U["C"].wait_filled(act, b, f"z{h}")
                    act.activation(half(zth, h), bank("C", f"z{h}"), ACT.Tanh, bias=half_bg[:],
                                   scale=0.5).then_inc(c_zz.sem, 1)
                    read("C", act.activation(half(zz, h), bank("C", f"z{h}"), ACT.Identity, bias=col["bg"]))
                    
                act.wait_ge(c_conv.sem, c_conv.at(b, 3))
                act.activation(conv_th, conv[:], ACT.Tanh, scale=0.5).then_inc(c_th.sem, 1)
                act.wait_ge(c_xs.sem, c_xs.at(b, 1))
                for h in range(NH):
                    U["C"].wait_filled(act, b, f"dt{h}")
                    act.activation(half(sp_abs, h), bank("C", f"dt{h}"), ACT.Abs, bias=col["bdt"],
                                   scale=0.5).then_inc(c_sp.sem, 1)
                    read("C", act.activation(half(dt, h), bank("C", f"dt{h}"), ACT.Relu, bias=col["bdt"], scale=0.5))
                act.wait_ge(c_sp.sem, c_sp.at(b, NH))
                act.activation(sp_abs, sp_abs, ACT.Exp, scale=-1.0).then_inc(c_sp.sem, 1)
                act.wait_ge(c_sp.sem, c_sp.at(b, NH + 1))
                act.activation(sp_log, sp_abs, ACT.Ln, bias=1.0).then_inc(c_sp.sem, 1)
                for h in range(NH):
                    U["C"].wait_filled(act, b, f"bc{h}")
                    ins = act.activation(half(bc_f, h), bank("C", f"bc{h}", 3 * 2 * NS), ACT.Identity,
                                         bias=col["bbc"][0:3 * 2 * NS], scale=0.5)
                    read("C", ins)
                U["C"].wait_read(act, b, f"bc{NH - 1}")
                act.copy(bc_parts[:], bc_f).then_inc(c_hi.sem, 1)
                act.wait_ge(c_r.sem, c_r.at(b, 1))
                act.copy(bc_mid[:], bc_r).then_inc(c_mid.sem, 1)
                act.wait_ge(c_dt.sem, c_dt.at(b, 1))
                for n in range(NS):
                    if n >= 4:
                        act.wait_ge(c_scan.sem, c_scan.at(b, n - 3))
                    act.activation(dA[:, n % 4, :], dt[:], ACT.Exp, scale=A_sb[:, n:n + 1]).then_inc(c_dA.sem, 1)
                for h in range(NH):
                    U["C"].wait_filled(act, b, f"o{h}")
                    read("C", act.activation(oT["AC"][:, h, :], bank("C", f"o{h}"), ACT.Identity, bias=col["bout"],
                                             scale=0.5))

            def mixture(s, b):
                tiles = TILES[s]
                NT = len(tiles)
                move_norm(s, b)
                U[s].wait_read(act, b, "logits")
                act.activation(g_e[:], g_lg[:], ACT.Exp).then_inc(g_exp[s].sem, 1)
                U[s].wait_filled(act, b, "gT")
                read(s, act.copy(gT[:], banks[U[s].bank("gT")].bitcast(BF16)[0:3 * E, :]))
                for h in range(NH):
                    for i, e, rows, _ in tiles:
                        k = h * NT + i
                        U[s].wait_filled(act, b, f"a{h}_{i}")
                        if k >= 2:
                            hh, ii = divmod(k - 2, NT)
                            U[s].wait_read(act, b, f"a{hh}_{ii}")
                        act.activation(th_ring[0:rows, k % 2, :], bank(s, f"a{h}_{i}", rows), ACT.Tanh,
                                       scale=0.5).then_inc(m_th[s].sem, 1)
                    U[s].wait_filled(act, b, f"y{h}")
                    read(s, act.copy(oT["BD"][:, h, :], bank(s, f"y{h}")))

            with act.Fori(0, B) as b:
                attention(b)
                mixture("B", b)
                ssm(b)
                mixture("D", b)

        @block.vector
        def _(dve):
            for s in "ABCD":
                dve.sem_inc(U[s].read["dve"].sem, 1)
            for s in "ACD":
                wait_weights(dve, s)
            dve.wait_ge(s_cons, 9)
            dve.wait_ge(s_base, 3)
            dve.tensor_scalar(lam_mul[:], tb[:], 0.05, 0.05, ALU.mult, ALU.add).then_inc(s_lamc, 1)
            dve.tensor_scalar(lam_add[:], tb[:], 0.55, 0.55, ALU.mult, ALU.add).then_inc(s_lamc, 1)
            dve.wait_ge(s_lamc, 2)

            def read(s, ins):
                ins.then_inc(U[s].read["dve"].sem, 1)

            def bank(s, name, rows=P):
                return banks[U[s].bank(name)][0:rows, :]

            def norm(s, b):
                n, x = NORM[s], XIN[s]
                for j in range(TT):
                    dve.bn_stats(n["stats"][:, j, :], x[:, j, :]).then_inc(stats[s].sem, 1)
                for j in range(TT):
                    dve.wait_ge(stats[s].sem, stats[s].at(b, j + 1))
                    dve.sem_inc(s_turn_dve, 1)
                    dve.bn_aggr(n["mv"][:, j, :], n["stats"][:, j, :]).then_inc(mv[s].sem, 1)
                dve.wait_ge(mv[s].sem, mv[s].at(b, TT))
                dve.wait_ge(rstd[s].sem, rstd[s].at(b, 1))
                for j in range(TT):
                    dve.tensor_scalar(n["xn"][:, j, :], x[:, j, :], n["mv"][:, j, 0:1], n["rstd"][:, j:j + 1],
                                      ALU.subtract, ALU.mult).then_inc(xn[s].sem, 1)

            def add_residual(s, b, h, scale):
                U[s].wait_filled(dve, b, f"outT{h}")
                js = slice(h * TH, (h + 1) * TH)
                ins = dve.scalar_tensor_tensor(
                    out=XOUT[s][:, js, :].rearrange("p j d -> p (j d)"), in0=bank(s, f"outT{h}"), scalar=scale,
                    in1=XIN[s][:, js, :].rearrange("p j d -> p (j d)"), op0=ALU.mult, op1=ALU.add)
                read(s, ins)

            def attention(b):
                dve.wait_ge(x_in.sem, x_in.at(b, 16))
                norm("A", b)
                for h in range(NH):
                    U["A"].wait_read(dve, b, f"lam{h}")
                    dve.tensor_scalar(half(lam, h), half(lam_th, h), lam_mul[:], lam_add[:],
                                      ALU.mult, ALU.add).then_inc(a_lin.sem, 1)
                for h in range(NH):
                    dve.wait_ge(a_lin.sem, a_lin.at(b, h + 1))
                    dve.tensor_scalar(half(lam, h), half(lam, h), LAM_MAX, 0.0, ALU.min,
                                      ALU.max).then_inc(a_lam.sem, 1)

                def outer(k):
                    h, f = divmod(k, EF)
                    U["A"].wait_filled(dve, b, f"v{h}_{f}")
                    if k >= 2:
                        dve.wait_ge(a_scan.sem, a_scan.at(b, k - 1))
                    ins = dve.tensor_tensor(kv[:, k % 2, :], bank("A", f"v{h}_{f}"), half(kT, h), ALU.mult)
                    read("A", ins)

                outer(0)
                for k in range(NH * EF):
                    h, f = divmod(k, EF)
                    if f + 1 < EF:
                        outer(k + 1)
                    U["A"].wait_read(dve, b, f"v{h}_{f}")
                    dve.wait_ge(a_lam.sem, a_lam.at(b, h + 1))
                    if h:
                        dve.wait_ge(a_qs.sem, a_qs.at(b, k - EF + 1))
                    dve.tensor_tensor_scan(S[:, f, :], half(lam, h), kv[:, k % 2, :],
                                           0.0 if h == 0 else S[:, f, HW - 1:HW], ALU.mult,
                                           ALU.add).then_inc(a_scan.sem, 1)
                    if f == EF - 1:
                        add_residual("A", b, h, 1.0)
                        if h + 1 < NH:
                            outer(k + 1)

            def ssm(b):
                U["B"].wait_read(dve, b, LAST_OUT)
                norm("C", b)
                U["C"].wait_read(dve, b, f"u{NH - 1}")
                dve.tensor_scalar(conv[:], upad[:, 1:T + 1], convw[:, 1:2], col["convb"], ALU.mult,
                                  ALU.add).then_inc(c_conv.sem, 1)
                for i in (0, 2):
                    dve.wait_ge(c_conv.sem, c_conv.at(b, 1 + i // 2))
                    dve.scalar_tensor_tensor(out=conv[:], in0=upad[:, i:T + i], scalar=convw[:, i:i + 1], in1=conv[:],
                                             op0=ALU.mult, op1=ALU.add).then_inc(c_conv.sem, 1)
                dve.wait_ge(c_zz.sem, c_zz.at(b, NH))
                U["C"].wait_read(dve, b, f"z{NH - 1}")
                dve.scalar_tensor_tensor(out=z2[:], in0=zth, scalar=1.0, in1=zz, op0=ALU.add,
                                         op1=ALU.mult).then_inc(c_z.sem, 1)
                dve.wait_ge(c_th.sem, c_th.at(b, 1))
                dve.scalar_tensor_tensor(out=xs2[:], in0=conv_th, scalar=1.0, in1=conv[:], op0=ALU.add,
                                         op1=ALU.mult).then_inc(c_xs.sem, 1)
                dve.wait_ge(c_hi.sem, c_hi.at(b, 1))
                dve.tensor_tensor(bc_r, bc_f, bc_parts[:], ALU.subtract).then_inc(c_r.sem, 1)
                dve.wait_ge(c_sp.sem, c_sp.at(b, NH + 2))
                dve.tensor_tensor(dt[:], dt[:], sp_log, ALU.add).then_inc(c_dt.sem, 1)
                dve.wait_ge(c_mid.sem, c_mid.at(b, 1))
                dve.tensor_tensor(bc_parts[4 * NS:6 * NS, :], bc_r[4 * NS:6 * NS, :], bc_mid[4 * NS:6 * NS, :],
                                  ALU.subtract).then_inc(c_lo.sem, 1)
                dve.wait_ge(c_dt.sem, c_dt.at(b, 1))
                dve.scalar_tensor_tensor(out=w[:], in0=dt[:], scalar=0.5, in1=xs2[:], op0=ALU.mult,
                                         op1=ALU.mult).then_inc(c_w.sem, 1)
                dve.wait_ge(c_w.sem, c_w.at(b, 1))
                dve.wait_ge(c_lo.sem, c_lo.at(b, 1))
                for s in range(NS + 2):
                    if s < NS:
                        for h in range(NH):
                            U["C"].wait_filled(dve, b, f"B{s}_{h}")
                            if s >= 2:
                                dve.wait_ge(c_scan.sem, c_scan.at(b, s - 1))
                            read("C", dve.tensor_tensor(half(dBx[:, s % 2, :], h), bank("C", f"B{s}_{h}"), half(w, h),
                                                        ALU.mult))
                    if 0 <= s - 1 < NS:
                        n = s - 1
                        U["C"].wait_read(dve, b, f"B{n}_{NH - 1}")
                        dve.wait_ge(c_dA.sem, c_dA.at(b, n + 1))
                        if n >= 2:
                            U["C"].wait_read(dve, b, f"C{n - 2}_{NH - 1}")
                        dve.tensor_tensor_scan(hst[:, n % 2, :], dA[:, n % 4, :], dBx[:, n % 2, :], 0.0, ALU.mult,
                                               ALU.add).then_inc(c_scan.sem, 1)
                    if 0 <= s - 2:
                        n = s - 2
                        dve.wait_ge(c_scan.sem, c_scan.at(b, n + 1))
                        if n >= 3:
                            dve.wait_ge(c_sum.sem, c_sum.at(b, n - 2))
                        dst = y if n == 0 else prod[:, n % 2, :]
                        for h in range(NH):
                            U["C"].wait_filled(dve, b, f"C{n}_{h}")
                            ins = dve.tensor_tensor(half(dst, h), bank("C", f"C{n}_{h}"), half(hst[:, n % 2, :], h),
                                                    ALU.mult)
                            read("C", ins)
                dve.wait_ge(c_sum.sem, c_sum.at(b, NS - 1))
                dve.wait_ge(c_z.sem, c_z.at(b, 1))
                dve.tensor_tensor(w[:], y[:], z2[:], ALU.mult).then_inc(c_yz.sem, 1)
                for h in range(NH):
                    add_residual("C", b, h, 1.0)

            def gates(s, b):
                count = [0]

                def step(ins):
                    count[0] += 1
                    ins.then_inc(g_step[s].sem, 1)
                    dve.wait_ge(g_step[s].sem, g_step[s].at(b, count[0]))

                def bc(ap):
                    return ap.unsqueeze(2).broadcast_to([P, TT, E])

                U[s].wait_filled(dve, b, "logits")
                lg = bank(s, "logits")[:, 0:TT * E].rearrange("p (j e) -> p j e", e=E)
                step(dve.tensor_reduce(g_mx[:], lg, AX.X, ALU.max))
                ins = dve.tensor_tensor(g_lg[:], lg, bc(g_mx[:]), ALU.subtract)
                read(s, ins)
                dve.wait_ge(g_exp[s].sem, g_exp[s].at(b, 1))
                step(dve.tensor_reduce(g_sum[:], g_e[:], AX.X, ALU.add))
                step(dve.reciprocal(g_rs[:], g_sum[:]))
                step(dve.tensor_tensor(g_sc[:], g_e[:], bc(g_rs[:]), ALU.mult))
                pick = g_sc
                if s == "D":
                    pick = g_sel
                    step(dve.tensor_tensor(g_sel[:], g_sc[:], gate_bias[:].unsqueeze(1).broadcast_to([P, TT, E]), ALU.add))
                dve.sem_inc(s_turn_dve, 1)
                for j in range(TT):
                    ins = dve.max(g_top[:, j, :], pick[:, j, :])
                step(ins)
                dve.sem_inc(s_turn_dve, 1)
                for j in range(TT):
                    ins = dve.max_index(g_idx[:, j, :], g_top[:, j, :], pick[:, j, :])
                step(ins)
                step(dve.tensor_copy(g_idf[:], g_idx[:, :, 0:2]))
                step(dve.tensor_tensor(g_m[:], expert_no[:], bc(g_idf[:, :, 0]), ALU.is_equal))
                step(dve.tensor_tensor(g_r1[:], expert_no[:], bc(g_idf[:, :, 1]), ALU.is_equal))
                step(dve.tensor_tensor(g_m[:], g_m[:], g_r1[:], ALU.add))
                step(dve.tensor_tensor(g_ms[:], g_m[:], g_sc[:], ALU.mult))
                if s == "B":
                    step(dve.tensor_reduce(g_den[:], g_ms[:], AX.X, ALU.add))
                    step(dve.tensor_scalar(g_den[:], g_den[:], 1e-20, None, ALU.add))
                    step(dve.reciprocal(g_rd[:], g_den[:]))
                    step(dve.tensor_tensor(g_ms[:], g_ms[:], bc(g_rd[:]), ALU.mult))
                step(dve.tensor_copy(g_parts[:, :, 0, :], g_ms[:]))
                step(dve.tensor_tensor(g_r1[:], g_ms[:], g_parts[:, :, 0, :], ALU.subtract))
                step(dve.tensor_copy(g_parts[:, :, 1, :], g_r1[:]))
                dve.tensor_tensor(g_parts[:, :, 2, :], g_r1[:], g_parts[:, :, 1, :], ALU.subtract).then_inc(g_done[s].sem, 1)
                assert count[0] == GATE_STEPS[s], count

            def mixture(s, b):
                tiles = TILES[s]
                NT = len(tiles)
                prev = {"B": "A", "D": "C"}[s]
                U[prev].wait_read(dve, b, LAST_OUT)
                norm(s, b)
                gates(s, b)
                xnT = NORM[s]["xnT"]
                if s == "D":
                    dve.wait_ge(x_out.sem, x_out.at(b, 0))
                for h in range(NH):
                    def scale_x(e):
                        U[s].wait_filled(dve, b, f"g{h}_{e}")
                        k = h * E + e
                        if k >= 2:
                            i = max(i for i, ee, _, _ in tiles if ee == (e - 2) % E)
                            hh = h if e >= 2 else h - 1
                            U[s].wait_filled(dve, b, f"b{hh}_{i}")
                        ins = dve.tensor_tensor(xg[:, e % 2, :], bank(s, f"g{h}_{e}"), half(xnT, h), ALU.mult)
                        read(s, ins)

                    scale_x(0)
                    for i, e, rows, _ in tiles:
                        k = h * NT + i
                        first = i == 0 or tiles[i - 1][1] != e
                        if first and e is not None and e + 1 < E:
                            scale_x(e + 1)
                        dve.wait_ge(m_th[s].sem, m_th[s].at(b, k + 1))
                        ins = dve.scalar_tensor_tensor(out=h1_ring[0:rows, k % 2, :], in0=th_ring[0:rows, k % 2, :],
                                                       scalar=1.0, in1=bank(s, f"a{h}_{i}", rows), op0=ALU.add,
                                                       op1=ALU.mult)
                        read(s, ins)
                        U[s].wait_read(dve, b, f"a{h}_{i}")
                        U[s].wait_filled(dve, b, f"b{h}_{i}")
                        if k >= 3:
                            dve.wait_ge(m_used[s].sem, m_used[s].at(b, k - 2))
                        ins = dve.tensor_tensor(h_ring[0:rows, k % 3, :], bank(s, f"b{h}_{i}", rows),
                                                h1_ring[0:rows, k % 2, :], ALU.mult)
                        read(s, ins)
                    add_residual(s, b, h, 0.5)

            with dve.Fori(0, B) as b:
                attention(b)
                mixture("B", b)
                ssm(b)
                mixture("D", b)


def kernel(**inputs):
    import numpy as np
    import concourse.bacc as bacc
    from concourse import mybir as mb
    from concourse.bass_utils import run_bass_kernel_spmd

    i = {k: np.asarray(v) for k, v in inputs.items()}
    H, EF = 16, 8
    D = 128

    def column(v):
        return v.reshape(-1, 1)

    def rows(v):
        return v.reshape(-1, v.shape[-1]).T

    bc = np.concatenate([i["L1_attn_Wb"], i["L1_attn_Wc"]], axis=1)
    bbc = np.concatenate([i["L1_attn_bb"], i["L1_attn_bc"]])
    v_t = i["L0_attn_v_w"].T.reshape(D, H, EF)
    o_t = i["L0_attn_o_w"].T.reshape(H, EF, D)
    t = {
        "x": i["L0_attn_x"],
        "Wk": i["L0_attn_k_w"].T, "Wq": i["L0_attn_q_w"].T,
        "Wv": np.repeat(v_t.transpose(0, 2, 1), EF, axis=2),
        "Wo": np.repeat(o_t, EF, axis=0),
        "cs1": i["L0_attn_cs_w1"].T, "cs2": np.repeat(i["L0_attn_cs_w2"].T, EF, axis=1),
        "cs_b1": column(i["L0_attn_cs_b1"]), "cs_b2": column(np.repeat(i["L0_attn_cs_b2"], EF)),
        "decay": column(i["L0_attn_decay_params"]),
        "Wg0": i["L0_ffn_Wg"].T, "W1_0": rows(i["L0_ffn_W1"]), "W3_0": rows(i["L0_ffn_W3"]),
        "W2_0": i["L0_ffn_W2"].transpose(0, 2, 1),
        "Win": i["L1_attn_Win"], "Wz": i["L1_attn_Wg"], "Wdt": i["L1_attn_Wdt"], "Wout": i["L1_attn_Wout"],
        "Wbc": np.concatenate([bc, bc, bc], axis=1), "bbc": column(np.concatenate([bbc, bbc, bbc])),
        "b_in": column(i["L1_attn_b_in"]), "bg": column(i["L1_attn_bg"]), "bout": column(i["L1_attn_bout"]),
        "convb": column(i["L1_attn_convb"]), "bdt": column(i["L1_attn_bdt"]),
        "convw": i["L1_attn_convw"], "A": i["L1_attn_A"],
        "Wg1": i["L1_ffn_gate_w"].T, "gate_bias": np.repeat(i["L1_ffn_gate_bias"].reshape(1, -1), D, axis=0),
        "W1_1": np.concatenate([rows(i["L1_ffn_w1"]), i["L1_ffn_sw1"].T], axis=1),
        "W3_1": np.concatenate([rows(i["L1_ffn_w3"]), i["L1_ffn_sw3"].T], axis=1),
        "W2_1": np.concatenate([i["L1_ffn_w2"].transpose(0, 2, 1), i["L1_ffn_sw2"].T.reshape(2, D, D)], axis=0),
    }
    nc = bacc.Bacc("TRN2", target_bir_lowering=False, num_devices=1)
    arrays, handles = {}, {}
    for name, a in t.items():
        a = np.ascontiguousarray(a)
        arrays[f"in_{name}"] = a
        handles[name] = nc.dram_tensor(f"in_{name}", a.shape, mb.dt.from_np(a.dtype), kind="ExternalInput").ap()
    out = nc.dram_tensor("out_0", i["L0_attn_x"].shape, mb.dt.float32, kind="ExternalOutput").ap()
    build(nc, handles, out)
    r = run_bass_kernel_spmd(nc, [arrays], core_ids=[0])
    return r.results[0]["out_0"]
```

```python
from contextlib import ExitStack

import concourse.bass as bass
from concourse import mybir

F32 = mybir.dt.float32
BF16 = mybir.dt.bfloat16
F16 = mybir.dt.float16
U32 = mybir.dt.uint32
ALU = mybir.AluOpType
ACT = mybir.ActivationFunctionType
AX = mybir.AxisListType

P = 128
EPS = 1e-5
FIRST = 16
LAM_MAX = 0.9995


class Signal:

    def __init__(self, sem, per_batch, first=0):
        self.sem = sem
        self.per_batch = per_batch
        self.first = first

    def at(self, batch, n):
        return batch * self.per_batch + (n + self.first)


class BankUses:

    def __init__(self, uses, filled, read):
        self.uses = uses
        self.place = {u[0]: i for i, u in enumerate(uses)}
        assert len(self.place) == len(uses)
        self.filled = Signal(filled, len(uses))
        self.read = {r: Signal(s, sum(u[2] == r for u in uses), first=FIRST) for r, s in read.items()}

    def bank(self, name):
        return self.uses[self.place[name]][1]

    def wait_filled(self, eng, b, name):
        eng.wait_ge(self.filled.sem, self.filled.at(b, self.place[name] + 1))

    def wait_bank_free(self, eng, b, name):
        i = self.place[name]
        before = [u[0] for u in self.uses[:i] if u[1] == self.uses[i][1]]
        if before:
            self.wait_read(eng, b, before[-1])

    def wait_read(self, eng, b, name):
        i = self.place[name]
        reader = self.uses[i][2]
        n = sum(u[2] == reader for u in self.uses[:i + 1])
        eng.wait_ge(self.read[reader].sem, self.read[reader].at(b, n))

    def wait_read_before(self, eng, b, name):
        i = self.place[name]
        reader = self.uses[i][2]
        n = -sum(u[2] == reader for u in self.uses[i + 1:])
        assert n + FIRST > 0
        eng.wait_ge(self.read[reader].sem, self.read[reader].at(b, n))

    def wait_last_read(self, eng, b, bank):
        self.wait_read_before(eng, b, [u[0] for u in self.uses if u[1] == bank][-1])

    def wait_all_read(self, eng, b):
        for s in self.read.values():
            eng.wait_ge(s.sem, s.at(b, 0))


class Steps:

    def __init__(self, norm, norm_transposed, attention_start, attention_step, attention_end, ssm_in, ssm_rates,
                 ssm_parts, ssm_step, ssm_gate, ssm_out, tile, mixture_out, logits, gates):
        self.norm, self.norm_transposed, self.logits, self.gates = norm, norm_transposed, logits, gates
        self.attention_start, self.attention_step = attention_start, attention_step
        self.attention_end = attention_end
        self.ssm_in, self.ssm_rates, self.ssm_parts = ssm_in, ssm_rates, ssm_parts
        self.ssm_step, self.ssm_gate, self.ssm_out = ssm_step, ssm_gate, ssm_out
        self.tile, self.mixture_out = tile, mixture_out


def mlp_tiles(experts, rows, shared):
    tiles = []
    for e in range(experts):
        for r in range(0, rows, P):
            tiles.append((len(tiles), e, min(P, rows - r), e * rows + r))
    for s in range(shared):
        tiles.append((len(tiles), None, P, experts * rows + s * P))
    return tiles


def steady(pairs, tiles):
    first, last, steps = pairs
    n = last - first
    return {first + i: range(steps * i // n, steps * (i + 1) // n) for i in range(n) if first + i < tiles}


def build(nc, t, out):
    B, T, D = t["x"].shape
    TT = T // P
    HW = 512
    NH = T // HW
    TH = HW // P
    E = t["Wg0"].shape[1]
    HEADS = 16
    EF = D // HEADS
    DH = t["cs1"].shape[1]
    NS = t["A"].shape[1]
    BC = 3 * 2 * NS
    R0 = t["W2_0"].shape[1]
    R1 = t["W2_1"].shape[1]
    SH = t["W1_1"].shape[1] // R1 - E
    TILES = {"B": mlp_tiles(E, R0, 0), "D": mlp_tiles(E, R1, SH)}
    NT = {s: len(TILES[s]) for s in "BD"}
    VK = NH * EF
    LAG = 2
    GATE_LAG, SECOND_LAG, DOWN_LAG = 2, 3, 5

    ctx = ExitStack()
    with ctx:
        def sb(name, shape, dt=F32):
            return ctx.enter_context(nc.sbuf_tensor(name, shape, dt))

        def sem(name):
            return ctx.enter_context(nc.semaphore(name))

        def signal(name, per_batch):
            return Signal(sem(name), per_batch)

        banks = [ctx.enter_context(nc.psum_tensor(f"bank{i}", [P, HW], F32)) for i in range(8)]

        Wk, Wq = sb("Wk", [P, D]), sb("Wq", [P, D])
        Wo = sb("Wo", [P, EF, D])
        cs1 = sb("cs1_w", [P, DH])
        cs2 = sb("cs2_w", [DH, P])
        Win, Wz, Wdt, Wout = (sb(n, [P, D]) for n in ("Win_w", "Wz_w", "Wdt_w", "Wout_w"))
        Wbc = sb("Wbc_w", [P, BC])
        SPLIT = {n: t[n].shape[1] for n in ("Wv", "W1_0", "W3_0", "W1_1", "W3_1")}
        Whi = {n: sb(f"{n}_hi", [P, m], F16) for n, m in SPLIT.items()}
        Wlo = {n: sb(f"{n}_lo", [P, m], F16) for n, m in SPLIT.items()}
        W1 = {"B": "W1_0", "D": "W1_1"}
        W3 = {"B": "W3_0", "D": "W3_1"}
        W2 = {s: sb(f"W2_{s}w", [P, NT[s], D]) for s in "BD"}
        Wgate = {"B": sb("Wg_0w", [P, E]), "D": sb("Wg_1w", [P, E])}
        gate_bias = sb("gate_bias", [P, E])
        cols = sb("cols", [P, 10])
        COL = {n: i for i, n in enumerate(("decay", "cs_b2", "cs_b1", "b_in", "bg", "bout", "convb", "bdt", "bbc"))}
        col = {n: cols[:, i:i + 1] for n, i in COL.items()}
        convw = sb("convw_w", [P, 3])
        A_sb = sb("A_w", [P, NS])
        wmax, wmin, wabs, wtop = (sb(n, [P, len(SPLIT)]) for n in ("wmax", "wmin", "wabs", "wtop"))
        wexp, wscale, winv = (sb(n, [P, len(SPLIT)], U32) for n in ("wexp", "wscale", "winv"))
        place = {n: i for i, n in enumerate(SPLIT)}
        up = {n: wscale[:, i:i + 1].bitcast(F32) for n, i in place.items()}
        down = {n: winv[:, i:i + 1].bitcast(F32) for n, i in place.items()}

        ident = sb("ident", [P, P])
        ident16 = sb("ident16", [P, P], BF16)
        sel_bc = sb("sel_bc", [BC, 2 * NS, P], BF16)
        sel_gate = sb("sel_gate", [3 * E, E, P], BF16)
        expert_no = sb("expert_no", [P, TT, E])
        expert_i = sb("expert_i", [P, TT * E], U32)
        neg_half = sb("neg_half", [P, TT])
        eps_t = sb("eps_t", [P, TT])
        tb = sb("tanh_base", [P, 1])
        lam_mul, lam_add = sb("lam_mul", [P, 1]), sb("lam_add", [P, 1])
        half_b2 = sb("half_b2", [P, 1])

        x0, x1, x2, x3, x4 = (sb(f"x{i}", [P, TT, D]) for i in range(5))
        XIN = {"A": x0, "B": x1, "C": x2, "D": x3}
        XOUT = {"A": x1, "B": x2, "C": x3, "D": x4}
        ENDS = {("out", "A", 0): x3, ("in", "B", 0): x3,
                ("out", "C", B - 1): x1, ("in", "D", B - 1): x1, ("norm", "D", B - 1): x0}

        stats_b = sb("stats_b", [P, TT, 6])
        mv_b, ve_b, rstd_b = sb("mv_b", [P, TT, 2]), sb("ve_b", [P, TT]), sb("rstd_b", [P, TT])

        upad = sb("upad", [P, T + 2])
        xs = sb("xs", [P, T])
        dt = sb("dt", [P, T])
        w = sb("w", [P, T])
        z = sb("z", [P, T])
        y = sb("y", [P, T])
        arena = sb("arena", [P, 10 * T])
        dA = arena[:, 0:4 * T].rearrange("p (r n) -> p r n", n=T)
        dBx = arena[:, 4 * T:6 * T].rearrange("p (r n) -> p r n", n=T)
        hst = arena[:, 6 * T:8 * T].rearrange("p (r n) -> p r n", n=T)
        prod = arena[:, 8 * T:10 * T].rearrange("p (r n) -> p r n", n=T)
        bc_parts = sb("bc_parts", [BC, T], BF16)
        bc_mid = sb("bc_mid", [BC, T], BF16)
        oT_mix = sb("oT_mix", [P, NH, HW])
        oT = {"A": arena[:, 6 * T:7 * T].rearrange("p (r n) -> p r n", n=HW)}
        oT.update({"C": oT["A"], "B": oT_mix, "D": oT_mix})
        conv = y
        sp_abs, sp_log = prod[:, 0, :], prod[:, 1, :]
        bc_f, bc_r = arena[0:BC, 4 * T:5 * T], arena[0:BC, 5 * T:6 * T]
        hid, lam_th, lam, kT, qT = xs[0:DH, :], dt, w, z, y
        kv = arena[:, 4 * T:5 * T].rearrange("p (r n) -> p r n", n=HW)
        xA = arena[:, 5 * T:6 * T].bitcast(F16)
        qs = arena[:, 8 * T:10 * T].rearrange("p (r n) -> p r n", n=HW)
        S = arena[:, 0:EF * HW].rearrange("p (r n) -> p r n", n=HW)
        x_parts = {s: sb(f"x_parts{s}", [P, 2 * T], F16) for s in "BD"}
        x_parts["A"] = xA

        def parts_of(s, b):
            buf = x_parts[{("B", 0): "D", ("D", B - 1): "B"}.get((s, b), s) if isinstance(b, int) else s]
            return buf[:, 0:T], buf[:, T:2 * T]

        def x_hi(s, b):
            return parts_of(s, b)[0]

        def x_lo(s, b):
            return parts_of(s, b)[1]

        XN = {"A": upad[:, 1:T + 1].rearrange("p (j d) -> p j d", d=D), "B": x0,
              "C": w[:].rearrange("p (j d) -> p j d", d=D), "D": x4}

        def stream(role, s, b):
            usual = {"in": XIN, "out": XOUT, "norm": XN}[role][s]
            return ENDS.get((role, s, b), usual) if isinstance(b, int) else usual

        def normT(s, b):
            return stream("norm", s, b)[:, :, :].rearrange("p j d -> p (j d)")

        at, stage = 0, {}
        for n, m in SPLIT.items():
            stage[n] = arena[:, at:at + m]
            at += m

        RS = {"B": 6, "D": 5}
        RG, RH = 3, 4
        s_ring = sb("s_ring", [P, max(RS.values()), HW])
        h_ring = sb("h_ring", [P, RH, HW])
        g_ring = sb("g_ring", [P, RG, HW])
        g_lg, g_e, g_sc, g_sel, g_m, g_ms, g_r1 = (sb(f"g_{n}", [P, TT, E]) for n in
                                                   ("lg", "e", "sc", "sel", "m", "ms", "r1"))
        g_top = sb("g_top", [P, TT, 8])
        g_idx = sb("g_idx", [P, TT, 8], U32)
        g_idf = sb("g_idf", [P, TT, 2])
        g_mx, g_sum, g_rs, g_den, g_rd = (sb(f"g_{n}", [P, TT]) for n in ("mx", "sum", "rs", "den", "rd"))
        g_parts = sb("g_parts", [P, TT, 3, E], BF16)
        gT = {s: sb(f"gT{s}", [3 * E, T], BF16) for s in "BD"}

        norm_uses = [("lnT0", 5, "act"), ("lnT1", 6, "act")]
        usesA = list(norm_uses)
        for name in ("cs", "k", "q", "lam"):
            usesA += [(f"{name}{h}", 5 + h, "act") for h in range(NH)]
        usesA += [(f"v{k}", 5 + k % 2, "dve") for k in range(LAG)]
        for k in range(VK + LAG):
            if k >= LAG and (k - LAG) % EF == EF - 1:
                usesA.append((f"o{(k - LAG) // EF}", 7, "act"))
            if k + LAG < VK:
                usesA.append((f"v{k + LAG}", 5 + k % 2, "dve"))
        usesA += [(f"outT{h}", 5 + h, "dve") for h in range(NH)]
        usesC = list(norm_uses)
        for name in ("u", "z", "dt", "bc"):
            usesC += [(f"{name}{h}", 5 + h, "act") for h in range(NH)]
        ring = 0
        for s in range(NS + 2):
            for kind, n in (("B", s), ("C", s - 2)):
                if 0 <= n < NS:
                    for h in range(NH):
                        usesC.append((f"{kind}{n}_{h}", 5 + ring % 3, "dve"))
                        ring += 1
        usesC += [(f"o{h}", 5 + h, "act") for h in range(NH)] + [(f"outT{h}", 5 + h, "dve") for h in range(NH)]
        usesP = norm_uses + [("logits", 7, "dve")]

        def gate_first(s, k):
            if not 0 <= k < NH * NT[s]:
                return None
            h, i = divmod(k, NT[s])
            e = TILES[s][i][1]
            if e is None or (i and TILES[s][i - 1][1] == e):
                return None
            return h * E + e

        def mixture_uses(s):
            n, uses, ra, rb = NH * NT[s], [], 0, 0
            for k in range(n + DOWN_LAG):
                rows = [f"g{q}"] if (q := gate_first(s, k - GATE_LAG)) is not None else []
                for name in (["gT"] if k == GATE_LAG else []) + rows + ([f"a{k}"] if k < n else []):
                    uses.append((name, ra % 2, "act"))
                    ra += 1
                if 0 <= k - SECOND_LAG < n:
                    uses.append((f"b{k - SECOND_LAG}", 2 + rb % 2, "dve"))
                    rb += 1
                if k >= DOWN_LAG and (k - DOWN_LAG) % NT[s] == NT[s] - 1:
                    uses.append((f"y{(k - DOWN_LAG) // NT[s]}", 4, "act"))
            return uses + [(f"outT{h}", 7, "dve") for h in range(NH)]

        U = {}
        for s, uses in (("A", usesA), ("B", mixture_uses("B")), ("C", usesC), ("D", mixture_uses("D")),
                        ("PB", usesP), ("PD", usesP)):
            U[s] = BankUses(uses, sem(f"{s}_bank_filled"),
                            {"act": sem(f"{s}_bank_read_act"), "dve": sem(f"{s}_bank_read_dve")})
        NORM_U = {"A": "A", "B": "PB", "C": "C", "D": "PD"}

        s_w = {n: sem(f"loaded_weights_{n}") for n in "ABCD"}
        s_st = sem("staged_weights")
        s_cons, s_cons0 = sem("constants_ready"), sem("zeros_ready")
        s_turn_dve, s_turn_pool = sem("dve_wait_passed"), sem("pool_wait_passed")
        s_base, s_lamc = sem("tanh_decay_ready"), sem("decay_scalars_ready")
        s_wm, s_wt, s_ws, s_hi, s_lo = (sem(n) for n in ("weight_maxima", "weight_max_of_all", "weight_scales",
                                                         "weight_hi_parts", "weight_lo_parts"))
        x_in, x_out = signal("x_loaded", 16), Signal(sem("x_stored"), 16, first=16)
        stats = {s: signal(f"{s}_stats_done", TT) for s in "ABCD"}
        mv = {s: signal(f"{s}_mean_var_done", TT) for s in "ABCD"}
        veps = {s: signal(f"{s}_var_eps_done", 1) for s in "ABCD"}
        rstd = {s: signal(f"{s}_rstd_done", 1) for s in "ABCD"}
        xn = {s: signal(f"{s}_normalised", TT) for s in "ABCD"}
        xT = {s: signal(f"{s}_norm_f32_moved", NH) for s in "ABD"}
        xl = {s: signal(f"{s}_x_lo_parts", 1) for s in "ABD"}
        a_lin, a_lam = signal("A_lam_scaled", NH), signal("A_lam_clipped", NH)
        a_scan, a_qs = signal("A_scan", VK), signal("A_qs", VK)
        c_conv = signal("C_conv_steps", 3)
        c_xs = signal("C_xs", 1)
        c_sp = signal("C_softplus_parts", NH + 2)
        c_dt, c_w = signal("C_dt", 1), signal("C_w", 1)
        c_hi, c_r, c_mid = signal("C_bc_hi", 1), signal("C_bc_rest", 1), signal("C_bc_mid", 1)
        c_lo, c_midc = signal("C_bc_lo", 1), signal("C_bc_mid_placed", 1)
        c_dA, c_scan = signal("C_dA", NS), signal("C_scan", NS)
        c_sum, c_yz = signal("C_sum", NS - 1), signal("C_y_gated", 1)
        GATE_STEPS = {"B": 18, "D": 15}
        g_step = {s: signal(f"{s}_gate_steps", GATE_STEPS[s]) for s in "BD"}
        g_exp, g_done = ({s: signal(f"{s}_gate_{n}", 1) for s in "BD"} for n in ("exp", "parts"))
        GATED = {s: NH * sum(e is not None for _, e, _, _ in TILES[s]) for s in "BD"}
        m_sg = {s: Signal(sem(f"{s}_silu_gated"), GATED[s], first=1) for s in "BD"}

        OTHER = {"B": "D", "D": "B"}

        def wait_silu_slot(eng, s, b, k, done):
            if k >= RS[s]:
                U[s].wait_read(eng, b, f"b{k - RS[s]}")
                return
            o = OTHER[s]
            last = [j for j in range(NH * NT[o] - RS[o], NH * NT[o]) if j % RS[o] == k % RS[s]]
            if last:
                U[o].wait_read_before(eng, done[o], f"b{last[0]}")

        def gated_to(s, k):
            return sum(TILES[s][i % NT[s]][1] is not None for i in range(k + 1))

        N_W = {"A": 8, "B": 4, "C": 13, "D": 3}
        LAST_OUT = f"outT{NH - 1}"

        def wait_weights(eng, s):
            eng.wait_ge(s_w[s], 16 * N_W[s])

        def half(ap, h):
            return ap[:, h * HW:(h + 1) * HW]

        def wait_banks(eng, stages, done):
            for s in stages:
                U[s].wait_all_read(eng, done[s])

        def mixture_step(e, s, b, k, done, before):
            e.tile(s, b, k, done)
            if before:
                o, ob = before
                if k < DOWN_LAG:
                    e.tile(o, ob, NH * NT[o] + k, done)
                for h in range(NH):
                    if k == DOWN_LAG + h:
                        e.mixture_out(o, ob, h, done)

        def mixture_rest(e, s, b, done):
            n = NH * NT[s]
            for k in range(n, n + DOWN_LAG):
                e.tile(s, b, k, done)
            for h in range(NH):
                e.mixture_out(s, b, h, done)

        def attention_alone(e, a, done):
            e.norm("A", a)
            e.norm_transposed("A", a, done)
            e.attention_start(a)
            for u in range(VK + LAG):
                e.attention_step(a, u, done)
            for h in range(NH):
                e.attention_end(a, h)

        def attention_beside(e, a, s, b, done, prep, before):
            n = NH * NT[s]
            first, last = DOWN_LAG, n - 4
            units = steady((first, last, VK + LAG), n)
            for k in range(n):
                mixture_step(e, s, b, k, done, before)
                if k == 0:
                    e.norm("A", a)
                if k == 1:
                    e.norm_transposed("A", a, done)
                if k == 2:
                    e.attention_start(a)
                for u in units.get(k, ()):
                    e.attention_step(a, u, done)
                if k == last:
                    for h in range(NH):
                        e.attention_end(a, h)
                if k == last + 1:
                    e.norm(*prep)
                if k == last + 2:
                    e.norm_transposed(*prep, done)
                if k == last + 3:
                    e.logits(*prep)
            e.gates(*prep)

        def ssm_beside(e, c, s, b, done, prep, before):
            n = NH * NT[s]
            first, last = (10, n - 7) if s == "B" else (7, n - 6)
            units = steady((first, last, 3 * (NS + 2)), n)
            for k in range(n):
                mixture_step(e, s, b, k, done, before)
                if k == 0:
                    e.norm("C", c)
                if k == 1:
                    e.norm_transposed("C", c, done)
                if k == 2:
                    e.ssm_in(c)
                if k == first - 4:
                    e.ssm_rates(c)
                if k == first - 2:
                    e.ssm_parts(c)
                for u in units.get(k, ()):
                    e.ssm_step(c, u, done)
                if k == last:
                    e.ssm_gate(c)
                if k == last + 1:
                    e.ssm_out(c)
                if k == last + 3:
                    e.norm(*prep)
                if k == last + 4:
                    e.norm_transposed(*prep, done)
                if k == last + 5:
                    e.logits(*prep)
            e.gates(*prep)

        def prepare(e, s, b, done):
            e.norm(s, b)
            e.norm_transposed(s, b, done)
            e.logits(s, b)
            e.gates(s, b)

        def counts(**n):
            return n

        def program(e, eng):
            attention_alone(e, 0, counts(A=0, C=0, PB=0, PD=0, B=0, D=0))
            prepare(e, "B", 0, counts(A=1, C=0, PB=0, PD=0))
            attention_beside(e, 1, "B", 0, counts(A=1, B=0, C=0, D=0, PB=1, PD=0), ("B", 1), None)
            mixture_rest(e, "B", 0, counts(A=2, B=0, C=0, D=0, PB=2, PD=0))
            first = 0
            ssm_beside(e, first, "B", first + 1, counts(A=2, B=1, C=0, D=0, PB=2, PD=0), ("D", first), None)
            attention_beside(e, 2, "D", 0, counts(A=2, B=2, C=1, D=0, PB=2, PD=1), ("B", 2), ("B", 1))
            with eng.Fori(1, B - 2) as i:
                ssm_beside(e, i, "B", i + 1, counts(A=i + 2, B=i + 1, C=i, D=i, PB=i + 2, PD=i), ("D", i),
                           ("D", i - 1))
                attention_beside(e, i + 2, "D", i, counts(A=i + 2, B=i + 2, C=i + 1, D=i, PB=i + 2, PD=i + 1),
                                 ("B", i + 2), ("B", i + 1))
            i = B - 2
            ssm_beside(e, i, "B", i + 1, counts(A=B, B=i + 1, C=i, D=i, PB=B, PD=i), ("D", i), ("D", i - 1))
            mixture_rest(e, "B", i + 1, counts(A=B, B=i + 1, C=i + 1, D=i, PB=B, PD=i + 1))
            ssm_beside(e, i + 1, "D", i, counts(A=B, B=B, C=i + 1, D=i, PB=B, PD=i + 1), ("D", i + 1), None)
            mixture_rest(e, "D", i, counts(A=B, B=B, C=B, D=i, PB=B, PD=B))
            for k in range(NH * NT["D"]):
                mixture_step(e, "D", i + 1, k, counts(A=B, B=B, C=B, D=i + 1, PB=B, PD=B), None)
            mixture_rest(e, "D", i + 1, counts(A=B, B=B, C=B, D=i + 1, PB=B, PD=B))

        def nothing(*_):
            pass

        block = ctx.enter_context(nc.Block())

        @block.sync
        def _(sp):
            xv = t["x"].rearrange("b (j p) d -> b p j d", p=P)
            ov = out.rearrange("b (j p) d -> b p j d", p=P)

            def load_x(b):
                sp.dma_start(x0[:, :, :], xv[b]).then_inc(x_in.sem, 16)

            sp.sem_inc(x_out.sem, x_out.first)
            load_x(0)
            for n in SPLIT:
                sp.dma_start(stage[n], t[n]).then_inc(s_st, 16)
            for dst, n in ((Wk, "Wk"), (Wq, "Wq"), (cs1, "cs1"), (cs2, "cs2"), (Wo, "Wo")):
                sp.dma_start(dst[:], t[n]).then_inc(s_w["A"], 16)
            for n in ("decay", "cs_b2"):
                sp.dma_start(col[n], t[n]).then_inc(s_w["A"], 16)
            sp.dma_start(col["cs_b1"][0:DH], t["cs_b1"]).then_inc(s_w["A"], 16)
            sp.dma_start(Wgate["B"][:], t["Wg0"]).then_inc(s_w["B"], 16)
            per = -(-R0 // P)
            w2v = W2["B"][:, :, :].rearrange("p (e j) d -> p e j d", j=per)
            for j in range(per):
                rows = min(P, R0 - j * P)
                sp.dma_start(w2v[0:rows, :, j, :],
                             t["W2_0"][:, j * P:j * P + rows, :].rearrange("e r d -> r e d")).then_inc(s_w["B"], 16)
            for dst, n in ((Win, "Win"), (Wz, "Wz"), (Wdt, "Wdt"), (Wout, "Wout"), (Wbc, "Wbc"), (convw, "convw"), (A_sb, "A")):
                sp.dma_start(dst[:], t[n]).then_inc(s_w["C"], 16)
            for n in ("b_in", "bg", "bout", "convb", "bdt"):
                sp.dma_start(col[n], t[n]).then_inc(s_w["C"], 16)
            sp.dma_start(col["bbc"][0:BC], t["bbc"]).then_inc(s_w["C"], 16)
            sp.dma_start(Wgate["D"][:], t["Wg1"]).then_inc(s_w["D"], 16)
            sp.dma_start(gate_bias[:], t["gate_bias"]).then_inc(s_w["D"], 16)
            sp.dma_start(W2["D"][:], t["W2_1"].rearrange("e r d -> r e d")).then_inc(s_w["D"], 16)

            def next_x(b):
                sp.wait_ge(xl["B"].sem, xl["B"].at(b, 1))
                U["PB"].wait_filled(sp, b, "logits")
                load_x(b + 1)

            def store_x(b):
                U["D"].wait_read(sp, b, LAST_OUT)
                sp.dma_start(ov[b], x4[:, :, :]).then_inc(x_out.sem, 16)

            next_x(0)
            next_x(1)
            with sp.Fori(0, B - 3) as b:
                store_x(b)
                next_x(b + 2)
            for b in range(B - 3, B):
                store_x(b)
            sp.wait_ge(x_out.sem, x_out.at(B, 0))

        @block.gpsimd
        def _(pool):
            for s in "BD":
                pool.sem_inc(m_sg[s].sem, 1)
            zeroed = (ident, ident16, sel_bc, sel_gate)
            for m in zeroed:
                pool.memset(m[:], 0.0).then_inc(s_cons0, 1)
            pool.memset(neg_half[:], -0.5)
            pool.memset(eps_t[:], EPS)
            pool.memset(upad[:, 0:1], 0.0)
            pool.memset(upad[:, T + 1:T + 2], 0.0)
            pool.iota(expert_i[:], pattern=[[0, TT], [1, E]], base=0, channel_multiplier=0).then_inc(s_cons0, 1)
            pool.wait_ge(s_cons0, len(zeroed) + 1)
            pool.tensor_copy(expert_no[:, :, :].rearrange("p a b -> p (a b)"), expert_i[:]).then_inc(s_cons, 1)
            for m in (ident, ident16):
                pool.affine_select(out=m[:], in_=m[:], compare_op=ALU.not_equal, fill=1.0, base=0,
                                   pattern=[[-1, P]], channel_multiplier=1).then_inc(s_cons, 1)
            done = 0
            for m, rows in ((sel_bc, 2 * NS), (sel_gate, E)):
                for part in range(3):
                    pool.affine_select(out=m[:], in_=m[:], compare_op=ALU.not_equal, fill=1.0, base=-part * rows,
                                       pattern=[[-1, rows], [0, P]], channel_multiplier=1).then_inc(s_cons, 1)
                    done += 1
                    pool.wait_ge(s_cons, 3 + done)
            pool.wait_ge(s_wm, 2 * len(SPLIT) + 2)
            pool.partition_all_reduce(wtop[:], wabs[:], P, bass.bass_isa.ReduceOp.max).then_inc(s_wt, 1)

            def norm(s, b):
                pool.wait_ge(mv[s].sem, mv[s].at(b, TT))
                pool.tensor_tensor(ve_b[:], mv_b[:, :, 1], eps_t[:], ALU.add).then_inc(veps[s].sem, 1)
                pool.wait_ge(veps[s].sem, veps[s].at(b, 1))
                pool.tensor_tensor(rstd_b[:], ve_b[:], neg_half[:], ALU.pow).then_inc(rstd[s].sem, 1)

            def attention_step(b, u, done):
                k = u - 1
                if not 0 <= k < VK:
                    return
                if k == 0:
                    U["A"].wait_read(pool, b, f"q{NH - 1}")
                pool.wait_ge(a_scan.sem, a_scan.at(b, k + 1))
                pool.tensor_tensor(qs[:, k % 4, :], half(qT, k // EF), S[:, k % EF, :], ALU.mult).then_inc(a_qs.sem, 1)

            def ssm_gate(b):
                add_state(b, NS - 1)

            def add_state(b, n):
                U["C"].wait_read(pool, b, f"C{n}_{NH - 1}")
                if n > 1:
                    pool.wait_ge(c_sum.sem, c_sum.at(b, n - 1))
                pool.tensor_tensor(y[:], y[:], prod[:, n % 2, :], ALU.add).then_inc(c_sum.sem, 1)

            def ssm_step(b, u, done):
                s, part = divmod(u, 3)
                if part == 0 and 1 <= s - 3:
                    add_state(b, s - 3)

            def tile(s, b, step, done):
                k = step - GATE_LAG
                if not 0 <= k < NH * NT[s]:
                    return
                _, e, rows, _ = TILES[s][k % NT[s]]
                if e is None:
                    return
                q = k // NT[s] * E + e
                U[s].wait_read(pool, b, f"g{q}")
                U[s].wait_read(pool, b, f"a{k}")
                slot = s_ring[0:rows, k % RS[s], :]
                pool.tensor_tensor(slot, slot, g_ring[0:rows, q % RG, :], ALU.mult).then_inc(m_sg[s].sem, 1)

            program(Steps(
                norm=norm, norm_transposed=nothing, attention_start=nothing, attention_step=attention_step,
                attention_end=nothing, ssm_in=nothing, ssm_rates=nothing, ssm_parts=nothing, ssm_step=ssm_step,
                ssm_gate=ssm_gate, ssm_out=nothing, tile=tile, mixture_out=nothing, logits=nothing, gates=nothing), pool)

        @block.tensor
        def _(pe):
            pe.wait_ge(s_cons, 9)
            for s in "ABCD":
                wait_weights(pe, s)
            pe.wait_ge(s_lo, len(SPLIT))

            def fill(s, b, name, cols=HW, rows=P):
                U[s].wait_bank_free(pe, b, name)
                return banks[U[s].bank(name)][0:rows, 0:cols]

            def filled(s, ins):
                ins.then_inc(U[s].filled.sem, 1)

            def product(bank, weight, c0, c1, s, b, h):
                hi, lo = Whi[weight][:, c0:c1], Wlo[weight][:, c0:c1]
                xh, xlow = half(x_hi(s, b), h), half(x_lo(s, b), h)
                pe.matmul(bank, hi, xh, start=True, stop=False)
                pe.matmul(bank, hi, xlow, start=False, stop=False)
                return pe.matmul(bank, lo, xh, start=False, stop=True)

            def norm_transposed(s, b, done):
                u = NORM_U[s]
                wait_banks(pe, ("A", "C", "PB", "PD"), done_now(s, b, done))
                for h in range(NH):
                    bank = fill(u, b, f"lnT{h}")
                    for j in range(TH):
                        pe.wait_ge(xn[s].sem, xn[s].at(b, h * TH + j + 1))
                        last = pe.transpose(bank[:, j * P:(j + 1) * P], stream("norm", s, b)[:, h * TH + j, :], ident[:])
                    filled(u, last)

            def done_now(s, b, done):
                now = dict(done)
                if s == "B":
                    now["A"] = b + 1
                if s == "D":
                    now["C"] = b + 1
                return now

            def transpose_out(s, b, h, acc):
                U[s].wait_read(pe, b, f"{acc}{h}")
                bank = fill(s, b, f"outT{h}")
                for j in range(TH):
                    last = pe.transpose(bank[:, j * P:(j + 1) * P], oT[s][:, h, j * P:(j + 1) * P], ident[:])
                filled(s, last)

            def wait_mixtures_out(done):
                for s in "BD":
                    pe.wait_ge(U[s].read["dve"].sem, U[s].read["dve"].at(done[s], 0))

            def value(b, k):
                f = k % EF
                filled("A", product(fill("A", b, f"v{k}"), "Wv", f * P, (f + 1) * P, "A", b, k // EF))

            def attention_start(b):
                U["A"].wait_read(pe, b, f"lnT{NH - 1}")
                for name, wt, rows in (("cs", cs1, DH), ("k", Wk, P), ("q", Wq, P)):
                    for h in range(NH):
                        filled("A", pe.matmul(fill("A", b, f"{name}{h}", rows=rows), wt[:], half(normT("A", b), h),
                                              start=True, stop=True))
                for h in range(NH):
                    U["A"].wait_read(pe, b, f"cs{h}")
                    filled("A", pe.matmul(fill("A", b, f"lam{h}"), cs2[:], half(hid, h), start=True, stop=True))
                pe.wait_ge(xl["A"].sem, xl["A"].at(b, 1))
                for k in range(LAG):
                    value(b, k)

            def attention_step(b, u, done):
                k = u - LAG
                if k >= 0:
                    f = k % EF
                    if k == 0:
                        wait_mixtures_out(done)
                    if f == 0:
                        fill("A", b, f"o{k // EF}")
                    pe.wait_ge(a_qs.sem, a_qs.at(b, k + 1))
                    last = pe.matmul(banks[7][:], Wo[:, f, :], qs[:, k % 4, :], start=(f == 0), stop=(f == EF - 1))
                    if f == EF - 1:
                        filled("A", last)
                if u + LAG < VK:
                    value(b, u + LAG)

            def attention_end(b, h):
                transpose_out("A", b, h, "o")

            def ssm_in(b):
                U["C"].wait_read(pe, b, f"lnT{NH - 1}")
                for name, wt in (("u", Win), ("z", Wz)):
                    for h in range(NH):
                        filled("C", pe.matmul(fill("C", b, f"{name}{h}"), wt[:], half(normT("C", b), h), start=True, stop=True))

            def ssm_rates(b):
                pe.wait_ge(c_xs.sem, c_xs.at(b, 1))
                for name, wt, rows in (("dt", Wdt, P), ("bc", Wbc, BC)):
                    for h in range(NH):
                        filled("C", pe.matmul(fill("C", b, f"{name}{h}", rows=rows), wt[:], half(xs, h),
                                              start=True, stop=True))

            def ssm_step(b, u, done):
                s, part = divmod(u, 3)
                if u == 0:
                    wait_mixtures_out(done)
                    pe.wait_ge(c_lo.sem, c_lo.at(b, 1))
                    pe.wait_ge(c_midc.sem, c_midc.at(b, 1))
                for kind, n, when in (("B", s, 0), ("C", s - 2, 1)):
                    if part == when and 0 <= n < NS:
                        row = n + NS * (kind == "C")
                        for h in range(NH):
                            filled("C", pe.matmul(fill("C", b, f"{kind}{n}_{h}"), sel_bc[:, row, :],
                                                  half(bc_parts, h), start=True, stop=True))

            def ssm_out(b):
                pe.wait_ge(c_yz.sem, c_yz.at(b, 1))
                for h in range(NH):
                    filled("C", pe.matmul(fill("C", b, f"o{h}"), Wout[:], half(w, h), start=True, stop=True))
                for h in range(NH):
                    transpose_out("C", b, h, "o")

            def logits(s, b):
                u = NORM_U[s]
                U[u].wait_read(pe, b, f"lnT{NH - 1}")
                bank = fill(u, b, "logits", cols=TT * E)
                for j in range(TT):
                    last = pe.matmul(bank[:, j * E:(j + 1) * E], normT(s, b)[:, j * P:(j + 1) * P], Wgate[s][:],
                                     start=True, stop=True)
                filled(u, last)

            def gate_transposes(s, b):
                pe.wait_ge(g_done[s].sem, g_done[s].at(b, 1))
                fill(s, b, "gT")
                gbank = banks[U[s].bank("gT")].bitcast(BF16)
                for j in range(TT):
                    last = pe.transpose(gbank[0:3 * E, j * P:(j + 1) * P],
                                        g_parts[:, j, :, :].rearrange("p c e -> p (c e)"), ident16[:])
                filled(s, last)

            def gate_rows(s, b, q):
                if q == 0:
                    U[s].wait_read(pe, b, "gT")
                filled(s, pe.matmul(fill(s, b, f"g{q}"), sel_gate[:, q % E, :], half(gT[s], q // E),
                                    start=True, stop=True))

            def down_product(s, b, k, done):
                h, i = divmod(k, NT[s])
                rows = TILES[s][i][2]
                U[s].wait_read(pe, b, f"b{k}")
                if k == 0:
                    U[OTHER[s]].wait_last_read(pe, done[OTHER[s]], 4)
                if i == 0:
                    fill(s, b, f"y{h}")
                last = pe.matmul(banks[4][:], W2[s][0:rows, i, :], h_ring[0:rows, k % RH, :],
                                 start=(i == 0), stop=(i == NT[s] - 1))
                if i == NT[s] - 1:
                    filled(s, last)

            def tile(s, b, k, done):
                n, o = NH * NT[s], OTHER[s]
                if k == 0:
                    U[s].wait_all_read(pe, done[s])
                    for bank in (0, 1):
                        U[o].wait_last_read(pe, done[o], bank)
                    pe.wait_ge(xl[s].sem, xl[s].at(b, 1))
                if k == GATE_LAG:
                    gate_transposes(s, b)
                q = gate_first(s, k - GATE_LAG)
                if q is not None:
                    gate_rows(s, b, q)
                if k < n:
                    h, i = divmod(k, NT[s])
                    _, _, rows, r0 = TILES[s][i]
                    filled(s, product(fill(s, b, f"a{k}", rows=rows), W1[s], r0, r0 + rows, s, b, h))
                j = k - SECOND_LAG
                if j == 0:
                    for bank in (2, 3):
                        U[o].wait_last_read(pe, done[o], bank)
                if 0 <= j < n:
                    h, i = divmod(j, NT[s])
                    _, _, rows, r0 = TILES[s][i]
                    filled(s, product(fill(s, b, f"b{j}", rows=rows), W3[s], r0, r0 + rows, s, b, h))
                if k >= DOWN_LAG:
                    down_product(s, b, k - DOWN_LAG, done)

            def mixture_out(s, b, h, done):
                if h == 0:
                    for u in ("A", "C", "PB", "PD"):
                        U[u].wait_all_read(pe, done[u])
                transpose_out(s, b, h, "y")

            program(Steps(
                norm=nothing, norm_transposed=norm_transposed, attention_start=attention_start,
                attention_step=attention_step, attention_end=attention_end, ssm_in=ssm_in, ssm_rates=ssm_rates,
                ssm_parts=nothing, ssm_step=ssm_step, ssm_gate=nothing, ssm_out=ssm_out, tile=tile,
                mixture_out=mixture_out, logits=logits, gates=nothing), pe)

        @block.scalar
        def _(act):
            for s in U:
                act.sem_inc(U[s].read["act"].sem, FIRST)
            for s in "AC":
                wait_weights(act, s)
            act.activation(tb[:], col["decay"], ACT.Tanh, scale=0.5).then_inc(s_base, 1)
            act.mul(half_b2[:], col["cs_b2"], 0.5).then_inc(s_base, 1)
            act.wait_ge(s_base, 2)
            act.wait_ge(s_ws, 5)
            for n in SPLIT:
                act.activation(Whi[n][:], stage[n], ACT.Copy, scale=up[n]).then_inc(s_hi, 1)

            def read(s, ins):
                ins.then_inc(U[s].read["act"].sem, 1)

            def bank(s, name, rows=P):
                return banks[U[s].bank(name)][0:rows, :]

            def norm_transposed(s, b, done):
                u = NORM_U[s]
                for h in range(NH):
                    U[u].wait_filled(act, b, f"lnT{h}")
                    ins = act.copy(half(normT(s, b), h), bank(u, f"lnT{h}"))
                    if s != "C":
                        ins.then_inc(xT[s].sem, 1)
                        ins = act.copy(half(x_hi(s, b), h), bank(u, f"lnT{h}"))
                    read(u, ins)

            def attention_start(b):
                for h in range(NH):
                    U["A"].wait_filled(act, b, f"cs{h}")
                    read("A", act.activation(half(hid, h), bank("A", f"cs{h}", DH), ACT.Tanh, bias=col["cs_b1"][0:DH]))
                for h in range(NH):
                    U["A"].wait_filled(act, b, f"k{h}")
                    read("A", act.activation(half(kT, h), bank("A", f"k{h}"), ACT.Copy, scale=down["Wv"]))
                for h in range(NH):
                    U["A"].wait_filled(act, b, f"q{h}")
                    read("A", act.copy(half(qT, h), bank("A", f"q{h}")))
                for h in range(NH):
                    U["A"].wait_filled(act, b, f"lam{h}")
                    ins = act.activation(half(lam_th, h), bank("A", f"lam{h}"), ACT.Tanh, bias=half_b2[:], scale=0.5)
                    read("A", ins)

            def attention_step(b, u, done):
                k = u - LAG - 1
                if k >= 0 and k % EF == EF - 1:
                    h = k // EF
                    U["A"].wait_filled(act, b, f"o{h}")
                    read("A", act.copy(oT["A"][:, h, :], bank("A", f"o{h}")))

            def attention_end(b, h):
                if h == 0:
                    attention_step(b, VK + LAG, None)

            def ssm_in(b):
                for h in range(NH):
                    U["C"].wait_filled(act, b, f"u{h}")
                    read("C", act.activation(upad[:, 1 + h * HW:1 + (h + 1) * HW], bank("C", f"u{h}"), ACT.Identity,
                                             bias=col["b_in"]))
                for h in range(NH):
                    U["C"].wait_filled(act, b, f"z{h}")
                    read("C", act.activation(half(z, h), bank("C", f"z{h}"), ACT.Silu, bias=col["bg"]))

            def ssm_rates(b):
                act.wait_ge(c_conv.sem, c_conv.at(b, 3))
                act.activation(xs[:], conv[:], ACT.Silu).then_inc(c_xs.sem, 1)
                for h in range(NH):
                    U["C"].wait_filled(act, b, f"dt{h}")
                    act.activation(half(sp_abs, h), bank("C", f"dt{h}"), ACT.Abs, bias=col["bdt"]).then_inc(c_sp.sem, 1)
                    read("C", act.activation(half(dt, h), bank("C", f"dt{h}"), ACT.Relu, bias=col["bdt"]))
                for h in range(NH):
                    U["C"].wait_filled(act, b, f"bc{h}")
                    read("C", act.activation(half(bc_f, h), bank("C", f"bc{h}", BC), ACT.Identity, bias=col["bbc"][0:BC]))
                U["C"].wait_read(act, b, f"bc{NH - 1}")
                act.copy(bc_parts[:], bc_f).then_inc(c_hi.sem, 1)
                act.wait_ge(c_sp.sem, c_sp.at(b, NH))
                act.activation(sp_abs, sp_abs, ACT.Exp, scale=-1.0).then_inc(c_sp.sem, 1)
                act.wait_ge(c_sp.sem, c_sp.at(b, NH + 1))
                act.activation(sp_log, sp_abs, ACT.Ln, bias=1.0).then_inc(c_sp.sem, 1)

            def ssm_parts(b):
                act.wait_ge(c_r.sem, c_r.at(b, 1))
                for dst, rows, s in ((bc_parts, slice(2 * NS, 4 * NS), c_midc), (bc_mid, slice(4 * NS, 6 * NS), c_mid)):
                    act.copy(dst[rows, :], bc_r[rows, :]).then_inc(s.sem, 1)

            def decay(b, n):
                if n >= 4:
                    act.wait_ge(c_scan.sem, c_scan.at(b, n - 3))
                act.activation(dA[:, n % 4, :], dt[:], ACT.Exp, scale=A_sb[:, n:n + 1]).then_inc(c_dA.sem, 1)

            def ssm_step(b, u, done):
                s, part = divmod(u, 3)
                if u == 0:
                    act.wait_ge(c_dt.sem, c_dt.at(b, 1))
                    decay(b, 0)
                    decay(b, 1)
                elif part == 0 and s % 2 == 1 and s + 1 < NS:
                    decay(b, s + 1)
                    decay(b, s + 2)

            def ssm_out(b):
                for h in range(NH):
                    U["C"].wait_filled(act, b, f"o{h}")
                    read("C", act.activation(oT["C"][:, h, :], bank("C", f"o{h}"), ACT.Identity, bias=col["bout"]))

            def gates(s, b):
                u = NORM_U[s]
                U[u].wait_read(act, b, "logits")
                act.activation(g_e[:], g_lg[:], ACT.Exp).then_inc(g_exp[s].sem, 1)

            def gate_rows(s, b, q, done):
                if q >= RG:
                    k = max(k for k in range(NH * NT[s]) if gate_first(s, k) == q - RG + 1) - 1
                    act.wait_ge(m_sg[s].sem, m_sg[s].at(b, gated_to(s, k)))
                elif q == 0:
                    o = m_sg[OTHER[s]]
                    act.wait_ge(o.sem, o.at(done[OTHER[s]], 0))
                U[s].wait_filled(act, b, f"g{q}")
                read(s, act.copy(g_ring[:, q % RG, :], bank(s, f"g{q}")))

            def tile(s, b, k, done):
                if k == GATE_LAG:
                    U[s].wait_filled(act, b, "gT")
                    read(s, act.copy(gT[s][:], banks[U[s].bank("gT")].bitcast(BF16)[0:3 * E, :]))
                q = gate_first(s, k - GATE_LAG)
                if q is not None:
                    gate_rows(s, b, q, done)
                if k < NH * NT[s]:
                    rows = TILES[s][k % NT[s]][2]
                    U[s].wait_filled(act, b, f"a{k}")
                    wait_silu_slot(act, s, b, k, done)
                    read(s, act.activation(s_ring[0:rows, k % RS[s], :], bank(s, f"a{k}", rows), ACT.Silu,
                                           scale=down[W1[s]][0:rows]))
                h, i = divmod(k - DOWN_LAG, NT[s])
                if h >= 0 and i == NT[s] - 1:
                    U[s].wait_filled(act, b, f"y{h}")
                    read(s, act.copy(oT[s][:, h, :], bank(s, f"y{h}")))

            program(Steps(
                norm=nothing, norm_transposed=norm_transposed, attention_start=attention_start,
                attention_step=attention_step, attention_end=attention_end, ssm_in=ssm_in, ssm_rates=ssm_rates,
                ssm_parts=ssm_parts, ssm_step=ssm_step, ssm_gate=nothing, ssm_out=ssm_out, tile=tile,
                mixture_out=nothing, logits=nothing, gates=gates), act)

        @block.vector
        def _(dve):
            for s in U:
                dve.sem_inc(U[s].read["dve"].sem, FIRST)
            for s in "ACD":
                wait_weights(dve, s)
            dve.wait_ge(s_cons, 9)
            dve.wait_ge(s_base, 2)
            dve.tensor_scalar(lam_mul[:], tb[:], 0.05, 0.05, ALU.mult, ALU.add).then_inc(s_lamc, 1)
            dve.tensor_scalar(lam_add[:], tb[:], 0.55, 0.55, ALU.mult, ALU.add).then_inc(s_lamc, 1)
            dve.wait_ge(s_st, 16 * len(SPLIT))
            for i, n in enumerate(SPLIT):
                dve.tensor_reduce(wmax[:, i:i + 1], stage[n], AX.X, ALU.max).then_inc(s_wm, 1)
                dve.tensor_reduce(wmin[:, i:i + 1], stage[n], AX.X, ALU.min).then_inc(s_wm, 1)
            dve.wait_ge(s_wm, 2 * len(SPLIT))
            dve.scalar_tensor_tensor(out=wabs[:], in0=wmin[:], scalar=-1.0, in1=wmax[:], op0=ALU.mult,
                                     op1=ALU.max).then_inc(s_wm, 1)
            dve.wait_ge(s_wm, 2 * len(SPLIT) + 1)
            dve.tensor_scalar(wabs[:], wabs[:], 1e-30, None, ALU.max).then_inc(s_wm, 1)
            dve.wait_ge(s_wt, 1)
            dve.tensor_scalar(wexp[:], wtop[:].bitcast(U32), 0x7F800000, None, ALU.bitwise_and).then_inc(s_ws, 1)
            dve.wait_ge(s_ws, 1)
            TOP = 12
            dve.tensor_scalar(wscale[:], wexp[:], -1.0, float((254 + TOP) << 23), ALU.mult, ALU.add).then_inc(s_ws, 1)
            dve.tensor_scalar(winv[:], wexp[:], float(TOP << 23), None, ALU.subtract).then_inc(s_ws, 1)
            dve.wait_ge(s_ws, 3)
            dve.wait_ge(s_lamc, 2)
            dve.sem_inc(s_ws, 2)
            for i, n in enumerate(SPLIT):
                dve.wait_ge(s_hi, i + 1)
                dve.scalar_tensor_tensor(out=Wlo[n][:], in0=stage[n], scalar=up[n], in1=Whi[n][:], op0=ALU.mult,
                                         op1=ALU.subtract).then_inc(s_lo, 1)
            dve.wait_ge(s_lo, len(SPLIT))

            def read(s, ins):
                ins.then_inc(U[s].read["dve"].sem, 1)

            def bank(s, name, rows=P):
                return banks[U[s].bank(name)][0:rows, :]

            BEFORE = {"B": "A", "C": "B", "D": "C"}

            def norm(s, b):
                x = stream("in", s, b)
                if s == "A":
                    dve.wait_ge(x_in.sem, x_in.at(b, 16))
                else:
                    U[BEFORE[s]].wait_read(dve, b, LAST_OUT)
                if stream("norm", s, b) is x4:
                    dve.wait_ge(x_out.sem, x_out.at(b, 0))
                for j in range(TT):
                    dve.bn_stats(stats_b[:, j, :], x[:, j, :]).then_inc(stats[s].sem, 1)
                for j in range(TT):
                    dve.wait_ge(stats[s].sem, stats[s].at(b, j + 1))
                    dve.sem_inc(s_turn_dve, 1)
                    dve.bn_aggr(mv_b[:, j, :], stats_b[:, j, :]).then_inc(mv[s].sem, 1)
                dve.wait_ge(mv[s].sem, mv[s].at(b, TT))
                dve.wait_ge(rstd[s].sem, rstd[s].at(b, 1))
                for j in range(TT):
                    dve.tensor_scalar(stream("norm", s, b)[:, j, :], x[:, j, :], mv_b[:, j, 0:1], rstd_b[:, j:j + 1],
                                      ALU.subtract, ALU.mult).then_inc(xn[s].sem, 1)

            def norm_transposed(s, b, done):
                if s != "C":
                    U[NORM_U[s]].wait_read(dve, b, f"lnT{NH - 1}")
                    dve.tensor_tensor(x_lo(s, b), normT(s, b), x_hi(s, b), ALU.subtract).then_inc(xl[s].sem, 1)

            def add_residual(s, b, h):
                U[s].wait_filled(dve, b, f"outT{h}")
                js = slice(h * TH, (h + 1) * TH)
                read(s, dve.tensor_tensor(stream("out", s, b)[:, js, :].rearrange("p j d -> p (j d)"),
                                          bank(s, f"outT{h}"),
                                          stream("in", s, b)[:, js, :].rearrange("p j d -> p (j d)"), ALU.add))

            def outer(b, k):
                U["A"].wait_filled(dve, b, f"v{k}")
                if k >= 2:
                    dve.wait_ge(a_scan.sem, a_scan.at(b, k - 1))
                read("A", dve.tensor_tensor(kv[:, k % 2, :], bank("A", f"v{k}"), half(kT, k // EF), ALU.mult))

            def attention_start(b):
                for h in range(NH):
                    U["A"].wait_read(dve, b, f"lam{h}")
                    dve.tensor_scalar(half(lam, h), half(lam_th, h), lam_mul[:], lam_add[:],
                                      ALU.mult, ALU.add).then_inc(a_lin.sem, 1)
                for h in range(NH):
                    dve.wait_ge(a_lin.sem, a_lin.at(b, h + 1))
                    dve.tensor_scalar(half(lam, h), half(lam, h), LAM_MAX, 0.0, ALU.min,
                                      ALU.max).then_inc(a_lam.sem, 1)
                outer(b, 0)

            def attention_step(b, k, done):
                if k >= VK:
                    return
                if k + 1 < VK:
                    outer(b, k + 1)
                h, f = divmod(k, EF)
                U["A"].wait_read(dve, b, f"v{k}")
                dve.wait_ge(a_lam.sem, a_lam.at(b, h + 1))
                if h:
                    dve.wait_ge(a_qs.sem, a_qs.at(b, k - EF + 1))
                dve.tensor_tensor_scan(S[:, f, :], half(lam, h), kv[:, k % 2, :],
                                       0.0 if h == 0 else S[:, f, HW - 1:HW], ALU.mult,
                                       ALU.add).then_inc(a_scan.sem, 1)

            def attention_end(b, h):
                add_residual("A", b, h)

            def ssm_in(b):
                U["C"].wait_read(dve, b, f"u{NH - 1}")
                dve.tensor_scalar(conv[:], upad[:, 1:T + 1], convw[:, 1:2], col["convb"], ALU.mult,
                                  ALU.add).then_inc(c_conv.sem, 1)
                for i in (0, 2):
                    dve.wait_ge(c_conv.sem, c_conv.at(b, 1 + i // 2))
                    dve.scalar_tensor_tensor(out=conv[:], in0=upad[:, i:T + i], scalar=convw[:, i:i + 1], in1=conv[:],
                                             op0=ALU.mult, op1=ALU.add).then_inc(c_conv.sem, 1)

            def ssm_parts(b):
                dve.wait_ge(c_hi.sem, c_hi.at(b, 1))
                dve.tensor_tensor(bc_r, bc_f, bc_parts[:], ALU.subtract).then_inc(c_r.sem, 1)
                dve.wait_ge(c_sp.sem, c_sp.at(b, NH + 2))
                dve.tensor_tensor(dt[:], dt[:], sp_log, ALU.add).then_inc(c_dt.sem, 1)
                dve.wait_ge(c_mid.sem, c_mid.at(b, 1))
                dve.tensor_tensor(bc_parts[4 * NS:6 * NS, :], bc_r[4 * NS:6 * NS, :], bc_mid[4 * NS:6 * NS, :],
                                  ALU.subtract).then_inc(c_lo.sem, 1)
                dve.wait_ge(c_dt.sem, c_dt.at(b, 1))
                dve.tensor_tensor(w[:], dt[:], xs[:], ALU.mult).then_inc(c_w.sem, 1)

            def ssm_step(b, u, done):
                s, part = divmod(u, 3)
                if u == 0:
                    dve.wait_ge(c_w.sem, c_w.at(b, 1))
                    dve.wait_ge(c_lo.sem, c_lo.at(b, 1))
                if part == 0 and s < NS:
                    for h in range(NH):
                        U["C"].wait_filled(dve, b, f"B{s}_{h}")
                        if s >= 2:
                            dve.wait_ge(c_scan.sem, c_scan.at(b, s - 1))
                        read("C", dve.tensor_tensor(half(dBx[:, s % 2, :], h), bank("C", f"B{s}_{h}"), half(w, h),
                                                    ALU.mult))
                if part == 1 and 0 <= s - 1 < NS:
                    n = s - 1
                    U["C"].wait_read(dve, b, f"B{n}_{NH - 1}")
                    dve.wait_ge(c_dA.sem, c_dA.at(b, n + 1))
                    if n >= 2:
                        U["C"].wait_read(dve, b, f"C{n - 2}_{NH - 1}")
                    dve.tensor_tensor_scan(hst[:, n % 2, :], dA[:, n % 4, :], dBx[:, n % 2, :], 0.0, ALU.mult,
                                           ALU.add).then_inc(c_scan.sem, 1)
                if part == 2 and 0 <= s - 2:
                    n = s - 2
                    dve.wait_ge(c_scan.sem, c_scan.at(b, n + 1))
                    if n >= 3:
                        dve.wait_ge(c_sum.sem, c_sum.at(b, n - 2))
                    dst = y if n == 0 else prod[:, n % 2, :]
                    for h in range(NH):
                        U["C"].wait_filled(dve, b, f"C{n}_{h}")
                        read("C", dve.tensor_tensor(half(dst, h), bank("C", f"C{n}_{h}"), half(hst[:, n % 2, :], h),
                                                    ALU.mult))

            def ssm_gate(b):
                dve.wait_ge(c_sum.sem, c_sum.at(b, NS - 1))
                U["C"].wait_read(dve, b, f"z{NH - 1}")
                dve.tensor_tensor(w[:], y[:], z[:], ALU.mult).then_inc(c_yz.sem, 1)

            def ssm_out(b):
                for h in range(NH):
                    add_residual("C", b, h)

            def gates(s, b):
                u = NORM_U[s]
                count = [0]

                def step(ins):
                    count[0] += 1
                    ins.then_inc(g_step[s].sem, 1)
                    dve.wait_ge(g_step[s].sem, g_step[s].at(b, count[0]))

                def bc(ap):
                    return ap.unsqueeze(2).broadcast_to([P, TT, E])

                U[u].wait_filled(dve, b, "logits")
                lg = bank(u, "logits")[:, 0:TT * E].rearrange("p (j e) -> p j e", e=E)
                step(dve.tensor_reduce(g_mx[:], lg, AX.X, ALU.max))
                read(u, dve.tensor_tensor(g_lg[:], lg, bc(g_mx[:]), ALU.subtract))
                dve.wait_ge(g_exp[s].sem, g_exp[s].at(b, 1))
                step(dve.tensor_reduce(g_sum[:], g_e[:], AX.X, ALU.add))
                step(dve.reciprocal(g_rs[:], g_sum[:]))
                step(dve.tensor_tensor(g_sc[:], g_e[:], bc(g_rs[:]), ALU.mult))
                pick = g_sc
                if s == "D":
                    pick = g_sel
                    step(dve.tensor_tensor(g_sel[:], g_sc[:], gate_bias[:].unsqueeze(1).broadcast_to([P, TT, E]), ALU.add))
                dve.sem_inc(s_turn_dve, 1)
                for j in range(TT):
                    ins = dve.max(g_top[:, j, :], pick[:, j, :])
                step(ins)
                dve.sem_inc(s_turn_dve, 1)
                for j in range(TT):
                    ins = dve.max_index(g_idx[:, j, :], g_top[:, j, :], pick[:, j, :])
                step(ins)
                step(dve.tensor_copy(g_idf[:], g_idx[:, :, 0:2]))
                step(dve.tensor_tensor(g_m[:], expert_no[:], bc(g_idf[:, :, 0]), ALU.is_equal))
                step(dve.tensor_tensor(g_r1[:], expert_no[:], bc(g_idf[:, :, 1]), ALU.is_equal))
                step(dve.tensor_tensor(g_m[:], g_m[:], g_r1[:], ALU.add))
                step(dve.tensor_tensor(g_ms[:], g_m[:], g_sc[:], ALU.mult))
                if s == "B":
                    step(dve.tensor_reduce(g_den[:], g_ms[:], AX.X, ALU.add))
                    step(dve.tensor_scalar(g_den[:], g_den[:], 1e-20, None, ALU.add))
                    step(dve.reciprocal(g_rd[:], g_den[:]))
                    step(dve.tensor_tensor(g_ms[:], g_ms[:], bc(g_rd[:]), ALU.mult))
                step(dve.tensor_copy(g_parts[:, :, 0, :], g_ms[:]))
                step(dve.tensor_tensor(g_r1[:], g_ms[:], g_parts[:, :, 0, :], ALU.subtract))
                step(dve.tensor_copy(g_parts[:, :, 1, :], g_r1[:]))
                dve.tensor_tensor(g_parts[:, :, 2, :], g_r1[:], g_parts[:, :, 1, :], ALU.subtract).then_inc(g_done[s].sem, 1)
                assert count[0] == GATE_STEPS[s], count

            def tile(s, b, step, done):
                k = step - SECOND_LAG
                if not 0 <= k < NH * NT[s]:
                    return
                _, e, rows, _ = TILES[s][k % NT[s]]
                U[s].wait_filled(dve, b, f"b{k}")
                if e is None:
                    U[s].wait_read(dve, b, f"a{k}")
                else:
                    dve.wait_ge(m_sg[s].sem, m_sg[s].at(b, gated_to(s, k)))
                read(s, dve.scalar_tensor_tensor(out=h_ring[0:rows, k % RH, :], in0=bank(s, f"b{k}", rows),
                                                 scalar=down[W3[s]][0:rows], in1=s_ring[0:rows, k % RS[s], :],
                                                 op0=ALU.mult, op1=ALU.mult))

            def mixture_out(s, b, h, done):
                if s == "D":
                    dve.wait_ge(x_out.sem, x_out.at(b, 0))
                add_residual(s, b, h)

            program(Steps(
                norm=norm, norm_transposed=norm_transposed, attention_start=attention_start,
                attention_step=attention_step, attention_end=attention_end, ssm_in=ssm_in, ssm_rates=nothing,
                ssm_parts=ssm_parts, ssm_step=ssm_step, ssm_gate=ssm_gate, ssm_out=ssm_out, tile=tile,
                mixture_out=mixture_out, logits=nothing, gates=gates), dve)


def kernel(**inputs):
    import numpy as np
    import concourse.bacc as bacc
    from concourse import mybir as mb
    from concourse.bass_utils import run_bass_kernel_spmd

    i = {k: np.asarray(v) for k, v in inputs.items()}
    H, EF = 16, 8
    D = 128

    def column(v):
        return v.reshape(-1, 1)

    def rows(v):
        return v.reshape(-1, v.shape[-1]).T

    bc = np.concatenate([i["L1_attn_Wb"], i["L1_attn_Wc"]], axis=1)
    bbc = np.concatenate([i["L1_attn_bb"], i["L1_attn_bc"]])
    v_t = i["L0_attn_v_w"].T.reshape(D, H, EF)
    o_t = i["L0_attn_o_w"].T.reshape(H, EF, D)
    t = {
        "x": i["L0_attn_x"],
        "Wk": i["L0_attn_k_w"].T, "Wq": i["L0_attn_q_w"].T,
        "Wv": np.repeat(v_t.transpose(0, 2, 1), EF, axis=2).reshape(D, -1),
        "Wo": np.repeat(o_t, EF, axis=0),
        "cs1": i["L0_attn_cs_w1"].T, "cs2": np.repeat(i["L0_attn_cs_w2"].T, EF, axis=1),
        "cs_b1": column(i["L0_attn_cs_b1"]), "cs_b2": column(np.repeat(i["L0_attn_cs_b2"], EF)),
        "decay": column(i["L0_attn_decay_params"]),
        "Wg0": i["L0_ffn_Wg"].T, "W1_0": rows(i["L0_ffn_W1"]), "W3_0": rows(i["L0_ffn_W3"]),
        "W2_0": i["L0_ffn_W2"].transpose(0, 2, 1),
        "Win": i["L1_attn_Win"], "Wz": i["L1_attn_Wg"], "Wdt": i["L1_attn_Wdt"], "Wout": i["L1_attn_Wout"],
        "Wbc": np.concatenate([bc, bc, bc], axis=1), "bbc": column(np.concatenate([bbc, bbc, bbc])),
        "b_in": column(i["L1_attn_b_in"]), "bg": column(i["L1_attn_bg"]), "bout": column(i["L1_attn_bout"]),
        "convb": column(i["L1_attn_convb"]), "bdt": column(i["L1_attn_bdt"]),
        "convw": i["L1_attn_convw"], "A": i["L1_attn_A"],
        "Wg1": i["L1_ffn_gate_w"].T, "gate_bias": np.repeat(i["L1_ffn_gate_bias"].reshape(1, -1), D, axis=0),
        "W1_1": np.concatenate([rows(i["L1_ffn_w1"]), i["L1_ffn_sw1"].T], axis=1),
        "W3_1": np.concatenate([rows(i["L1_ffn_w3"]), i["L1_ffn_sw3"].T], axis=1),
        "W2_1": np.concatenate([i["L1_ffn_w2"].transpose(0, 2, 1), i["L1_ffn_sw2"].T.reshape(2, D, D)], axis=0),
    }
    nc = bacc.Bacc("TRN2", target_bir_lowering=False, num_devices=1)
    arrays, handles = {}, {}
    for name, a in t.items():
        a = np.ascontiguousarray(a)
        arrays[f"in_{name}"] = a
        handles[name] = nc.dram_tensor(f"in_{name}", a.shape, mb.dt.from_np(a.dtype), kind="ExternalInput").ap()
    out = nc.dram_tensor("out_0", i["L0_attn_x"].shape, mb.dt.float32, kind="ExternalOutput").ap()
    build(nc, handles, out)
    r = run_bass_kernel_spmd(nc, [arrays], core_ids=[0])
    return r.results[0]["out_0"]
```

```python
from contextlib import ExitStack

import concourse.bass as bass
from concourse import mybir

F32 = mybir.dt.float32
BF16 = mybir.dt.bfloat16
F16 = mybir.dt.float16
U32 = mybir.dt.uint32
ALU = mybir.AluOpType
ACT = mybir.ActivationFunctionType
AX = mybir.AxisListType

P = 128
EPS = 1e-5
FIRST = 16
LAM_MAX = 0.9995


class Signal:

    def __init__(self, sem, per_batch, first=0):
        self.sem = sem
        self.per_batch = per_batch
        self.first = first

    def at(self, batch, n):
        return batch * self.per_batch + (n + self.first)


class BankUses:

    def __init__(self, uses, filled, read):
        self.uses = uses
        self.place = {u[0]: i for i, u in enumerate(uses)}
        assert len(self.place) == len(uses)
        self.filled = Signal(filled, len(uses))
        self.read = {r: Signal(s, sum(u[2] == r for u in uses), first=FIRST) for r, s in read.items()}

    def bank(self, name):
        return self.uses[self.place[name]][1]

    def wait_filled(self, eng, b, name):
        eng.wait_ge(self.filled.sem, self.filled.at(b, self.place[name] + 1))

    def wait_bank_free(self, eng, b, name):
        i = self.place[name]
        before = [u[0] for u in self.uses[:i] if u[1] == self.uses[i][1]]
        if before:
            self.wait_read(eng, b, before[-1])

    def wait_read(self, eng, b, name):
        i = self.place[name]
        reader = self.uses[i][2]
        n = sum(u[2] == reader for u in self.uses[:i + 1])
        eng.wait_ge(self.read[reader].sem, self.read[reader].at(b, n))

    def wait_read_before(self, eng, b, name):
        i = self.place[name]
        reader = self.uses[i][2]
        n = -sum(u[2] == reader for u in self.uses[i + 1:])
        assert n + FIRST > 0
        eng.wait_ge(self.read[reader].sem, self.read[reader].at(b, n))

    def wait_last_read(self, eng, b, bank):
        self.wait_read_before(eng, b, [u[0] for u in self.uses if u[1] == bank][-1])

    def wait_all_read(self, eng, b):
        for s in self.read.values():
            eng.wait_ge(s.sem, s.at(b, 0))


class Steps:

    def __init__(self, start, weights_peak, weights_scale, weights_split, loaded, stats, norm, norm_transposed, attention_start, attention_step, attention_end, ssm_in, ssm_rates,
                 ssm_parts, ssm_softplus, ssm_step, ssm_gate, ssm_out, tile, mixture_out, logits, gates):
        self.start, self.weights_peak, self.weights_scale = start, weights_peak, weights_scale
        self.weights_split, self.loaded = weights_split, loaded
        self.stats, self.norm, self.norm_transposed, self.logits, self.gates = stats, norm, norm_transposed, logits, gates
        self.attention_start, self.attention_step = attention_start, attention_step
        self.attention_end = attention_end
        self.ssm_in, self.ssm_rates, self.ssm_parts = ssm_in, ssm_rates, ssm_parts
        self.ssm_softplus, self.ssm_step, self.ssm_gate, self.ssm_out = ssm_softplus, ssm_step, ssm_gate, ssm_out
        self.tile, self.mixture_out = tile, mixture_out


def mlp_tiles(experts, rows, shared):
    tiles = []
    for e in range(experts):
        for r in range(0, rows, P):
            tiles.append((len(tiles), e, min(P, rows - r), e * rows + r))
    for s in range(shared):
        tiles.append((len(tiles), None, P, experts * rows + s * P))
    return tiles


def steady(pairs, tiles):
    first, last, steps = pairs
    n = last - first
    return {first + i: range(steps * i // n, steps * (i + 1) // n) for i in range(n) if first + i < tiles}


def build(nc, t, out):
    B, T, D = t["x"].shape
    TT = T // P
    HW = 512
    NH = T // HW
    TH = HW // P
    E = t["Wg0"].shape[1]
    HEADS = 16
    EF = D // HEADS
    DH = t["cs1"].shape[1]
    NS = t["A"].shape[1]
    BC = 3 * 2 * NS
    R0 = t["W2_0"].shape[1]
    R1 = t["W2_1"].shape[1]
    SH = t["W1_1"].shape[1] // R1 - E
    TILES = {"B": mlp_tiles(E, R0, 0), "D": mlp_tiles(E, R1, SH)}
    NT = {s: len(TILES[s]) for s in "BD"}
    VK = NH * EF
    LAG = 2
    GATE_LAG, SECOND_LAG, DOWN_LAG = 2, 3, 5
    A_FIRST, A_TAIL = 5, 8
    OUT_LAG = 2
    RATES_LEAD, PARTS_LEAD, SOFTPLUS_LEAD = 4, 3, 1
    NORM_AHEAD = 4
    C_FIRST, C_TAIL = 10, {"B": 9, "D": 8}

    ctx = ExitStack()
    with ctx:
        def sb(name, shape, dt=F32):
            return ctx.enter_context(nc.sbuf_tensor(name, shape, dt))

        def sem(name):
            return ctx.enter_context(nc.semaphore(name))

        def signal(name, per_batch):
            return Signal(sem(name), per_batch)

        banks = [ctx.enter_context(nc.psum_tensor(f"bank{i}", [P, HW], F32)) for i in range(8)]

        Wk, Wq = sb("Wk", [P, D]), sb("Wq", [P, D])
        Wo = sb("Wo", [P, EF, D])
        cs1 = sb("cs1_w", [P, DH])
        cs2 = sb("cs2_w", [DH, P])
        Win, Wz, Wdt, Wout = (sb(n, [P, D]) for n in ("Win_w", "Wz_w", "Wdt_w", "Wout_w"))
        Wbc = sb("Wbc_w", [P, BC])
        SPLIT = {n: t[n].shape[1] for n in ("Wv", "W1_0", "W3_0", "W1_1", "W3_1")}
        Whi = {n: sb(f"{n}_hi", [P, m], F16) for n, m in SPLIT.items()}
        Wlo = {n: sb(f"{n}_lo", [P, m], F16) for n, m in SPLIT.items()}
        W1 = {"B": "W1_0", "D": "W1_1"}
        W3 = {"B": "W3_0", "D": "W3_1"}
        W2 = {s: sb(f"W2_{s}w", [P, NT[s], D]) for s in "BD"}
        Wgate = {"B": sb("Wg_0w", [P, E]), "D": sb("Wg_1w", [P, E])}
        gate_bias = sb("gate_bias", [P, E])
        cols = sb("cols", [P, 10])
        COL = {n: i for i, n in enumerate(("decay", "cs_b2", "cs_b1", "b_in", "bg", "bout", "convb", "bdt", "bbc"))}
        col = {n: cols[:, i:i + 1] for n, i in COL.items()}
        convw = sb("convw_w", [P, 3])
        A_sb = sb("A_w", [P, NS])
        wpeak, wfloor, wtop = (sb(n, [P, len(SPLIT)]) for n in ("wpeak", "wfloor", "wtop"))
        wexp, wscale, winv = (sb(n, [P, len(SPLIT)], U32) for n in ("wexp", "wscale", "winv"))
        place = {n: i for i, n in enumerate(SPLIT)}
        GROUPS = (slice(0, 1), slice(1, len(SPLIT)))
        up = {n: wscale[:, i:i + 1].bitcast(F32) for n, i in place.items()}
        down = {n: winv[:, i:i + 1].bitcast(F32) for n, i in place.items()}

        ident = sb("ident", [P, P])
        ident16 = sb("ident16", [P, P], BF16)
        sel_bc = sb("sel_bc", [BC, 2 * NS, P], BF16)
        sel_gate = sb("sel_gate", [3 * E, E, P], BF16)
        expert_no = sb("expert_no", [P, TT, E])
        expert_i = sb("expert_i", [P, TT * E], U32)
        neg_half = sb("neg_half", [P, TT])
        eps_t = sb("eps_t", [P, TT])
        tb = sb("tanh_base", [P, 1])
        lam_mul, lam_add = sb("lam_mul", [P, 1]), sb("lam_add", [P, 1])
        half_b2 = sb("half_b2", [P, 1])

        x0, x3, x4 = (sb(f"x{i}", [P, TT, D]) for i in (0, 3, 4))
        x12 = sb("x12", [P, 2 * TT, D])
        x1, x2 = x12[:, 0:TT, :], x12[:, TT:2 * TT, :]
        XIN = {"A": x0, "B": x1, "C": x2, "D": x3}
        XOUT = {"A": x1, "B": x2, "C": x3, "D": x4}
        ENDS = {("out", "A", 0): x3, ("in", "B", 0): x3,
                ("out", "C", B - 1): x1, ("in", "D", B - 1): x1, ("norm", "D", B - 1): x0}

        stats_b = sb("stats_b", [P, TT, 6])
        mv_b, ve_b, rstd_b = sb("mv_b", [P, TT, 2]), sb("ve_b", [P, TT]), sb("rstd_b", [P, TT])

        upad = sb("upad", [P, T + 2])
        xs = sb("xs", [P, T])
        dt = sb("dt", [P, T])
        w = sb("w", [P, T])
        z = sb("z", [P, T])
        y = sb("y", [P, T])
        arena = sb("arena", [P, 10 * T])
        dA = arena[:, 0:4 * T].rearrange("p (r n) -> p r n", n=T)
        dBx = arena[:, 4 * T:6 * T].rearrange("p (r n) -> p r n", n=T)
        hst = arena[:, 6 * T:8 * T].rearrange("p (r n) -> p r n", n=T)
        prod = arena[:, 8 * T:10 * T].rearrange("p (r n) -> p r n", n=T)
        bc_parts = sb("bc_parts", [BC, T], BF16)
        bc_mid = sb("bc_mid", [BC, T], BF16)
        RS = {"B": 6, "D": 5}
        RG, RH = 3, 4
        slots = max(RS.values())
        mix_arena = sb("mix_arena", [P, slots + RH + RG + NH, HW])
        s_ring = mix_arena[:, 0:slots, :]
        h_ring = mix_arena[:, slots:slots + RH, :]
        g_ring = mix_arena[:, slots + RH:slots + RH + RG, :]
        oT_mix = mix_arena[:, slots + RH + RG:, :]
        oT = {"A": arena[:, 6 * T:7 * T].rearrange("p (r n) -> p r n", n=HW)}
        oT.update({"C": oT["A"], "B": oT_mix, "D": oT_mix})
        conv = y
        sp_abs, sp_log = prod[:, 0, :], prod[:, 1, :]
        bc_f, bc_r = arena[0:BC, 4 * T:5 * T], arena[0:BC, 5 * T:6 * T]
        hid, lam_th, lam, kT, qT = xs[0:DH, :], dt, w, z, y
        kv = arena[:, 4 * T:5 * T].rearrange("p (r n) -> p r n", n=HW)
        xA = arena[:, 5 * T:6 * T].bitcast(F16)
        qs = arena[:, 8 * T:10 * T].rearrange("p (r n) -> p r n", n=HW)
        S = arena[:, 0:EF * HW].rearrange("p (r n) -> p r n", n=HW)
        x_parts = {s: sb(f"x_parts{s}", [P, 2 * T], F16) for s in "BD"}
        x_parts["A"] = xA

        def parts_of(s, b):
            buf = x_parts[{("B", 0): "D", ("D", B - 1): "B"}.get((s, b), s) if isinstance(b, int) else s]
            return buf[:, 0:T], buf[:, T:2 * T]

        def x_hi(s, b):
            return parts_of(s, b)[0]

        def x_lo(s, b):
            return parts_of(s, b)[1]

        XN = {"A": upad[:, 1:T + 1].rearrange("p (j d) -> p j d", d=D), "B": x0,
              "C": xs[:].rearrange("p (j d) -> p j d", d=D), "D": x4}

        def stream(role, s, b):
            usual = {"in": XIN, "out": XOUT, "norm": XN}[role][s]
            return ENDS.get((role, s, b), usual) if isinstance(b, int) else usual

        def normT(s, b):
            return stream("norm", s, b)[:, :, :].rearrange("p j d -> p (j d)")

        flat = mix_arena[:, :, :].rearrange("p r n -> p (r n)")
        stage = {"Wv": x4[:, :, :].rearrange("p j d -> p (j d)"),
                 "W3_1": x12[:, :, :].rearrange("p j d -> p (j d)")[:, 0:SPLIT["W3_1"]]}
        at = 0
        for n in ("W1_0", "W3_0", "W1_1"):
            stage[n] = flat[:, at:at + SPLIT[n]]
            at += SPLIT[n]

        g_lg, g_e, g_sc, g_sel, g_m, g_ms, g_r1 = (sb(f"g_{n}", [P, TT, E]) for n in
                                                   ("lg", "e", "sc", "sel", "m", "ms", "r1"))
        g_top = sb("g_top", [P, TT, 8])
        g_idx = sb("g_idx", [P, TT, 8], U32)
        g_idf = sb("g_idf", [P, TT, 2])
        g_mx, g_sum, g_rs, g_den, g_rd = (sb(f"g_{n}", [P, TT]) for n in ("mx", "sum", "rs", "den", "rd"))
        g_parts = sb("g_parts", [P, TT, 3, E], BF16)
        gT = {s: sb(f"gT{s}", [3 * E, T], BF16) for s in "BD"}

        norm_uses = [("lnT0", 5, "act"), ("lnT1", 6, "act")]
        usesA = list(norm_uses)
        for name in ("cs", "k", "q", "lam"):
            usesA += [(f"{name}{h}", 5 + h, "act") for h in range(NH)]
        usesA += [(f"v{k}", 5 + k % 2, "dve") for k in range(LAG)]
        for k in range(VK + LAG):
            if k >= LAG and (k - LAG) % EF == EF - 1:
                usesA.append((f"o{(k - LAG) // EF}", 7, "act"))
            if k + LAG < VK:
                usesA.append((f"v{k + LAG}", 5 + k % 2, "dve"))
        usesA += [(f"outT{h}", 5 + h, "dve") for h in range(NH)]
        usesC = list(norm_uses)
        for name, reader in (("u", "act"), ("z", "act"), ("dt", "dve"), ("bc", "act")):
            usesC += [(f"{name}{h}", 5 + h, reader) for h in range(NH)]
        ring = 0
        for s in range(NS + 2):
            for kind, n in (("B", s), ("C", s - 2)):
                if 0 <= n < NS:
                    for h in range(NH):
                        usesC.append((f"{kind}{n}_{h}", 5 + ring % 3, "dve"))
                        ring += 1
        usesC += [(f"o{h}", 5 + h, "act") for h in range(NH)] + [(f"outT{h}", 5 + h, "dve") for h in range(NH)]
        usesP = norm_uses + [("logits", 7, "dve")]

        def gate_first(s, k):
            if not 0 <= k < NH * NT[s]:
                return None
            h, i = divmod(k, NT[s])
            e = TILES[s][i][1]
            if e is None or (i and TILES[s][i - 1][1] == e):
                return None
            return h * E + e

        def mixture_uses(s):
            n, uses, ra, rb = NH * NT[s], [], 0, 0
            for k in range(n + DOWN_LAG):
                rows = [f"g{q}"] if (q := gate_first(s, k - GATE_LAG)) is not None else []
                for name in (["gT"] if k == GATE_LAG else []) + rows + ([f"a{k}"] if k < n else []):
                    uses.append((name, ra % 2, "act"))
                    ra += 1
                if 0 <= k - SECOND_LAG < n:
                    uses.append((f"b{k - SECOND_LAG}", 2 + rb % 2, "dve"))
                    rb += 1
                if k >= DOWN_LAG and (k - DOWN_LAG) % NT[s] == NT[s] - 1:
                    uses.append((f"y{(k - DOWN_LAG) // NT[s]}", 4, "act"))
            return uses + [(f"outT{h}", 7, "dve") for h in range(NH)]

        U = {}
        for s, uses in (("A", usesA), ("B", mixture_uses("B")), ("C", usesC), ("D", mixture_uses("D")),
                        ("PB", usesP), ("PD", usesP)):
            U[s] = BankUses(uses, sem(f"{s}_bank_filled"),
                            {"act": sem(f"{s}_bank_read_act"), "dve": sem(f"{s}_bank_read_dve")})
        NORM_U = {"A": "A", "B": "PB", "C": "C", "D": "PD"}

        s_w = {n: sem(f"loaded_weights_{n}") for n in "ABCD"}
        s_st = {n: sem(f"staged_{n}") for n in SPLIT}
        s_cons, s_cons0, s_ident = sem("constants_ready"), sem("zeros_ready"), sem("ident_ready")
        s_turn_dve = sem("dve_wait_passed")
        s_base, s_lamc = sem("tanh_decay_ready"), sem("decay_scalars_ready")
        s_wm, s_wf, s_wt, s_ws, s_hi, s_lo = (sem(n) for n in (
            "weight_maxima", "weight_floors", "weight_max_of_all", "weight_scales", "weight_hi_parts",
            "weight_lo_parts"))
        x_in, x_out = signal("x_loaded", 16), Signal(sem("x_stored"), 16, first=16)
        stats = {s: signal(f"{s}_stats_done", TT) for s in "ABCD"}
        mv = {s: signal(f"{s}_mean_var_done", TT) for s in "ABCD"}
        veps = {s: signal(f"{s}_var_eps_done", 1) for s in "ABCD"}
        rstd = {s: signal(f"{s}_rstd_done", 1) for s in "ABCD"}
        xn = {s: signal(f"{s}_normalised", TT) for s in "ABCD"}
        xT = {s: signal(f"{s}_norm_f32_moved", NH) for s in "ABD"}
        xl = {s: signal(f"{s}_x_lo_parts", 1) for s in "ABD"}
        a_lin, a_lam = signal("A_lam_scaled", NH), signal("A_lam_clipped", NH)
        a_scan, a_qs = signal("A_scan", VK), signal("A_qs", VK)
        c_conv = signal("C_conv_steps", 3)
        c_xs = signal("C_xs", 1)
        c_sp = signal("C_softplus_parts", NH + 2)
        c_dt, c_w = signal("C_dt", 1), signal("C_w", 1)
        c_hi, c_r, c_mid = signal("C_bc_hi", 1), signal("C_bc_rest", 1), signal("C_bc_mid", 1)
        c_lo, c_midc = signal("C_bc_lo", 1), signal("C_bc_mid_placed", 1)
        c_dA, c_scan = signal("C_dA", NS), signal("C_scan", NS)
        c_sum, c_yz = signal("C_sum", NS - 1), signal("C_y_gated", 1)
        GATE_STEPS = {"B": 18, "D": 15}
        g_step = {s: signal(f"{s}_gate_steps", GATE_STEPS[s]) for s in "BD"}
        g_exp, g_done = ({s: signal(f"{s}_gate_{n}", 1) for s in "BD"} for n in ("exp", "parts"))
        GATED = {s: NH * sum(e is not None for _, e, _, _ in TILES[s]) for s in "BD"}
        m_sg = {s: Signal(sem(f"{s}_silu_gated"), GATED[s], first=1) for s in "BD"}

        OTHER = {"B": "D", "D": "B"}

        def wait_silu_slot(eng, s, b, k, done):
            if k >= RS[s]:
                U[s].wait_read(eng, b, f"b{k - RS[s]}")
                return
            o = OTHER[s]
            last = [j for j in range(NH * NT[o] - RS[o], NH * NT[o]) if j % RS[o] == k % RS[s]]
            if last:
                U[o].wait_read_before(eng, done[o], f"b{last[0]}")

        def gated_to(s, k):
            return sum(TILES[s][i % NT[s]][1] is not None for i in range(k + 1))

        N_W = {"A": 8, "B": 4, "C": 13, "D": 3}
        LAST_OUT = f"outT{NH - 1}"

        def wait_weights(eng, s):
            eng.wait_ge(s_w[s], 16 * N_W[s])

        def half(ap, h):
            return ap[:, h * HW:(h + 1) * HW]

        def wait_banks(eng, stages, done):
            for s in stages:
                U[s].wait_all_read(eng, done[s])

        def mixture_step(e, s, b, k, done, before):
            e.tile(s, b, k, done)
            if before:
                o, ob = before
                if k < DOWN_LAG:
                    e.tile(o, ob, NH * NT[o] + k, done)
                for h in range(NH):
                    if k == DOWN_LAG + h:
                        e.mixture_out(o, ob, h, done)

        def mixture_rest(e, s, b, done):
            n = NH * NT[s]
            for k in range(n, n + DOWN_LAG):
                e.tile(s, b, k, done)
            for h in range(NH):
                e.mixture_out(s, b, h, done)

        def norm_now(e, s, b):
            e.stats(s, b)
            e.norm(s, b)

        def attention_alone(e, a, done):
            e.start()
            e.weights_peak("Wv")
            e.stats("A", a)
            e.weights_scale(0)
            e.norm("A", a)
            e.weights_split("Wv")
            e.loaded("A")
            e.norm_transposed("A", a, done)
            e.attention_start(a)
            mixtures = list(SPLIT)[1:]
            for u in range(VK + LAG):
                e.attention_step(a, u, done)
                if u < len(mixtures):
                    e.weights_peak(mixtures[u])
                if u == len(mixtures) + 1:
                    e.weights_scale(1)
                i, odd = divmod(u - len(mixtures) - 3, 2)
                if not odd and 0 <= i < len(mixtures):
                    e.weights_split(mixtures[i])
            for h in range(NH):
                e.attention_end(a, h)

        def attention_beside(e, a, s, b, done, prep, before, ahead):
            n = NH * NT[s]
            first, last = A_FIRST, n - A_TAIL
            units = steady((first, last, VK + LAG), n)
            for k in range(n):
                mixture_step(e, s, b, k, done, before)
                if k == 0:
                    e.norm_transposed("A", a, done)
                if k == 1:
                    e.attention_start(a)
                for u in units.get(k, ()):
                    e.attention_step(a, u, done)
                if ahead and k == DOWN_LAG + NORM_AHEAD:
                    e.stats(*ahead)
                if ahead and k == DOWN_LAG + NORM_AHEAD + 2:
                    e.norm(*ahead)
                if k == last:
                    for h in range(NH):
                        e.attention_end(a, h)
                if k == last + 1:
                    e.stats(*prep)
                if k == last + 3:
                    e.norm(*prep)
                if k == last + 4:
                    e.norm_transposed(*prep, done)
                if k == last + 5:
                    e.logits(*prep)
            e.gates(*prep)

        def ssm_beside(e, c, s, b, done, prep, before, ahead):
            n = NH * NT[s]
            first, last = C_FIRST, n - C_TAIL[s]
            units = steady((first, last, 3 * (NS + 2)), n)
            for k in range(n):
                mixture_step(e, s, b, k, done, before)
                if k == 0:
                    e.norm_transposed("C", c, done)
                if k == 1:
                    e.ssm_in(c)
                if k == first - RATES_LEAD:
                    e.ssm_rates(c)
                if k == first - PARTS_LEAD:
                    e.ssm_parts(c)
                if k == first - SOFTPLUS_LEAD:
                    e.ssm_softplus(c)
                for u in units.get(k, ()):
                    e.ssm_step(c, u, done)
                if k == last:
                    e.ssm_gate(c)
                if k == last + OUT_LAG:
                    e.ssm_out(c)
                if k == last + 3:
                    e.stats(*prep)
                if k == last + 5:
                    e.norm(*prep)
                if k == last + 6:
                    e.norm_transposed(*prep, done)
                if k == last + 7:
                    e.logits(*prep)
                if ahead and k == last - 4:
                    e.stats(*ahead)
                if ahead and k == last - 2:
                    e.norm(*ahead)
            e.gates(*prep)

        def prepare(e, s, b, done):
            norm_now(e, s, b)
            e.norm_transposed(s, b, done)
            e.logits(s, b)
            e.gates(s, b)

        def counts(**n):
            return n

        def program(e, eng):
            attention_alone(e, 0, counts(A=0, C=0, PB=0, PD=0, B=0, D=0))
            e.loaded("B")
            prepare(e, "B", 0, counts(A=1, C=0, PB=0, PD=0))
            norm_now(e, "A", 1)
            attention_beside(e, 1, "B", 0, counts(A=1, B=0, C=0, D=0, PB=1, PD=0), ("B", 1), None, None)
            mixture_rest(e, "B", 0, counts(A=2, B=0, C=0, D=0, PB=2, PD=0))
            e.loaded("C")
            norm_now(e, "C", 0)
            e.loaded("D")
            ssm_beside(e, 0, "B", 1, counts(A=2, B=1, C=0, D=0, PB=2, PD=0), ("D", 0), None, ("A", 2))
            attention_beside(e, 2, "D", 0, counts(A=2, B=2, C=1, D=0, PB=2, PD=1), ("B", 2), ("B", 1), ("C", 1))
            with eng.Fori(1, B - 2) as i:
                ssm_beside(e, i, "B", i + 1, counts(A=i + 2, B=i + 1, C=i, D=i, PB=i + 2, PD=i), ("D", i),
                           ("D", i - 1), ("A", i + 2))
                attention_beside(e, i + 2, "D", i, counts(A=i + 2, B=i + 2, C=i + 1, D=i, PB=i + 2, PD=i + 1),
                                 ("B", i + 2), ("B", i + 1), ("C", i + 1))
            i = B - 2
            ssm_beside(e, i, "B", i + 1, counts(A=B, B=i + 1, C=i, D=i, PB=B, PD=i), ("D", i), ("D", i - 1), None)
            mixture_rest(e, "B", i + 1, counts(A=B, B=i + 1, C=i + 1, D=i, PB=B, PD=i + 1))
            norm_now(e, "C", i + 1)
            ssm_beside(e, i + 1, "D", i, counts(A=B, B=B, C=i + 1, D=i, PB=B, PD=i + 1), ("D", i + 1), None, None)
            mixture_rest(e, "D", i, counts(A=B, B=B, C=B, D=i, PB=B, PD=B))
            for k in range(NH * NT["D"]):
                mixture_step(e, "D", i + 1, k, counts(A=B, B=B, C=B, D=i + 1, PB=B, PD=B), None)
            mixture_rest(e, "D", i + 1, counts(A=B, B=B, C=B, D=i + 1, PB=B, PD=B))

        def nothing(*_):
            pass

        block = ctx.enter_context(nc.Block())

        @block.sync
        def _(sp):
            xv = t["x"].rearrange("b (j p) d -> b p j d", p=P)
            ov = out.rearrange("b (j p) d -> b p j d", p=P)

            def load_x(b):
                sp.dma_start(x0[:, :, :], xv[b]).then_inc(x_in.sem, 16)

            sp.sem_inc(x_out.sem, x_out.first)
            load_x(0)

            def load_stage(*names):
                for n in names:
                    sp.dma_start(stage[n], t[n]).then_inc(s_st[n], 16)

            load_stage("Wv")
            for dst, n in ((cs1, "cs1"), (Wk, "Wk"), (Wq, "Wq"), (cs2, "cs2")):
                sp.dma_start(dst[:], t[n]).then_inc(s_w["A"], 16)
            for n in ("decay", "cs_b2"):
                sp.dma_start(col[n], t[n]).then_inc(s_w["A"], 16)
            sp.dma_start(col["cs_b1"][0:DH], t["cs_b1"]).then_inc(s_w["A"], 16)
            sp.dma_start(Wo[:], t["Wo"]).then_inc(s_w["A"], 16)
            load_stage("W1_0", "W3_0", "W1_1", "W3_1")
            sp.dma_start(Wgate["B"][:], t["Wg0"]).then_inc(s_w["B"], 16)
            per = -(-R0 // P)
            w2v = W2["B"][:, :, :].rearrange("p (e j) d -> p e j d", j=per)
            for j in range(per):
                rows = min(P, R0 - j * P)
                sp.dma_start(w2v[0:rows, :, j, :],
                             t["W2_0"][:, j * P:j * P + rows, :].rearrange("e r d -> r e d")).then_inc(s_w["B"], 16)
            for dst, n in ((Win, "Win"), (Wz, "Wz"), (Wdt, "Wdt"), (Wout, "Wout"), (Wbc, "Wbc"), (convw, "convw"), (A_sb, "A")):
                sp.dma_start(dst[:], t[n]).then_inc(s_w["C"], 16)
            for n in ("b_in", "bg", "bout", "convb", "bdt"):
                sp.dma_start(col[n], t[n]).then_inc(s_w["C"], 16)
            sp.dma_start(col["bbc"][0:BC], t["bbc"]).then_inc(s_w["C"], 16)
            sp.dma_start(Wgate["D"][:], t["Wg1"]).then_inc(s_w["D"], 16)
            sp.dma_start(gate_bias[:], t["gate_bias"]).then_inc(s_w["D"], 16)
            sp.dma_start(W2["D"][:], t["W2_1"].rearrange("e r d -> r e d")).then_inc(s_w["D"], 16)

            def next_x(b):
                sp.wait_ge(xl["B"].sem, xl["B"].at(b, 1))
                U["PB"].wait_filled(sp, b, "logits")
                load_x(b + 1)

            def store_x(b):
                U["D"].wait_read(sp, b, LAST_OUT)
                sp.dma_start(ov[b], x4[:, :, :]).then_inc(x_out.sem, 16)

            next_x(0)
            next_x(1)
            with sp.Fori(0, B - 3) as b:
                store_x(b)
                next_x(b + 2)
            for b in range(B - 3, B):
                store_x(b)
            sp.wait_ge(x_out.sem, x_out.at(B, 0))

        @block.gpsimd
        def _(pool):
            for s in "BD":
                pool.sem_inc(m_sg[s].sem, 1)
            pool.memset(ident[:], 0.0).then_inc(s_cons0, 1)
            pool.memset(neg_half[:], -0.5).then_inc(s_cons0, 1)
            pool.memset(eps_t[:], EPS).then_inc(s_cons0, 1)
            pool.wait_ge(s_cons0, 3)
            pool.affine_select(out=ident[:], in_=ident[:], compare_op=ALU.not_equal, fill=1.0, base=0,
                               pattern=[[-1, P]], channel_multiplier=1).then_inc(s_ident, 1)

            def loaded(s):
                if s != "A":
                    return
                zeroed = (ident16, sel_bc, sel_gate)
                for m in zeroed:
                    pool.memset(m[:], 0.0).then_inc(s_cons0, 1)
                pool.memset(upad[:, 0:1], 0.0)
                pool.memset(upad[:, T + 1:T + 2], 0.0)
                pool.iota(expert_i[:], pattern=[[0, TT], [1, E]], base=0, channel_multiplier=0).then_inc(s_cons0, 1)
                pool.wait_ge(s_cons0, 3 + len(zeroed) + 1)
                pool.tensor_copy(expert_no[:, :, :].rearrange("p a b -> p (a b)"), expert_i[:]).then_inc(s_cons, 1)
                pool.affine_select(out=ident16[:], in_=ident16[:], compare_op=ALU.not_equal, fill=1.0, base=0,
                                   pattern=[[-1, P]], channel_multiplier=1).then_inc(s_cons, 1)
                done = 0
                for m, rows in ((sel_bc, 2 * NS), (sel_gate, E)):
                    for part in range(3):
                        pool.affine_select(out=m[:], in_=m[:], compare_op=ALU.not_equal, fill=1.0, base=-part * rows,
                                           pattern=[[-1, rows], [0, P]], channel_multiplier=1).then_inc(s_cons, 1)
                        done += 1
                        pool.wait_ge(s_cons, 2 + done)

            def weights_scale(g):
                pool.wait_ge(s_wf, g + 1)
                pool.partition_all_reduce(wtop[:, GROUPS[g]], wfloor[:, GROUPS[g]], P,
                                          bass.bass_isa.ReduceOp.max).then_inc(s_wt, 1)

            def inverse_deviation(s, b):
                pool.wait_ge(mv[s].sem, mv[s].at(b, TT))
                pool.tensor_tensor(ve_b[:], mv_b[:, :, 1], eps_t[:], ALU.add).then_inc(veps[s].sem, 1)
                pool.wait_ge(veps[s].sem, veps[s].at(b, 1))
                pool.tensor_tensor(rstd_b[:], ve_b[:], neg_half[:], ALU.pow).then_inc(rstd[s].sem, 1)

            def attention_step(b, u, done):
                k = u - 1
                if not 0 <= k < VK:
                    return
                if k == 0:
                    U["A"].wait_read(pool, b, f"q{NH - 1}")
                pool.wait_ge(a_scan.sem, a_scan.at(b, k + 1))
                pool.tensor_tensor(qs[:, k % 4, :], half(qT, k // EF), S[:, k % EF, :], ALU.mult).then_inc(a_qs.sem, 1)

            def ssm_gate(b):
                add_state(b, NS - 1)

            def add_state(b, n):
                U["C"].wait_read(pool, b, f"C{n}_{NH - 1}")
                if n > 1:
                    pool.wait_ge(c_sum.sem, c_sum.at(b, n - 1))
                pool.tensor_tensor(y[:], y[:], prod[:, n % 2, :], ALU.add).then_inc(c_sum.sem, 1)

            def ssm_step(b, u, done):
                s, part = divmod(u, 3)
                if part == 0 and 1 <= s - 3:
                    add_state(b, s - 3)

            def tile(s, b, step, done):
                k = step - GATE_LAG
                if not 0 <= k < NH * NT[s]:
                    return
                _, e, rows, _ = TILES[s][k % NT[s]]
                if e is None:
                    return
                q = k // NT[s] * E + e
                U[s].wait_read(pool, b, f"g{q}")
                U[s].wait_read(pool, b, f"a{k}")
                slot = s_ring[0:rows, k % RS[s], :]
                pool.tensor_tensor(slot, slot, g_ring[0:rows, q % RG, :], ALU.mult).then_inc(m_sg[s].sem, 1)

            program(Steps(
                start=nothing, weights_peak=nothing, weights_scale=weights_scale, weights_split=nothing, loaded=loaded,
                stats=inverse_deviation, norm=nothing, norm_transposed=nothing, attention_start=nothing, attention_step=attention_step,
                attention_end=nothing, ssm_in=nothing, ssm_rates=nothing, ssm_parts=nothing, ssm_softplus=nothing, ssm_step=ssm_step,
                ssm_gate=ssm_gate, ssm_out=nothing, tile=tile, mixture_out=nothing, logits=nothing, gates=nothing), pool)

        @block.tensor
        def _(pe):
            def loaded(s):
                wait_weights(pe, s)
                if s == "A":
                    pe.wait_ge(s_ident, 1)
                if s == "B":
                    pe.wait_ge(s_cons, 8)
                parts = {"A": "Wv", "B": "W3_0", "D": "W3_1"}
                if s in parts:
                    pe.wait_ge(s_lo, place[parts[s]] + 1)

            def fill(s, b, name, cols=HW, rows=P):
                U[s].wait_bank_free(pe, b, name)
                return banks[U[s].bank(name)][0:rows, 0:cols]

            def filled(s, ins):
                ins.then_inc(U[s].filled.sem, 1)

            def product(bank, weight, c0, c1, s, b, h):
                hi, lo = Whi[weight][:, c0:c1], Wlo[weight][:, c0:c1]
                xh, xlow = half(x_hi(s, b), h), half(x_lo(s, b), h)
                pe.matmul(bank, hi, xh, start=True, stop=False)
                pe.matmul(bank, hi, xlow, start=False, stop=False)
                return pe.matmul(bank, lo, xh, start=False, stop=True)

            def norm_transposed(s, b, done):
                u = NORM_U[s]
                wait_banks(pe, ("A", "C", "PB", "PD"), done_now(s, b, done))
                for h in range(NH):
                    bank = fill(u, b, f"lnT{h}")
                    for j in range(TH):
                        pe.wait_ge(xn[s].sem, xn[s].at(b, h * TH + j + 1))
                        last = pe.transpose(bank[:, j * P:(j + 1) * P], stream("norm", s, b)[:, h * TH + j, :], ident[:])
                    filled(u, last)

            def done_now(s, b, done):
                now = dict(done)
                if s == "B":
                    now["A"] = b + 1
                if s == "D":
                    now["C"] = b + 1
                return now

            def transpose_out(s, b, h, acc):
                U[s].wait_read(pe, b, f"{acc}{h}")
                bank = fill(s, b, f"outT{h}")
                for j in range(TH):
                    last = pe.transpose(bank[:, j * P:(j + 1) * P], oT[s][:, h, j * P:(j + 1) * P], ident[:])
                filled(s, last)

            def wait_mixtures_out(done):
                for s in "BD":
                    pe.wait_ge(U[s].read["dve"].sem, U[s].read["dve"].at(done[s], 0))

            def value(b, k):
                f = k % EF
                filled("A", product(fill("A", b, f"v{k}"), "Wv", f * P, (f + 1) * P, "A", b, k // EF))

            def attention_start(b):
                U["A"].wait_read(pe, b, f"lnT{NH - 1}")
                for name, wt, rows in (("cs", cs1, DH), ("k", Wk, P), ("q", Wq, P)):
                    for h in range(NH):
                        filled("A", pe.matmul(fill("A", b, f"{name}{h}", rows=rows), wt[:], half(normT("A", b), h),
                                              start=True, stop=True))
                for h in range(NH):
                    U["A"].wait_read(pe, b, f"cs{h}")
                    filled("A", pe.matmul(fill("A", b, f"lam{h}"), cs2[:], half(hid, h), start=True, stop=True))
                pe.wait_ge(xl["A"].sem, xl["A"].at(b, 1))
                for k in range(LAG):
                    value(b, k)

            def attention_step(b, u, done):
                k = u - LAG
                if k >= 0:
                    f = k % EF
                    if k == 0:
                        wait_mixtures_out(done)
                    if f == 0:
                        fill("A", b, f"o{k // EF}")
                    pe.wait_ge(a_qs.sem, a_qs.at(b, k + 1))
                    last = pe.matmul(banks[7][:], Wo[:, f, :], qs[:, k % 4, :], start=(f == 0), stop=(f == EF - 1))
                    if f == EF - 1:
                        filled("A", last)
                if u + LAG < VK:
                    value(b, u + LAG)

            def attention_end(b, h):
                transpose_out("A", b, h, "o")

            def ssm_in(b):
                U["C"].wait_read(pe, b, f"lnT{NH - 1}")
                for name, wt in (("u", Win), ("z", Wz)):
                    for h in range(NH):
                        filled("C", pe.matmul(fill("C", b, f"{name}{h}"), wt[:], half(normT("C", b), h), start=True, stop=True))

            def ssm_rates(b):
                pe.wait_ge(c_xs.sem, c_xs.at(b, 1))
                for name, wt, rows in (("dt", Wdt, P), ("bc", Wbc, BC)):
                    for h in range(NH):
                        filled("C", pe.matmul(fill("C", b, f"{name}{h}", rows=rows), wt[:], half(xs, h),
                                              start=True, stop=True))

            def ssm_step(b, u, done):
                s, part = divmod(u, 3)
                if u == 0:
                    wait_mixtures_out(done)
                    pe.wait_ge(c_lo.sem, c_lo.at(b, 1))
                    pe.wait_ge(c_midc.sem, c_midc.at(b, 1))
                for kind, n, when in (("B", s, 0), ("C", s - 2, 1)):
                    if part == when and 0 <= n < NS:
                        row = n + NS * (kind == "C")
                        for h in range(NH):
                            filled("C", pe.matmul(fill("C", b, f"{kind}{n}_{h}"), sel_bc[:, row, :],
                                                  half(bc_parts, h), start=True, stop=True))

            def ssm_out(b):
                pe.wait_ge(c_yz.sem, c_yz.at(b, 1))
                for h in range(NH):
                    filled("C", pe.matmul(fill("C", b, f"o{h}"), Wout[:], half(w, h), start=True, stop=True))
                for h in range(NH):
                    transpose_out("C", b, h, "o")

            def logits(s, b):
                u = NORM_U[s]
                U[u].wait_read(pe, b, f"lnT{NH - 1}")
                bank = fill(u, b, "logits", cols=TT * E)
                for j in range(TT):
                    last = pe.matmul(bank[:, j * E:(j + 1) * E], normT(s, b)[:, j * P:(j + 1) * P], Wgate[s][:],
                                     start=True, stop=True)
                filled(u, last)

            def gate_transposes(s, b):
                pe.wait_ge(g_done[s].sem, g_done[s].at(b, 1))
                fill(s, b, "gT")
                gbank = banks[U[s].bank("gT")].bitcast(BF16)
                for j in range(TT):
                    last = pe.transpose(gbank[0:3 * E, j * P:(j + 1) * P],
                                        g_parts[:, j, :, :].rearrange("p c e -> p (c e)"), ident16[:])
                filled(s, last)

            def gate_rows(s, b, q):
                if q == 0:
                    U[s].wait_read(pe, b, "gT")
                filled(s, pe.matmul(fill(s, b, f"g{q}"), sel_gate[:, q % E, :], half(gT[s], q // E),
                                    start=True, stop=True))

            def down_product(s, b, k, done):
                h, i = divmod(k, NT[s])
                rows = TILES[s][i][2]
                U[s].wait_read(pe, b, f"b{k}")
                if k == 0:
                    U[OTHER[s]].wait_last_read(pe, done[OTHER[s]], 4)
                if i == 0:
                    fill(s, b, f"y{h}")
                last = pe.matmul(banks[4][:], W2[s][0:rows, i, :], h_ring[0:rows, k % RH, :],
                                 start=(i == 0), stop=(i == NT[s] - 1))
                if i == NT[s] - 1:
                    filled(s, last)

            def tile(s, b, k, done):
                n, o = NH * NT[s], OTHER[s]
                if k == 0:
                    U[s].wait_all_read(pe, done[s])
                    for bank in (0, 1):
                        U[o].wait_last_read(pe, done[o], bank)
                    pe.wait_ge(xl[s].sem, xl[s].at(b, 1))
                if k == GATE_LAG:
                    gate_transposes(s, b)
                q = gate_first(s, k - GATE_LAG)
                if q is not None:
                    gate_rows(s, b, q)
                if k < n:
                    h, i = divmod(k, NT[s])
                    _, _, rows, r0 = TILES[s][i]
                    filled(s, product(fill(s, b, f"a{k}", rows=rows), W1[s], r0, r0 + rows, s, b, h))
                j = k - SECOND_LAG
                if j == 0:
                    for bank in (2, 3):
                        U[o].wait_last_read(pe, done[o], bank)
                if 0 <= j < n:
                    h, i = divmod(j, NT[s])
                    _, _, rows, r0 = TILES[s][i]
                    filled(s, product(fill(s, b, f"b{j}", rows=rows), W3[s], r0, r0 + rows, s, b, h))
                if k >= DOWN_LAG:
                    down_product(s, b, k - DOWN_LAG, done)

            def mixture_out(s, b, h, done):
                if h == 0:
                    for u in ("A", "C", "PB", "PD"):
                        U[u].wait_all_read(pe, done[u])
                transpose_out(s, b, h, "y")

            program(Steps(
                start=nothing, weights_peak=nothing, weights_scale=nothing, weights_split=nothing, loaded=loaded,
                stats=nothing, norm=nothing, norm_transposed=norm_transposed, attention_start=attention_start,
                attention_step=attention_step, attention_end=attention_end, ssm_in=ssm_in, ssm_rates=ssm_rates,
                ssm_parts=nothing, ssm_softplus=nothing, ssm_step=ssm_step, ssm_gate=nothing, ssm_out=ssm_out, tile=tile,
                mixture_out=mixture_out, logits=logits, gates=nothing), pe)

        @block.scalar
        def _(act):
            for s in U:
                act.sem_inc(U[s].read["act"].sem, FIRST)

            def start():
                wait_weights(act, "A")
                act.activation(tb[:], col["decay"], ACT.Tanh, scale=0.5).then_inc(s_base, 1)
                act.mul(half_b2[:], col["cs_b2"], 0.5).then_inc(s_base, 1)
                act.wait_ge(s_base, 2)

            def weights_split(n):
                act.wait_ge(s_ws, 3 if n == "Wv" else 6)
                act.activation(Whi[n][:], stage[n], ACT.Copy, scale=up[n]).then_inc(s_hi, 1)

            def loaded(s):
                if s == "C":
                    wait_weights(act, s)

            def read(s, ins):
                ins.then_inc(U[s].read["act"].sem, 1)

            def bank(s, name, rows=P):
                return banks[U[s].bank(name)][0:rows, :]

            def norm_transposed(s, b, done):
                u = NORM_U[s]
                for h in range(NH):
                    U[u].wait_filled(act, b, f"lnT{h}")
                    ins = act.copy(half(normT(s, b), h), bank(u, f"lnT{h}"))
                    if s != "C":
                        ins.then_inc(xT[s].sem, 1)
                        ins = act.copy(half(x_hi(s, b), h), bank(u, f"lnT{h}"))
                    read(u, ins)

            def attention_start(b):
                for h in range(NH):
                    U["A"].wait_filled(act, b, f"cs{h}")
                    read("A", act.activation(half(hid, h), bank("A", f"cs{h}", DH), ACT.Tanh, bias=col["cs_b1"][0:DH]))
                for h in range(NH):
                    U["A"].wait_filled(act, b, f"k{h}")
                    read("A", act.activation(half(kT, h), bank("A", f"k{h}"), ACT.Copy, scale=down["Wv"]))
                for h in range(NH):
                    U["A"].wait_filled(act, b, f"q{h}")
                    read("A", act.copy(half(qT, h), bank("A", f"q{h}")))
                for h in range(NH):
                    U["A"].wait_filled(act, b, f"lam{h}")
                    ins = act.activation(half(lam_th, h), bank("A", f"lam{h}"), ACT.Tanh, bias=half_b2[:], scale=0.5)
                    read("A", ins)

            def attention_step(b, u, done):
                k = u - LAG - 1
                if k >= 0 and k % EF == EF - 1:
                    h = k // EF
                    U["A"].wait_filled(act, b, f"o{h}")
                    read("A", act.copy(oT["A"][:, h, :], bank("A", f"o{h}")))

            def attention_end(b, h):
                if h == 0:
                    attention_step(b, VK + LAG, None)

            def ssm_in(b):
                for h in range(NH):
                    U["C"].wait_filled(act, b, f"u{h}")
                    read("C", act.activation(upad[:, 1 + h * HW:1 + (h + 1) * HW], bank("C", f"u{h}"), ACT.Identity,
                                             bias=col["b_in"]))
                for h in range(NH):
                    U["C"].wait_filled(act, b, f"z{h}")
                    read("C", act.activation(half(z, h), bank("C", f"z{h}"), ACT.Silu, bias=col["bg"]))

            def ssm_rates(b):
                act.wait_ge(c_conv.sem, c_conv.at(b, 3))
                act.activation(xs[:], conv[:], ACT.Silu).then_inc(c_xs.sem, 1)
                for h in range(NH):
                    U["C"].wait_filled(act, b, f"dt{h}")
                    act.activation(half(sp_abs, h), bank("C", f"dt{h}"), ACT.Abs, bias=col["bdt"]).then_inc(c_sp.sem, 1)
                for h in range(NH):
                    U["C"].wait_filled(act, b, f"bc{h}")
                    read("C", act.activation(half(bc_f, h), bank("C", f"bc{h}", BC), ACT.Identity, bias=col["bbc"][0:BC]))
                U["C"].wait_read(act, b, f"bc{NH - 1}")
                act.copy(bc_parts[:], bc_f).then_inc(c_hi.sem, 1)

            def ssm_parts(b):
                act.wait_ge(c_r.sem, c_r.at(b, 1))
                for dst, rows, s in ((bc_parts, slice(2 * NS, 4 * NS), c_midc), (bc_mid, slice(4 * NS, 6 * NS), c_mid)):
                    act.copy(dst[rows, :], bc_r[rows, :]).then_inc(s.sem, 1)

            def ssm_softplus(b):
                act.wait_ge(c_sp.sem, c_sp.at(b, NH))
                act.activation(sp_abs, sp_abs, ACT.Exp, scale=-1.0).then_inc(c_sp.sem, 1)
                act.wait_ge(c_sp.sem, c_sp.at(b, NH + 1))
                act.activation(sp_log, sp_abs, ACT.Ln, bias=1.0).then_inc(c_sp.sem, 1)

            def decay(b, n):
                if n >= 4:
                    act.wait_ge(c_scan.sem, c_scan.at(b, n - 3))
                act.activation(dA[:, n % 4, :], dt[:], ACT.Exp, scale=A_sb[:, n:n + 1]).then_inc(c_dA.sem, 1)

            def ssm_step(b, u, done):
                s, part = divmod(u, 3)
                if u == 0:
                    act.wait_ge(c_dt.sem, c_dt.at(b, 1))
                    decay(b, 0)
                    decay(b, 1)
                elif part == 0 and s % 2 == 1 and s + 1 < NS:
                    decay(b, s + 1)
                    decay(b, s + 2)

            def ssm_out(b):
                for h in range(NH):
                    U["C"].wait_filled(act, b, f"o{h}")
                    read("C", act.activation(oT["C"][:, h, :], bank("C", f"o{h}"), ACT.Identity, bias=col["bout"]))

            def gates(s, b):
                u = NORM_U[s]
                U[u].wait_read(act, b, "logits")
                act.activation(g_e[:], g_lg[:], ACT.Exp).then_inc(g_exp[s].sem, 1)

            def gate_rows(s, b, q, done):
                if q >= RG:
                    k = max(k for k in range(NH * NT[s]) if gate_first(s, k) == q - RG + 1) - 1
                    act.wait_ge(m_sg[s].sem, m_sg[s].at(b, gated_to(s, k)))
                elif q == 0:
                    o = m_sg[OTHER[s]]
                    act.wait_ge(o.sem, o.at(done[OTHER[s]], 0))
                U[s].wait_filled(act, b, f"g{q}")
                read(s, act.copy(g_ring[:, q % RG, :], bank(s, f"g{q}")))

            def tile(s, b, k, done):
                if k == GATE_LAG:
                    U[s].wait_filled(act, b, "gT")
                    read(s, act.copy(gT[s][:], banks[U[s].bank("gT")].bitcast(BF16)[0:3 * E, :]))
                q = gate_first(s, k - GATE_LAG)
                if q is not None:
                    gate_rows(s, b, q, done)
                if k < NH * NT[s]:
                    rows = TILES[s][k % NT[s]][2]
                    U[s].wait_filled(act, b, f"a{k}")
                    wait_silu_slot(act, s, b, k, done)
                    read(s, act.activation(s_ring[0:rows, k % RS[s], :], bank(s, f"a{k}", rows), ACT.Silu,
                                           scale=down[W1[s]][0:rows]))
                h, i = divmod(k - DOWN_LAG, NT[s])
                if h >= 0 and i == NT[s] - 1:
                    U[s].wait_filled(act, b, f"y{h}")
                    read(s, act.copy(oT[s][:, h, :], bank(s, f"y{h}")))

            program(Steps(
                start=start, weights_peak=nothing, weights_scale=nothing, weights_split=weights_split, loaded=loaded,
                stats=nothing, norm=nothing, norm_transposed=norm_transposed, attention_start=attention_start,
                attention_step=attention_step, attention_end=attention_end, ssm_in=ssm_in, ssm_rates=ssm_rates,
                ssm_parts=ssm_parts, ssm_softplus=ssm_softplus, ssm_step=ssm_step, ssm_gate=nothing, ssm_out=ssm_out, tile=tile,
                mixture_out=nothing, logits=nothing, gates=gates), act)

        @block.vector
        def _(dve):
            for s in U:
                dve.sem_inc(U[s].read["dve"].sem, FIRST)

            def weights_peak(n):
                i = place[n]
                dve.wait_ge(s_st[n], 16)
                dve.tensor_reduce(wpeak[:, i:i + 1], stage[n], AX.X, ALU.max,
                                  apply_absolute_value=True).then_inc(s_wm, 1)

            def weights_scale(g):
                TOP = 12
                own = GROUPS[g]
                dve.wait_ge(s_wm, own.stop)
                dve.tensor_scalar(wfloor[:, own], wpeak[:, own], 1e-30, None, ALU.max).then_inc(s_wf, 1)
                dve.wait_ge(s_wt, g + 1)
                dve.tensor_scalar(wexp[:, own], wtop[:, own].bitcast(U32), 0x7F800000, None,
                                  ALU.bitwise_and).then_inc(s_ws, 1)
                dve.wait_ge(s_ws, 3 * g + 1)
                dve.tensor_scalar(wscale[:, own], wexp[:, own], -1.0, float((254 + TOP) << 23), ALU.mult,
                                  ALU.add).then_inc(s_ws, 1)
                dve.tensor_scalar(winv[:, own], wexp[:, own], float(TOP << 23), None, ALU.subtract).then_inc(s_ws, 1)
                dve.wait_ge(s_ws, 3 * g + 3)

            def weights_split(n):
                dve.wait_ge(s_hi, place[n] + 1)
                dve.scalar_tensor_tensor(out=Wlo[n][:], in0=stage[n], scalar=up[n], in1=Whi[n][:], op0=ALU.mult,
                                         op1=ALU.subtract).then_inc(s_lo, 1)

            def loaded(s):
                wait_weights(dve, s)
                if s == "A":
                    dve.wait_ge(s_base, 2)
                    dve.tensor_scalar(lam_mul[:], tb[:], 0.05, 0.05, ALU.mult, ALU.add).then_inc(s_lamc, 1)
                    dve.tensor_scalar(lam_add[:], tb[:], 0.55, 0.55, ALU.mult, ALU.add).then_inc(s_lamc, 1)
                    dve.wait_ge(s_lamc, 2)
                if s == "B":
                    dve.wait_ge(s_cons, 8)
                    dve.wait_ge(s_lo, len(SPLIT))

            def read(s, ins):
                ins.then_inc(U[s].read["dve"].sem, 1)

            def bank(s, name, rows=P):
                return banks[U[s].bank(name)][0:rows, :]

            BEFORE = {"B": "A", "C": "B", "D": "C"}

            def row_stats(s, b):
                x = stream("in", s, b)
                if s == "A":
                    dve.wait_ge(x_in.sem, x_in.at(b, 16))
                else:
                    U[BEFORE[s]].wait_read(dve, b, LAST_OUT)
                for j in range(TT):
                    dve.bn_stats(stats_b[:, j, :], x[:, j, :]).then_inc(stats[s].sem, 1)
                for j in range(TT):
                    dve.wait_ge(stats[s].sem, stats[s].at(b, j + 1))
                    dve.sem_inc(s_turn_dve, 1)
                    dve.bn_aggr(mv_b[:, j, :], stats_b[:, j, :]).then_inc(mv[s].sem, 1)

            def norm(s, b):
                x = stream("in", s, b)
                if stream("norm", s, b) is x4:
                    dve.wait_ge(x_out.sem, x_out.at(b, 0))
                dve.wait_ge(mv[s].sem, mv[s].at(b, TT))
                dve.wait_ge(rstd[s].sem, rstd[s].at(b, 1))
                for j in range(TT):
                    dve.tensor_scalar(stream("norm", s, b)[:, j, :], x[:, j, :], mv_b[:, j, 0:1], rstd_b[:, j:j + 1],
                                      ALU.subtract, ALU.mult).then_inc(xn[s].sem, 1)

            def norm_transposed(s, b, done):
                if s != "C":
                    U[NORM_U[s]].wait_read(dve, b, f"lnT{NH - 1}")
                    dve.tensor_tensor(x_lo(s, b), normT(s, b), x_hi(s, b), ALU.subtract).then_inc(xl[s].sem, 1)

            def add_residual(s, b, h):
                U[s].wait_filled(dve, b, f"outT{h}")
                js = slice(h * TH, (h + 1) * TH)
                read(s, dve.tensor_tensor(stream("out", s, b)[:, js, :].rearrange("p j d -> p (j d)"),
                                          bank(s, f"outT{h}"),
                                          stream("in", s, b)[:, js, :].rearrange("p j d -> p (j d)"), ALU.add))

            def outer(b, k):
                U["A"].wait_filled(dve, b, f"v{k}")
                if k >= 2:
                    dve.wait_ge(a_scan.sem, a_scan.at(b, k - 1))
                read("A", dve.tensor_tensor(kv[:, k % 2, :], bank("A", f"v{k}"), half(kT, k // EF), ALU.mult))

            def attention_start(b):
                for h in range(NH):
                    U["A"].wait_read(dve, b, f"lam{h}")
                    dve.tensor_scalar(half(lam, h), half(lam_th, h), lam_mul[:], lam_add[:],
                                      ALU.mult, ALU.add).then_inc(a_lin.sem, 1)
                for h in range(NH):
                    dve.wait_ge(a_lin.sem, a_lin.at(b, h + 1))
                    dve.tensor_scalar(half(lam, h), half(lam, h), LAM_MAX, 0.0, ALU.min,
                                      ALU.max).then_inc(a_lam.sem, 1)
                outer(b, 0)

            def attention_step(b, k, done):
                if k >= VK:
                    return
                if k + 1 < VK:
                    outer(b, k + 1)
                h, f = divmod(k, EF)
                U["A"].wait_read(dve, b, f"v{k}")
                dve.wait_ge(a_lam.sem, a_lam.at(b, h + 1))
                if h:
                    dve.wait_ge(a_qs.sem, a_qs.at(b, k - EF + 1))
                dve.tensor_tensor_scan(S[:, f, :], half(lam, h), kv[:, k % 2, :],
                                       0.0 if h == 0 else S[:, f, HW - 1:HW], ALU.mult,
                                       ALU.add).then_inc(a_scan.sem, 1)

            def attention_end(b, h):
                add_residual("A", b, h)

            def ssm_in(b):
                U["C"].wait_read(dve, b, f"u{NH - 1}")
                dve.tensor_scalar(conv[:], upad[:, 1:T + 1], convw[:, 1:2], col["convb"], ALU.mult,
                                  ALU.add).then_inc(c_conv.sem, 1)
                for i in (0, 2):
                    dve.wait_ge(c_conv.sem, c_conv.at(b, 1 + i // 2))
                    dve.scalar_tensor_tensor(out=conv[:], in0=upad[:, i:T + i], scalar=convw[:, i:i + 1], in1=conv[:],
                                             op0=ALU.mult, op1=ALU.add).then_inc(c_conv.sem, 1)

            def ssm_rates(b):
                for h in range(NH):
                    dve.wait_ge(c_sp.sem, c_sp.at(b, h + 1))
                    read("C", dve.tensor_scalar(half(dt, h), bank("C", f"dt{h}"), col["bdt"], 0.0, ALU.add, ALU.max))

            def ssm_parts(b):
                dve.wait_ge(c_hi.sem, c_hi.at(b, 1))
                dve.tensor_tensor(bc_r, bc_f, bc_parts[:], ALU.subtract).then_inc(c_r.sem, 1)
                dve.wait_ge(c_mid.sem, c_mid.at(b, 1))
                dve.tensor_tensor(bc_parts[4 * NS:6 * NS, :], bc_r[4 * NS:6 * NS, :], bc_mid[4 * NS:6 * NS, :],
                                  ALU.subtract).then_inc(c_lo.sem, 1)

            def ssm_softplus(b):
                dve.wait_ge(c_sp.sem, c_sp.at(b, NH + 2))
                U["C"].wait_read(dve, b, f"dt{NH - 1}")
                dve.tensor_tensor(dt[:], dt[:], sp_log, ALU.add).then_inc(c_dt.sem, 1)
                dve.wait_ge(c_dt.sem, c_dt.at(b, 1))
                dve.tensor_tensor(w[:], dt[:], xs[:], ALU.mult).then_inc(c_w.sem, 1)

            def ssm_step(b, u, done):
                s, part = divmod(u, 3)
                if u == 0:
                    dve.wait_ge(c_w.sem, c_w.at(b, 1))
                    dve.wait_ge(c_lo.sem, c_lo.at(b, 1))
                if part == 0 and s < NS:
                    for h in range(NH):
                        U["C"].wait_filled(dve, b, f"B{s}_{h}")
                        if s >= 2:
                            dve.wait_ge(c_scan.sem, c_scan.at(b, s - 1))
                        read("C", dve.tensor_tensor(half(dBx[:, s % 2, :], h), bank("C", f"B{s}_{h}"), half(w, h),
                                                    ALU.mult))
                if part == 1 and 0 <= s - 1 < NS:
                    n = s - 1
                    U["C"].wait_read(dve, b, f"B{n}_{NH - 1}")
                    dve.wait_ge(c_dA.sem, c_dA.at(b, n + 1))
                    if n >= 2:
                        U["C"].wait_read(dve, b, f"C{n - 2}_{NH - 1}")
                    dve.tensor_tensor_scan(hst[:, n % 2, :], dA[:, n % 4, :], dBx[:, n % 2, :], 0.0, ALU.mult,
                                           ALU.add).then_inc(c_scan.sem, 1)
                if part == 2 and 0 <= s - 2:
                    n = s - 2
                    dve.wait_ge(c_scan.sem, c_scan.at(b, n + 1))
                    if n >= 3:
                        dve.wait_ge(c_sum.sem, c_sum.at(b, n - 2))
                    dst = y if n == 0 else prod[:, n % 2, :]
                    for h in range(NH):
                        U["C"].wait_filled(dve, b, f"C{n}_{h}")
                        read("C", dve.tensor_tensor(half(dst, h), bank("C", f"C{n}_{h}"), half(hst[:, n % 2, :], h),
                                                    ALU.mult))

            def ssm_gate(b):
                dve.wait_ge(c_sum.sem, c_sum.at(b, NS - 1))
                U["C"].wait_read(dve, b, f"z{NH - 1}")
                dve.tensor_tensor(w[:], y[:], z[:], ALU.mult).then_inc(c_yz.sem, 1)

            def ssm_out(b):
                for h in range(NH):
                    add_residual("C", b, h)

            def gates(s, b):
                u = NORM_U[s]
                count = [0]

                def step(ins):
                    count[0] += 1
                    ins.then_inc(g_step[s].sem, 1)
                    dve.wait_ge(g_step[s].sem, g_step[s].at(b, count[0]))

                def bc(ap):
                    return ap.unsqueeze(2).broadcast_to([P, TT, E])

                U[u].wait_filled(dve, b, "logits")
                lg = bank(u, "logits")[:, 0:TT * E].rearrange("p (j e) -> p j e", e=E)
                step(dve.tensor_reduce(g_mx[:], lg, AX.X, ALU.max))
                read(u, dve.tensor_tensor(g_lg[:], lg, bc(g_mx[:]), ALU.subtract))
                dve.wait_ge(g_exp[s].sem, g_exp[s].at(b, 1))
                step(dve.tensor_reduce(g_sum[:], g_e[:], AX.X, ALU.add))
                step(dve.reciprocal(g_rs[:], g_sum[:]))
                step(dve.tensor_tensor(g_sc[:], g_e[:], bc(g_rs[:]), ALU.mult))
                pick = g_sc
                if s == "D":
                    pick = g_sel
                    step(dve.tensor_tensor(g_sel[:], g_sc[:], gate_bias[:].unsqueeze(1).broadcast_to([P, TT, E]), ALU.add))
                dve.sem_inc(s_turn_dve, 1)
                for j in range(TT):
                    ins = dve.max(g_top[:, j, :], pick[:, j, :])
                step(ins)
                dve.sem_inc(s_turn_dve, 1)
                for j in range(TT):
                    ins = dve.max_index(g_idx[:, j, :], g_top[:, j, :], pick[:, j, :])
                step(ins)
                step(dve.tensor_copy(g_idf[:], g_idx[:, :, 0:2]))
                step(dve.tensor_tensor(g_m[:], expert_no[:], bc(g_idf[:, :, 0]), ALU.is_equal))
                step(dve.tensor_tensor(g_r1[:], expert_no[:], bc(g_idf[:, :, 1]), ALU.is_equal))
                step(dve.tensor_tensor(g_m[:], g_m[:], g_r1[:], ALU.add))
                step(dve.tensor_tensor(g_ms[:], g_m[:], g_sc[:], ALU.mult))
                if s == "B":
                    step(dve.tensor_reduce(g_den[:], g_ms[:], AX.X, ALU.add))
                    step(dve.tensor_scalar(g_den[:], g_den[:], 1e-20, None, ALU.add))
                    step(dve.reciprocal(g_rd[:], g_den[:]))
                    step(dve.tensor_tensor(g_ms[:], g_ms[:], bc(g_rd[:]), ALU.mult))
                step(dve.tensor_copy(g_parts[:, :, 0, :], g_ms[:]))
                step(dve.tensor_tensor(g_r1[:], g_ms[:], g_parts[:, :, 0, :], ALU.subtract))
                step(dve.tensor_copy(g_parts[:, :, 1, :], g_r1[:]))
                dve.tensor_tensor(g_parts[:, :, 2, :], g_r1[:], g_parts[:, :, 1, :], ALU.subtract).then_inc(g_done[s].sem, 1)
                assert count[0] == GATE_STEPS[s], count

            def tile(s, b, step, done):
                k = step - SECOND_LAG
                if not 0 <= k < NH * NT[s]:
                    return
                _, e, rows, _ = TILES[s][k % NT[s]]
                U[s].wait_filled(dve, b, f"b{k}")
                if e is None:
                    U[s].wait_read(dve, b, f"a{k}")
                else:
                    dve.wait_ge(m_sg[s].sem, m_sg[s].at(b, gated_to(s, k)))
                read(s, dve.scalar_tensor_tensor(out=h_ring[0:rows, k % RH, :], in0=bank(s, f"b{k}", rows),
                                                 scalar=down[W3[s]][0:rows], in1=s_ring[0:rows, k % RS[s], :],
                                                 op0=ALU.mult, op1=ALU.mult))

            def mixture_out(s, b, h, done):
                if s == "D":
                    dve.wait_ge(x_out.sem, x_out.at(b, 0))
                add_residual(s, b, h)

            program(Steps(
                start=nothing, weights_peak=weights_peak, weights_scale=weights_scale, weights_split=weights_split,
                loaded=loaded,
                stats=row_stats, norm=norm, norm_transposed=norm_transposed, attention_start=attention_start,
                attention_step=attention_step, attention_end=attention_end, ssm_in=ssm_in, ssm_rates=ssm_rates,
                ssm_parts=ssm_parts, ssm_softplus=ssm_softplus, ssm_step=ssm_step, ssm_gate=ssm_gate, ssm_out=ssm_out, tile=tile,
                mixture_out=mixture_out, logits=nothing, gates=gates), dve)


def kernel(**inputs):
    import numpy as np
    import concourse.bacc as bacc
    from concourse import mybir as mb
    from concourse.bass_utils import run_bass_kernel_spmd

    i = {k: np.asarray(v) for k, v in inputs.items()}
    H, EF = 16, 8
    D = 128

    def column(v):
        return v.reshape(-1, 1)

    def rows(v):
        return v.reshape(-1, v.shape[-1]).T

    bc = np.concatenate([i["L1_attn_Wb"], i["L1_attn_Wc"]], axis=1)
    bbc = np.concatenate([i["L1_attn_bb"], i["L1_attn_bc"]])
    v_t = i["L0_attn_v_w"].T.reshape(D, H, EF)
    o_t = i["L0_attn_o_w"].T.reshape(H, EF, D)
    t = {
        "x": i["L0_attn_x"],
        "Wk": i["L0_attn_k_w"].T, "Wq": i["L0_attn_q_w"].T,
        "Wv": np.repeat(v_t.transpose(0, 2, 1), EF, axis=2).reshape(D, -1),
        "Wo": np.repeat(o_t, EF, axis=0),
        "cs1": i["L0_attn_cs_w1"].T, "cs2": np.repeat(i["L0_attn_cs_w2"].T, EF, axis=1),
        "cs_b1": column(i["L0_attn_cs_b1"]), "cs_b2": column(np.repeat(i["L0_attn_cs_b2"], EF)),
        "decay": column(i["L0_attn_decay_params"]),
        "Wg0": i["L0_ffn_Wg"].T, "W1_0": rows(i["L0_ffn_W1"]), "W3_0": rows(i["L0_ffn_W3"]),
        "W2_0": i["L0_ffn_W2"].transpose(0, 2, 1),
        "Win": i["L1_attn_Win"], "Wz": i["L1_attn_Wg"], "Wdt": i["L1_attn_Wdt"], "Wout": i["L1_attn_Wout"],
        "Wbc": np.concatenate([bc, bc, bc], axis=1), "bbc": column(np.concatenate([bbc, bbc, bbc])),
        "b_in": column(i["L1_attn_b_in"]), "bg": column(i["L1_attn_bg"]), "bout": column(i["L1_attn_bout"]),
        "convb": column(i["L1_attn_convb"]), "bdt": column(i["L1_attn_bdt"]),
        "convw": i["L1_attn_convw"], "A": i["L1_attn_A"],
        "Wg1": i["L1_ffn_gate_w"].T, "gate_bias": np.repeat(i["L1_ffn_gate_bias"].reshape(1, -1), D, axis=0),
        "W1_1": np.concatenate([rows(i["L1_ffn_w1"]), i["L1_ffn_sw1"].T], axis=1),
        "W3_1": np.concatenate([rows(i["L1_ffn_w3"]), i["L1_ffn_sw3"].T], axis=1),
        "W2_1": np.concatenate([i["L1_ffn_w2"].transpose(0, 2, 1), i["L1_ffn_sw2"].T.reshape(2, D, D)], axis=0),
    }
    nc = bacc.Bacc("TRN2", target_bir_lowering=False, num_devices=1)
    arrays, handles = {}, {}
    for name, a in t.items():
        a = np.ascontiguousarray(a)
        arrays[f"in_{name}"] = a
        handles[name] = nc.dram_tensor(f"in_{name}", a.shape, mb.dt.from_np(a.dtype), kind="ExternalInput").ap()
    out = nc.dram_tensor("out_0", i["L0_attn_x"].shape, mb.dt.float32, kind="ExternalOutput").ap()
    build(nc, handles, out)
    r = run_bass_kernel_spmd(nc, [arrays], core_ids=[0])
    return r.results[0]["out_0"]
```
